# Optimizing a Trainium2 kernel written in Bass

```python
import numpy as np
import jax
import jax.numpy as jnp

def _softmax(x, axis=-1):
    return jax.nn.softmax(x, axis=axis)
def _gelu(x):
    return jax.nn.gelu(x, approximate=True)
def _silu(x):
    return jax.nn.silu(x)
def _sigmoid(x):
    return jax.nn.sigmoid(x)
def _layernorm(x, axis=-1, eps=1e-5):
    m = jnp.mean(x, axis=axis, keepdims=True)
    v = jnp.var(x, axis=axis, keepdims=True)
    return (x - m) / jnp.sqrt(v + eps)
def _scatter_add(tgt, idx, src, axis=0):
    return tgt.at[idx].add(src)
def _segment_sum(src, seg, n):
    return jax.ops.segment_sum(src, seg, n)

kernel_name = 'mk_adj_preln_d2_adj_256_7b9207'

def setup_inputs(seed: int = 0):
    np.random.seed(seed)
    _w = jnp.asarray
    def _rec_inputs():
        import jax
        import jax.numpy as jnp
        _gk = jax.random.key(seed)
        x = -8.015e-05 + 0.9999 * jax.random.normal(jax.random.fold_in(_gk, 1), (16, 1024, 256), jnp.float32)
        _w = (1.0 + jnp.arange(1024, dtype=jnp.float32)) ** -0.5
        _w = _w / _w.mean()
        _pij = jnp.clip(0.00390625 * _w[:, None] * _w[None, :], 0.0, 1.0)
        _a = jax.random.uniform(jax.random.fold_in(_gk, 2), (16, 1024, 1024)) < _pij
        _a = jnp.logical_or(_a, jnp.swapaxes(_a, -1, -2))
        _a = jnp.logical_or(_a, jnp.eye(1024, dtype=bool))
        _af = _a.astype(jnp.float32)
        _af = _af * jax.random.uniform(jax.random.fold_in(_gk, 3), (16, 1024, 1024), jnp.float32, 0.05, 0.999837)
        adj = _af
        return x, adj
    x, adj = _rec_inputs()
    def _L0_gnn_setup():
        import jax, jax.numpy as jnp
        import numpy as np
        GROUPS = [list(range(25)), [0, 1, 2, 3, 4, 5, 6, 7, 8], [0, 9, 10, 11, 12, 13, 14], [6, 7, 8, 12, 13, 14], [3, 4, 5, 9, 10, 11]]
        B, N, D_IN, D_HID = (8192, 25, 256, 512)

        def _graph_conv(x, adj, W, b):
            n = adj.shape[-1]
            A = adj + jnp.eye(n, dtype=adj.dtype)
            deg = jnp.sum(A, axis=-1)
            deg_safe = jnp.where(deg == 0, 1.0, deg)
            dinv = jnp.where(deg == 0, 0.0, deg_safe ** (-0.5))
            norm_adj = dinv[:, :, None] * A * dinv[:, None, :]
            support = jnp.einsum('bnd,de->bne', x, W)
            out = jnp.einsum('bnm,bme->bne', norm_adj, support) + b
            return jax.nn.relu(out)
        key = jax.random.key(seed)
        ks = jax.random.split(key, 7)
        s1 = float(np.sqrt(6.0 / (D_IN + D_HID)))
        s2 = float(np.sqrt(6.0 / (D_HID + D_IN)))
        return {'x': jax.random.normal(ks[0], (B, N, D_IN), dtype=jnp.float32), 'adj': jax.random.uniform(ks[1], (B, N, N), dtype=jnp.float32), 'W1': jax.random.uniform(ks[2], (5, D_IN, D_HID), jnp.float32, -s1, s1), 'b1': jnp.zeros((5, D_HID), dtype=jnp.float32), 'W2': jax.random.uniform(ks[3], (5, D_HID, D_IN), jnp.float32, -s2, s2), 'b2': jnp.zeros((5, D_IN), dtype=jnp.float32), 'fusion_w': jnp.ones((5,), dtype=jnp.float32)}
    _L0_gnn_all = _L0_gnn_setup()
    _L0_gnn_in = {k: v for k, v in _L0_gnn_all.items() if k in ('W1', 'b1', 'W2', 'b2', 'fusion_w', )}
    del _L0_gnn_all

    def _L1_gnn_setup():
        import jax, jax.numpy as jnp
        import numpy as np
        from jax import lax
        DIM = 256
        EPS = 1e-05

        def _bn(h, g, b, m, v):
            scale = g / jnp.sqrt(v + EPS)
            return h * scale[None, :, None] + (b - m * scale)[None, :, None]

        def _conv1d(h, w, pad):
            return lax.conv_general_dilated(h, w, window_strides=(1,), padding=[(pad, pad)], dimension_numbers=('NCH', 'OIH', 'NCH'))
        key = jax.random.key(seed)
        ks = jax.random.split(key, 16)
        bs, n, d = (16, 2048, DIM)
        s = 0.05
        return {'x': jax.random.normal(ks[0], (bs, n, d), jnp.float32), 'mask': jnp.ones((bs, n, n), jnp.float32), 'w_se': jax.random.normal(ks[1], (3, d), jnp.float32) * s, 'b_se': jnp.zeros((3,), jnp.float32), 'conv1_w': jax.random.normal(ks[2], (d, d, 1), jnp.float32) * s, 'bn1_g': jnp.ones((d,), jnp.float32), 'bn1_b': jnp.zeros((d,), jnp.float32), 'bn1_m': jnp.zeros((d,), jnp.float32), 'bn1_v': jnp.ones((d,), jnp.float32), 'conv2_w': jax.random.normal(ks[3], (d, d, 17), jnp.float32) * s, 'bn2_g': jnp.ones((d,), jnp.float32), 'bn2_b': jnp.zeros((d,), jnp.float32), 'bn2_m': jnp.zeros((d,), jnp.float32), 'bn2_v': jnp.ones((d,), jnp.float32), 'w_msg': jax.random.normal(ks[4], (d, d), jnp.float32) * s, 'b_msg': jnp.zeros((d,), jnp.float32), 'w_ih': jax.random.normal(ks[5], (3 * d, 2 * d), jnp.float32) * s, 'b_ih': jnp.zeros((3 * d,), jnp.float32), 'w_hh': jax.random.normal(ks[6], (3 * d, d), jnp.float32) * s, 'b_hh': jnp.zeros((3 * d,), jnp.float32)}
    _L1_gnn_all = _L1_gnn_setup()
    _L1_gnn_in = {k: v for k, v in _L1_gnn_all.items() if k in ('w_se', 'b_se', 'conv1_w', 'bn1_g', 'bn1_b', 'bn1_m', 'bn1_v', 'conv2_w', 'bn2_g', 'bn2_b', 'bn2_m', 'bn2_v', 'w_msg', 'b_msg', 'w_ih', 'b_ih', 'w_hh', 'b_hh', )}
    del _L1_gnn_all

    return {
        "x": x,
        "adj": adj,
        "L0_gnn_W1": _L0_gnn_in["W1"],
        "L0_gnn_b1": _L0_gnn_in["b1"],
        "L0_gnn_W2": _L0_gnn_in["W2"],
        "L0_gnn_b2": _L0_gnn_in["b2"],
        "L0_gnn_fusion_w": _L0_gnn_in["fusion_w"],
        "L1_gnn_w_se": _L1_gnn_in["w_se"],
        "L1_gnn_b_se": _L1_gnn_in["b_se"],
        "L1_gnn_conv1_w": _L1_gnn_in["conv1_w"],
        "L1_gnn_bn1_g": _L1_gnn_in["bn1_g"],
        "L1_gnn_bn1_b": _L1_gnn_in["bn1_b"],
        "L1_gnn_bn1_m": _L1_gnn_in["bn1_m"],
        "L1_gnn_bn1_v": _L1_gnn_in["bn1_v"],
        "L1_gnn_conv2_w": _L1_gnn_in["conv2_w"],
        "L1_gnn_bn2_g": _L1_gnn_in["bn2_g"],
        "L1_gnn_bn2_b": _L1_gnn_in["bn2_b"],
        "L1_gnn_bn2_m": _L1_gnn_in["bn2_m"],
        "L1_gnn_bn2_v": _L1_gnn_in["bn2_v"],
        "L1_gnn_w_msg": _L1_gnn_in["w_msg"],
        "L1_gnn_b_msg": _L1_gnn_in["b_msg"],
        "L1_gnn_w_ih": _L1_gnn_in["w_ih"],
        "L1_gnn_b_ih": _L1_gnn_in["b_ih"],
        "L1_gnn_w_hh": _L1_gnn_in["w_hh"],
        "L1_gnn_b_hh": _L1_gnn_in["b_hh"],
    }

def reference(x, adj, L0_gnn_W1, L0_gnn_b1, L0_gnn_W2, L0_gnn_b2, L0_gnn_fusion_w, L1_gnn_w_se, L1_gnn_b_se, L1_gnn_conv1_w, L1_gnn_bn1_g, L1_gnn_bn1_b, L1_gnn_bn1_m, L1_gnn_bn1_v, L1_gnn_conv2_w, L1_gnn_bn2_g, L1_gnn_bn2_b, L1_gnn_bn2_m, L1_gnn_bn2_v, L1_gnn_w_msg, L1_gnn_b_msg, L1_gnn_w_ih, L1_gnn_b_ih, L1_gnn_w_hh, L1_gnn_b_hh):
    import jax
    import jax.numpy as jnp
    def _L0_gnn_ref(x, adj, W1, b1, W2, b2, fusion_w):
        import jax, jax.numpy as jnp
        import numpy as np
        GROUPS = [list(range(25)), [0, 1, 2, 3, 4, 5, 6, 7, 8], [0, 9, 10, 11, 12, 13, 14], [6, 7, 8, 12, 13, 14], [3, 4, 5, 9, 10, 11]]
        B, N, D_IN, D_HID = (8192, 25, 256, 512)

        def _graph_conv(x, adj, W, b):
            n = adj.shape[-1]
            A = adj + jnp.eye(n, dtype=adj.dtype)
            deg = jnp.sum(A, axis=-1)
            deg_safe = jnp.where(deg == 0, 1.0, deg)
            dinv = jnp.where(deg == 0, 0.0, deg_safe ** (-0.5))
            norm_adj = dinv[:, :, None] * A * dinv[:, None, :]
            support = jnp.einsum('bnd,de->bne', x, W)
            out = jnp.einsum('bnm,bme->bne', norm_adj, support) + b
            return jax.nn.relu(out)
        norm_w = jax.nn.softmax(fusion_w)
        fused = jnp.zeros_like(x)
        for g, idx_list in enumerate(GROUPS):
            idx = jnp.asarray(idx_list)
            x_g = x[:, idx, :]
            adj_g = adj[:, idx][:, :, idx]
            h = _graph_conv(x_g, adj_g, W1[g], b1[g])
            out_g = _graph_conv(h, adj_g, W2[g], b2[g])
            fused = fused.at[:, idx, :].add(norm_w[g] * out_g)
        return fused

    def _L1_gnn_ref(x, mask, w_se, b_se, conv1_w, bn1_g, bn1_b, bn1_m, bn1_v, conv2_w, bn2_g, bn2_b, bn2_m, bn2_v, w_msg, b_msg, w_ih, b_ih, w_hh, b_hh):
        import jax, jax.numpy as jnp
        import numpy as np
        from jax import lax
        DIM = 256
        EPS = 1e-05

        def _bn(h, g, b, m, v):
            scale = g / jnp.sqrt(v + EPS)
            return h * scale[None, :, None] + (b - m * scale)[None, :, None]

        def _conv1d(h, w, pad):
            return lax.conv_general_dilated(h, w, window_strides=(1,), padding=[(pad, pad)], dimension_numbers=('NCH', 'OIH', 'NCH'))
        d = x.shape[-1]
        xc = jnp.transpose(x, (0, 2, 1))
        h = _bn(_conv1d(xc, conv1_w, 0), bn1_g, bn1_b, bn1_m, bn1_v)
        h = jax.nn.relu(h)
        h = _bn(_conv1d(h, conv2_w, 8), bn2_g, bn2_b, bn2_m, bn2_v)
        x_conv = jnp.transpose(jax.nn.relu(h + xc), (0, 2, 1))
        s = x @ w_se.T + b_se
        sq = jnp.sum(s * s, axis=-1)
        dist = sq[:, :, None] + sq[:, None, :] - 2.0 * jnp.einsum('bnd,bmd->bnm', s, s)
        A = jnp.exp(-dist) * mask
        msg = jax.nn.relu(x @ w_msg.T + b_msg)
        x_nmp = jnp.einsum('bnm,bmd->bnd', A, msg)
        x_in = jnp.concatenate([x_conv, x_nmp], axis=-1)
        gi = x_in @ w_ih.T + b_ih
        gh = x @ w_hh.T + b_hh
        gi_r, gi_z, gi_n = (gi[..., :d], gi[..., d:2 * d], gi[..., 2 * d:])
        gh_r, gh_z, gh_n = (gh[..., :d], gh[..., d:2 * d], gh[..., 2 * d:])
        r = jax.nn.sigmoid(gi_r + gh_r)
        z = jax.nn.sigmoid(gi_z + gh_z)
        nn_ = jnp.tanh(gi_n + r * gh_n)
        return (1.0 - z) * nn_ + z * x

    h = jnp.maximum(_layernorm(x, axis=-1), 0.0)
    x = x + _L0_gnn_ref(h, adj, L0_gnn_W1, L0_gnn_b1, L0_gnn_W2, L0_gnn_b2, L0_gnn_fusion_w)
    h = jnp.maximum(_layernorm(x, axis=-1), 0.0)
    x = x + _L1_gnn_ref(h, adj, L1_gnn_w_se, L1_gnn_b_se, L1_gnn_conv1_w, L1_gnn_bn1_g, L1_gnn_bn1_b, L1_gnn_bn1_m, L1_gnn_bn1_v, L1_gnn_conv2_w, L1_gnn_bn2_g, L1_gnn_bn2_b, L1_gnn_bn2_m, L1_gnn_bn2_v, L1_gnn_w_msg, L1_gnn_b_msg, L1_gnn_w_ih, L1_gnn_b_ih, L1_gnn_w_hh, L1_gnn_b_hh)
    return x


_drawn_inputs = setup_inputs


def setup_inputs(seed=0):
    import zlib

    import numpy as np

    out = dict(_drawn_inputs(seed))
    spreads = {'L0_gnn_b1': (0.0, 0.8),
     'L0_gnn_b2': (0.0, 2.0),
     'L0_gnn_fusion_w': (1.0, 0.6),
     'L1_gnn_b_se': (0.0, 2.0),
     'L1_gnn_bn1_g': (1.0, 0.2),
     'L1_gnn_bn1_b': (0.0, 0.1),
     'L1_gnn_bn1_m': (0.0, 0.1),
     'L1_gnn_bn1_v': (1.0, 0.6),
     'L1_gnn_bn2_g': (1.0, 0.2),
     'L1_gnn_bn2_b': (0.0, 0.456),
     'L1_gnn_bn2_m': (0.0, 0.372),
     'L1_gnn_bn2_v': (1.0, 0.6),
     'L1_gnn_b_msg': (0.0, 0.1),
     'L1_gnn_b_ih': (0.0, 0.287),
     'L1_gnn_b_hh': (0.0, 0.375)}
    factors = {'L0_gnn_W1': 7.016, 'L0_gnn_W2': 5.856}
    for name, (base, spread) in spreads.items():
        noise = np.random.default_rng([zlib.crc32(name.encode()), seed]).standard_normal(out[name].shape)
        drawn = base * np.exp(spread * noise) if base else spread * noise
        out[name] = jnp.asarray(drawn.astype(out[name].dtype))
    for name, factor in factors.items():
        out[name] = (out[name] * factor).astype(out[name].dtype)
    return out
```

```python
from contextlib import ExitStack

import concourse.bass as bass
from concourse import mybir

F32 = mybir.dt.float32
F16 = mybir.dt.float16
BF16 = mybir.dt.bfloat16
ALU = mybir.AluOpType
ACT = mybir.ActivationFunctionType
AX = mybir.AxisListType

P = 128
HALF = 512
WSCALE = 16.0
ASCALE = 256.0
EPS = 1e-5

NODES = 25
GROUPS = [list(range(25)), list(range(9)), [0, 9, 10, 11, 12, 13, 14],
          [6, 7, 8, 12, 13, 14], [3, 4, 5, 9, 10, 11]]
RUN = [(min(g), max(g) - min(g) + 1) for g in GROUPS]
NG = len(GROUPS)
SLOT = 32
PER = P // SLOT

PAIRS = [(0, 0), (0, 1), (1, 0), (1, 1), (0, 2), (2, 0)]


def wait(engine, sem, value):
    if isinstance(value, int) and value <= 0:
        return
    engine.wait_ge(sem, value)


def build(nc, x, adj_t, adj_head, l0_w1, l0_w2, l0_b1, l0_b2, fusion_w, masks, eye_d, weights, cols_d, row_d, out):
    B, N, D = x.shape
    HID = l0_w1.shape[-1]
    C = D // P
    HC = HID // P
    T = N // P
    H = N // HALF
    Q = B // PER
    TAPS = 17
    PAD = TAPS // 2
    MW = D + 3
    OFF_CONV1 = 0
    OFF_MSG = OFF_CONV1 + C * D
    OFF_CONV2 = OFF_MSG + C * MW
    OFF_IH = OFF_CONV2 + C * TAPS * D
    OFF_HH = OFF_IH + 2 * C * 3 * D
    NW = OFF_HH + C * 3 * D
    WCHUNK = 1024
    NCHUNK = -(-NW // WCHUNK)
    assert weights.shape[1] == NW and H == 2 and C == 2 and T == 8

    with ExitStack() as ctx:
        def sem(name):
            return ctx.enter_context(nc.semaphore(name))

        def keep(name, shape, dt):
            return ctx.enter_context(nc.sbuf_tensor(name, shape, dt))

        w_hi = keep("w_hi", [P, NW], F16)
        w_lo = keep("w_lo", [P, NW], F16)
        w_raw = keep("w_raw", [P, 2, WCHUNK], F32)
        eye = keep("eye", [P, P], F32)
        eye_b = keep("eye_b", [P, P], BF16)
        cols = keep("cols", [P, 28], F32)
        bn_scale = keep("bn_scale", [P, 4], F32)
        bn_psum = keep("bn_psum", [P, 4], F32)
        bn_shift = keep("bn_shift", [P, 4], F32)
        gate_b = keep("gate_b", [P, 6], F32)
        row_b = keep("row_b", [P, MW], F32)
        half_neg = keep("half_neg", [P, 4 * NG], F32)
        ps = ctx.enter_context(nc.psum_tensor("ps", [P, 8, HALF], F32))
        xnew = nc.dram_tensor("xnew", [B, NODES, D], F32).ap()

        l0_small = sem("l0_small_loaded")
        l0_x = sem("l0_x_loaded")
        l0_w1_in = sem("l0_w1_loaded")
        l0_w2_in = sem("l0_w2_loaded")
        w_in = [sem(f"w_raw_loaded{i}") for i in range(2)]
        zeroed = sem("l0_zeroed")
        chain = sem("dve_chain")
        deg_ready = sem("deg_ready")
        pool_dinv = sem("pool_dinv")
        b_ready = sem("l0_b_ready")
        pe_nt = sem("pe_nt")
        nt_ready = sem("nt_ready")
        var0_ready = sem("var0_ready")
        pool_rstd0 = sem("pool_rstd0")
        h0_ready = sem("h0_ready")
        pe_agg1 = sem("pe_agg1")
        g_ready = sem("g_ready")
        pe_w1 = sem("pe_w1")
        h2_ready = sem("h2_ready")
        pe_w2 = sem("pe_w2")
        s2t_ready = sem("s2t_ready")
        pe_s2 = sem("pe_s2")
        s2_ready = sem("s2_ready")
        pe_agg2 = sem("pe_agg2")
        act_chain = sem("act_chain")
        fus_ready = sem("fus_ready")
        fus_max = sem("fus_max")
        rw_ready = sem("rw_ready")
        relu2 = sem("relu2")
        acc_done = sem("acc_done")
        xnew_ready = sem("xnew_ready")
        xnew_stored = sem("xnew_stored")
        var_bn = sem("var_bn")
        pool_bn = sem("pool_bn")
        w_split = sem("w_split")
        w_used = sem("w_raw_used")
        consts_ready = sem("consts_ready")
        half_set = sem("half_set")
        eyeb_ready = sem("eyeb_ready")

        with ExitStack() as l0:
            def sb(name, shape, dt=F32):
                return l0.enter_context(nc.sbuf_tensor(name, shape, dt))

            x0 = sb("x0", [P, Q, D])
            h0 = sb("h0", [P, Q, D])
            A = sb("A", [P, Q, P])
            AM = sb("AM", [P, NG, Q, P])
            NT = sb("NT", [P, NG, Q, P])
            mask = sb("mask", [P, NG, P])
            rowmask = sb("rowmask", [P, NG])
            W1 = sb("W1", [P, NG, C, HID])
            W2 = sb("W2", [P, NG, HC, D])
            b1 = sb("b1", [P, NG, HC])
            b2 = sb("b2", [1, NG, D])
            ones = sb("ones", [1, P])
            fus = sb("fus", [P, NG])
            fmx = sb("fmx", [P, 1])
            fex = sb("fex", [P, NG])
            fsum = sb("fsum", [P, 2])
            rw = sb("rw", [P, NG])
            deg = sb("deg", [P, NG, Q])
            nz = sb("nz", [P, NG, Q])
            dinv = sb("dinv", [P, NG, Q])
            dm = sb("dm", [P, NG, Q])
            st0 = sb("st0", [P, Q, 6])
            mv0 = sb("mv0", [P, Q, 2])
            rs0 = sb("rs0", [P, Q])
            nm0 = sb("nm0", [P, Q])
            gT = [sb(f"gT{g}", [P, C, B * RUN[g][1]]) for g in range(NG)]
            h2 = [sb(f"h2{g}", [P, HC, B * RUN[g][1]]) for g in range(NG)]
            s2T = sb("s2T", [P, 2, C, B, SLOT])
            S2 = sb("S2", [P, 2, Q, D])
            r2 = sb("r2", [P, 2, Q, D])
            acc = sb("acc", [P, Q, D])

            with nc.Block() as block:
                @block.sync
                def _(sp):
                    sp.dma_start(mask[:], masks[:, 0:NG * P].rearrange("p (g n) -> p g n", g=NG)).then_inc(l0_small, 16)
                    sp.dma_start(rowmask[:], masks[:, NG * P:]).then_inc(l0_small, 16)
                    sp.dma_start(eye[:], eye_d).then_inc(l0_small, 16)
                    sp.dma_start(cols[:], cols_d).then_inc(l0_small, 16)
                    sp.dma_start(row_b[:], row_d.partition_broadcast(P)).then_inc(l0_small, 16)
                    sp.dma_start(fus[:], fusion_w.partition_broadcast(P)).then_inc(l0_small, 16)
                    sp.dma_start(b1[:], l0_b1.rearrange("p (g h) -> p g h", g=NG)).then_inc(l0_small, 16)
                    sp.dma_start(b2[:], l0_b2.rearrange("(a g) d -> a g d", a=1)).then_inc(l0_small, 16)
                    sp.wait_ge(zeroed, 2)
                    for j in range(PER):
                        lo = SLOT * j
                        sp.dma_start(A[lo:lo + NODES, :, lo:lo + NODES],
                                     adj_head.rearrange("(q j) n m -> j n q m", j=PER)[j]).then_inc(l0_small, 16)
                        sp.dma_start(x0[lo:lo + NODES, :, :],
                                     x[:, 0:NODES, :].rearrange("(q j) n d -> j n q d", j=PER)[j]).then_inc(l0_x, 16)
                    sp.dma_start(W1[:], l0_w1.rearrange("g (c p) h -> p g c h", p=P)).then_inc(l0_w1_in, 16)
                    sp.dma_start(W2[:], l0_w2.rearrange("g (c p) d -> p g c d", p=P)).then_inc(l0_w2_in, 16)
                    for i in range(NCHUNK):
                        n = min(WCHUNK, NW - i * WCHUNK)
                        if i >= 2:
                            sp.wait_ge(w_used, i - 1)
                        sp.dma_start(w_raw[:, i % 2, 0:n], weights[:, i * WCHUNK:i * WCHUNK + n]).then_inc(w_in[i % 2], 16)
                    sp.wait_ge(xnew_ready, 1)
                    for j in range(PER):
                        sp.dma_start(xnew.rearrange("(q j) n d -> j n q d", j=PER)[j],
                                     acc[SLOT * j:SLOT * j + NODES, :, :]).then_inc(xnew_stored, 16)
                    sp.wait_ge(xnew_stored, 16 * PER)

                @block.gpsimd
                def _(pool):
                    nc.gpsimd.memset(A[:], 0.0).then_inc(zeroed, 1)
                    nc.gpsimd.memset(x0[:], 0.0).then_inc(zeroed, 1)
                    nc.gpsimd.memset(half_neg[:], -0.5).then_inc(half_set, 1)
                    nc.gpsimd.memset(s2T[:], 0.0).then_inc(zeroed, 1)
                    nc.gpsimd.memset(ones[:], 1.0).then_inc(zeroed, 1)
                    pool.wait_ge(half_set, 1)
                    pool.wait_ge(deg_ready, 1)
                    nc.gpsimd.tensor_tensor(dinv[:].rearrange("p g q -> p (g q)"), deg[:].rearrange("p g q -> p (g q)"),
                                            half_neg[:], ALU.pow).then_inc(pool_dinv, 1)
                    pool.wait_ge(var0_ready, 1)
                    nc.gpsimd.tensor_tensor(rs0[:], rs0[:], half_neg[:, 0:Q], ALU.pow).then_inc(pool_rstd0, 1)
                    pool.wait_ge(var_bn, 1)
                    nc.gpsimd.tensor_tensor(bn_scale[:], bn_scale[:], half_neg[:, 0:4], ALU.pow).then_inc(pool_bn, 1)

                @block.vector
                def _(dve):
                    step = [0]

                    def link(ins):
                        step[0] += 1
                        ins.then_inc(chain, 1)
                        dve.wait_ge(chain, step[0])

                    dve.wait_ge(l0_small, 16 * (8 + PER))
                    link(nc.vector.tensor_tensor(A[:], A[:], eye[:].unsqueeze(1).to_broadcast([P, Q, P]), ALU.add))
                    for g in range(NG):
                        last = nc.vector.tensor_tensor(AM[:, g], A[:], mask[:, g].unsqueeze(1).to_broadcast([P, Q, P]), ALU.mult)
                    link(last)
                    link(nc.vector.tensor_reduce(deg[:], AM[:], AX.X, ALU.add))
                    link(nc.vector.tensor_scalar(nz[:], deg[:], 0.0, None, ALU.is_equal))
                    nc.vector.tensor_tensor(deg[:], deg[:], nz[:], ALU.add).then_inc(deg_ready, 1)
                    dve.wait_ge(deg_ready, 1)
                    link(nc.vector.tensor_scalar(nz[:], nz[:], -1.0, 1.0, ALU.mult, ALU.add))
                    dve.wait_ge(l0_x, 16 * PER)
                    for q in range(Q):
                        last = nc.vector.bn_stats(st0[:, q], x0[:, q])
                    link(last)
                    for q in range(Q):
                        last = nc.vector.bn_aggr(mv0[:, q], st0[:, q])
                    link(last)
                    nc.vector.tensor_scalar(rs0[:], mv0[:, :, 1], EPS, None, ALU.add).then_inc(var0_ready, 1)
                    nc.vector.tensor_scalar(bn_scale[:, 0:2], cols[:, 6:8], EPS, None, ALU.add)
                    nc.vector.tensor_scalar(bn_scale[:, 2:4], cols[:, 14:16], EPS, None, ALU.add).then_inc(var_bn, 1)
                    dve.wait_ge(pool_dinv, 1)
                    link(nc.vector.tensor_tensor(dinv[:], dinv[:], nz[:], ALU.mult))
                    nc.vector.tensor_tensor(dm[:], dinv[:], rowmask[:].unsqueeze(2).to_broadcast([P, NG, Q]), ALU.mult)
                    link(nc.vector.tensor_tensor(AM[:].rearrange("p g q n -> p (g q) n"), AM[:].rearrange("p g q n -> p (g q) n"),
                                                 dinv[:].rearrange("p g q -> p (g q)").unsqueeze(2).to_broadcast([P, NG * Q, P]), ALU.mult))
                    nc.vector.tensor_copy(eye_b[:], eye[:]).then_inc(b_ready, 1)
                    dve.wait_ge(pool_rstd0, 1)
                    for q in range(Q):
                        last = nc.vector.tensor_scalar(h0[:, q], x0[:, q], mv0[:, q, 0:1], rs0[:, q:q + 1], ALU.subtract, ALU.mult)
                    link(last)
                    nc.vector.tensor_scalar(h0[:], h0[:], 0.0, None, ALU.max).then_inc(h0_ready, 1)
                    for g in range(NG):
                        dve.wait_ge(pe_nt, g + 1)
                        nc.vector.tensor_tensor(NT[:, g], ps[:, g, :].rearrange("p (q n) -> p q n", q=Q),
                                                dm[:, g].unsqueeze(2).to_broadcast([P, Q, P]), ALU.mult).then_inc(nt_ready, 1)
                    link(nc.vector.tensor_reduce(fmx[:], fus[:], AX.X, ALU.max))
                    nc.vector.tensor_scalar(fus[:], fus[:], fmx[:], None, ALU.subtract).then_inc(fus_max, 1)
                    dve.wait_ge(fus_ready, 1)
                    link(nc.vector.tensor_reduce(fsum[:, 0:1], fex[:], AX.X, ALU.add))
                    link(nc.vector.reciprocal(fsum[:, 1:2], fsum[:, 0:1]))
                    nc.vector.scalar_tensor_tensor(rw[:], fex[:], fsum[:, 1:2], rowmask[:], ALU.mult, ALU.mult).then_inc(rw_ready, 1)
                    dve.wait_ge(pool_bn, 1)
                    link(nc.vector.tensor_tensor(bn_scale[:, 0:2], bn_scale[:, 0:2], cols[:, 0:2], ALU.mult))
                    link(nc.vector.tensor_tensor(bn_scale[:, 2:4], bn_scale[:, 2:4], cols[:, 8:10], ALU.mult))
                    nc.vector.tensor_scalar(bn_psum[:], bn_scale[:], 1.0 / WSCALE, None, ALU.mult)
                    nc.vector.tensor_tensor(bn_shift[:, 0:2], bn_scale[:, 0:2], cols[:, 4:6], ALU.mult)
                    link(nc.vector.tensor_tensor(bn_shift[:, 2:4], bn_scale[:, 2:4], cols[:, 12:14], ALU.mult))
                    nc.vector.tensor_tensor(bn_shift[:, 0:2], cols[:, 2:4], bn_shift[:, 0:2], ALU.subtract)
                    nc.vector.tensor_tensor(bn_shift[:, 2:4], cols[:, 10:12], bn_shift[:, 2:4], ALU.subtract)
                    nc.vector.tensor_scalar(gate_b[:, 4:6], cols[:, 26:28], 0.5, None, ALU.mult)
                    link(nc.vector.tensor_tensor(gate_b[:, 0:4], cols[:, 16:20], cols[:, 22:26], ALU.add))
                    nc.vector.tensor_scalar(gate_b[:, 0:4], gate_b[:, 0:4], 0.5, None, ALU.mult).then_inc(consts_ready, 1)
                    for i in range(NCHUNK):
                        n = min(WCHUNK, NW - i * WCHUNK)
                        cut = slice(i * WCHUNK, i * WCHUNK + n)
                        dve.wait_ge(w_in[i % 2], 16 * (i // 2 + 1))
                        nc.vector.tensor_scalar(w_hi[:, cut], w_raw[:, i % 2, 0:n], WSCALE, None, ALU.mult).then_inc(w_split, 1)
                        dve.wait_ge(w_split, i + 1)
                        nc.vector.scalar_tensor_tensor(w_lo[:, cut], w_raw[:, i % 2, 0:n], WSCALE, w_hi[:, cut],
                                                       ALU.mult, ALU.subtract).then_inc(w_used, 1)
                    dve.wait_ge(zeroed, 4)

                    def slots(g):
                        lo, n = RUN[g]
                        for d in range(C):
                            i = g * C + d
                            dve.wait_ge(pe_w2, i + 1)
                            if g >= 2:
                                dve.wait_ge(pe_s2, 2 * (g - 1))
                            nc.vector.tensor_copy(s2T[:, g % 2, d, :, lo:lo + n],
                                                  ps[:, 5 + i % 3, 0:B * n].rearrange("p (b n) -> p b n", n=n)).then_inc(s2t_ready, 1)

                    def rows(g):
                        for k in range(2):
                            i = 2 * g + k
                            dve.wait_ge(pe_s2, i + 1)
                            if g >= 2:
                                dve.wait_ge(pe_agg2, 2 * (g - 1))
                            nc.vector.tensor_copy(S2[:, g % 2, 2 * k:2 * k + 2, :],
                                                  ps[:, i % 2, :].rearrange("p (q d) -> p q d", q=2)).then_inc(s2_ready, 1)

                    def fuse(g):
                        dve.wait_ge(relu2, 2 * g + 2)
                        if g == 0:
                            dve.wait_ge(h0_ready, 1)
                            nc.vector.tensor_tensor(acc[:], x0[:], r2[:, 0], ALU.add).then_inc(acc_done, 1)
                        else:
                            dve.wait_ge(acc_done, g)
                            ins = nc.vector.tensor_tensor(acc[:], acc[:], r2[:, g % 2], ALU.add)
                            ins.then_inc(xnew_ready if g == NG - 1 else acc_done, 1)

                    for g in range(NG + 2):
                        if g < NG:
                            slots(g)
                        if 1 <= g <= NG:
                            rows(g - 1)
                        if g >= 2:
                            fuse(g - 2)

                @block.scalar
                def _(act):
                    act.wait_ge(fus_max, 1)
                    nc.scalar.activation(fex[:], fus[:], ACT.Exp).then_inc(fus_ready, 1)
                    for i in range(NG * C):
                        g, c = divmod(i, C)
                        act.wait_ge(pe_agg1, i + 1)
                        nc.scalar.activation(gT[g][:, c, :], ps[:, 5 + i % 3, 0:B * RUN[g][1]], ACT.Copy).then_inc(g_ready, 1)
                    for i in range(NG * HC):
                        g, hc = divmod(i, HC)
                        act.wait_ge(pe_w1, i + 1)
                        nc.scalar.activation(h2[g][:, hc, :], ps[:, i % 5, 0:B * RUN[g][1]], ACT.Relu,
                                             bias=b1[:, g, hc:hc + 1]).then_inc(h2_ready, 1)
                    act.wait_ge(rw_ready, 1)
                    for i in range(NG * 2):
                        g, k = divmod(i, 2)
                        act.wait_ge(pe_agg2, i + 1)
                        if g >= 2:
                            act.wait_ge(acc_done, g - 1)
                        nc.scalar.activation(r2[:, g % 2, 2 * k:2 * k + 2, :],
                                             ps[:, 2 + i % 3, :].rearrange("p (q d) -> p q d", q=2),
                                             ACT.Relu, scale=rw[:, g:g + 1]).then_inc(relu2, 1)

                @block.tensor
                def _(pe):
                    pe.wait_ge(b_ready, 1)
                    pe.wait_ge(chain, 9)
                    for g in range(NG):
                        for q in range(Q):
                            last = nc.tensor.transpose(ps[:, g, q * P:(q + 1) * P], AM[:, g, q], eye[:])
                        last.then_inc(pe_nt, 1)
                    pe.wait_ge(h0_ready, 1)
                    for i in range(NG * C):
                        g, c = divmod(i, C)
                        lo, n = RUN[g]
                        pe.wait_ge(nt_ready, g + 1)
                        wait(pe, g_ready, i - 2)
                        for q in range(Q):
                            last = nc.tensor.matmul(ps[:, 5 + i % 3, q * PER * n:(q + 1) * PER * n].rearrange("p (j n) -> p j n", n=n),
                                                    h0[:, q, c * P:(c + 1) * P],
                                                    NT[:, g, q].rearrange("p (j n) -> p j n", n=SLOT)[:, :, lo:lo + n],
                                                    start=True, stop=True)
                        last.then_inc(pe_agg1, 1)
                    pe.wait_ge(l0_w1_in, 16)
                    for i in range(NG * HC):
                        g, hc = divmod(i, HC)
                        n = B * RUN[g][1]
                        pe.wait_ge(g_ready, C * (g + 1))
                        pe.wait_ge(nt_ready, NG)
                        wait(pe, h2_ready, i - 4)
                        for c in range(C):
                            last = nc.tensor.matmul(ps[:, i % 5, 0:n], W1[:, g, c, hc * P:(hc + 1) * P], gT[g][:, c, :],
                                                    start=(c == 0), stop=(c == C - 1))
                        last.then_inc(pe_w1, 1)
                    def second(g):
                        n = B * RUN[g][1]
                        for d in range(C):
                            i = g * C + d
                            wait(pe, s2t_ready, i - 2)
                            for hc in range(HC):
                                last = nc.tensor.matmul(ps[:, 5 + i % 3, 0:n], W2[:, g, hc, d * P:(d + 1) * P], h2[g][:, hc, :],
                                                        start=(hc == 0), stop=(hc == HC - 1))
                            last.then_inc(pe_w2, 1)

                    def to_rows(g):
                        pe.wait_ge(s2t_ready, C * (g + 1))
                        for k in range(2):
                            i = 2 * g + k
                            wait(pe, s2_ready, i - 1)
                            for q in range(2):
                                for d in range(C):
                                    src = s2T[:, g % 2, d, (2 * k + q) * PER:(2 * k + q + 1) * PER, :].rearrange("p b n -> p (b n)")
                                    last = nc.tensor.transpose(ps[:, i % 2, q * D + d * P:q * D + (d + 1) * P], src, eye[:])
                            last.then_inc(pe_s2, 1)

                    def aggregate(g):
                        for k in range(2):
                            i = 2 * g + k
                            pe.wait_ge(s2_ready, i + 1)
                            wait(pe, relu2, i - 2)
                            for q in range(2):
                                dst = ps[:, 2 + i % 3, q * D:(q + 1) * D]
                                nc.tensor.matmul(dst, NT[:, g, 2 * k + q], S2[:, g % 2, 2 * k + q], start=True, stop=False)
                                last = nc.tensor.matmul(dst, ones[0:1, :], b2[0:1, g, :], start=False, stop=True)
                            last.then_inc(pe_agg2, 1)

                    pe.wait_ge(l0_w2_in, 16)
                    pe.wait_ge(g_ready, NG * C)
                    pe.wait_ge(h2_ready, NG * HC)
                    pe.wait_ge(zeroed, 4)
                    for g in range(NG + 2):
                        if g < NG:
                            second(g)
                        if 1 <= g <= NG:
                            to_rows(g - 1)
                        if g >= 2:
                            aggregate(g - 2)

        def sb(name, shape, dt=F32):
            return ctx.enter_context(nc.sbuf_tensor(name, shape, dt))

        xrow = sb("xrow", [P, 2, T, D])
        xn = sb("xn", [P, T, D])
        res = xn[:].rearrange("p t d -> p (t d)").rearrange("p (c n) -> p c n", c=C)
        hf = sb("hf", [P, 2, HALF])
        h_hi = sb("h_hi", [P, 2, C, N], F16)
        h_lo = sb("h_lo", [P, 2, C, N], F16)
        h1f = sb("h1f", [P, 2, HALF])
        h1_hi = sb("h1_hi", [P, C, N + 2 * PAD], F16)
        h1_lo = sb("h1_lo", [P, C, N + 2 * PAD], F16)
        mf = sb("mf", [P, 2, D])
        m_hi = sb("m_hi", [P, T, D], F16)
        m_lo = sb("m_lo", [P, T, D], F16)
        n_hi = m_hi[:].rearrange("p t d -> p (t d)").rearrange("p (c n) -> p c n", c=C)
        n_lo = m_lo[:].rearrange("p t d -> p (t d)").rearrange("p (c n) -> p c n", c=C)
        emb = sb("emb", [P, T, 4])
        emb_r = sb("emb_r", [P, T, 4])
        parts = [sb(f"part{i}", [P, T, 4], BF16) for i in range(3)]
        ssq = sb("ssq", [P, T, 3])
        nsq = sb("nsq", [P, T])
        RS = sb("RS", [P, T, P], BF16)
        LS = sb("LS", [P, T, P], BF16)
        RT = sb("RT", [P, N], BF16)
        LT = sb("LT", [P, N], BF16)
        E = sb("E", [P, 2, N])
        a_hi = sb("a_hi", [P, 4, N], F16)
        a_lo = sb("a_lo", [P, 4, N], F16)
        adj = sb("adj", [P, 2, N])
        c2f = sb("c2f", [P, 2, HALF])
        xc_hi = sb("xc_hi", [P, C, N], F16)
        xc_lo = sb("xc_lo", [P, C, N], F16)
        nf = sb("nf", [P, 2, HALF])
        cand = sb("cand", [P, 2, HALF])
        tr = sb("tr", [P, 2, HALF])
        tz = sb("tz", [P, 2, HALF])
        ot = sb("ot", [P, 2, 2, D])
        stats = sb("stats", [P, T, 6])
        mv = sb("mv", [P, T, 3])
        rstd = sb("rstd", [P, T])

        x_in = [sem(f"x_loaded{i}") for i in range(2)]
        adj_in = [sem(f"adj_loaded{i}") for i in range(2)]
        pads = sem("pads_zeroed")
        pe_h = sem("pe_h")
        pe_conv1 = sem("pe_conv1")
        pe_msg = sem("pe_msg")
        pe_out = sem("pe_out")
        pe_conv2 = sem("pe_conv2")
        pe_stack = sem("pe_stack")
        pe_dist = sem("pe_dist")
        pe_chunk = sem("pe_chunk")
        pe_hn = sem("pe_hn")
        pe_r = sem("pe_r")
        pe_z = sem("pe_z")
        pe_in = sem("pe_in")
        act_h = sem("act_h")
        act_h1 = sem("act_h1")
        act_msg = sem("act_msg")
        act_stack = sem("act_stack")
        act_exp = sem("act_exp")
        act_ahi = sem("act_ahi")
        act_xc = sem("act_xc")
        act_nmp = sem("act_nmp")
        act_hn = sem("act_hn")
        act_r = sem("act_r")
        act_z = sem("act_z")
        act_cand = sem("act_cand")
        ln_stats = sem("ln_stats")
        ln_sums = sem("ln_sums")
        ln_terms = sem("ln_terms")
        ln_var = sem("ln_var")
        ln_xn = sem("ln_xn")
        h_hi_done = sem("h_hi_done")
        h_done = sem("h_done")
        h1_hi_done = sem("h1_hi_done")
        h1_done = sem("h1_done")
        msg_f = sem("msg_f")
        m_done = sem("m_done")
        emb_chain = sem("emb_chain")
        stack_done = sem("stack_done")
        out_done = sem("out_done")
        a_done = sem("a_done")
        c2_hi = sem("c2_plus_hi")
        c2_done = sem("c2_done")
        xc_hi_done = sem("xc_hi_done")
        xc_done = sem("xc_done")
        n_hi_done = sem("n_hi_done")
        n_done = sem("n_done")
        g_rh = sem("g_rh")
        g_cand = sem("g_cand")
        g_dlo = sem("g_dlo")
        g_mix = sem("g_mix")
        g_res = sem("g_res")
        pool_rstd = sem("pool_rstd")
        pool_alo = sem("pool_alo")
        pool_d = sem("pool_d")
        stored = [sem(f"out_stored{i}") for i in range(2)]

        block = ctx.enter_context(nc.Block())

        def batches(engine, body):
            body(0, 0, 0, False)
            with engine.Fori(0, B // 2 - 1) as j:
                body(2 * j + 1, 1, j, False)
                body(2 * j + 2, 0, j + 1, False)
            body(B - 1, 1, B // 2 - 1, True)

        def first(b):
            return isinstance(b, int) and b == 0

        @block.sync
        def _(sp):
            def load_x(b, p):
                sp.dma_start(xrow[NODES:P, p, 0, :], x[b, NODES:P, :]).then_inc(x_in[p], 16)
                sp.dma_start(xrow[:, p, 1:T, :], x[b, P:N, :].rearrange("(t p) d -> p t d", p=P)).then_inc(x_in[p], 16)
                sp.dma_start(xrow[0:NODES, p, 0, :], xnew[b]).then_inc(x_in[p], 16)

            def load_adj(b, t):
                wait(sp, a_done, T * b + t - 1)
                sp.dma_start(adj[:, t % 2, :], adj_t[b, t * P:(t + 1) * P, :]).then_inc(adj_in[t % 2], 16)

            def body(b, p, q, last):
                if not first(b):
                    for k in range(4):
                        sp.wait_ge(out_done, 4 * (b - 1) + k + 1)
                        sp.dma_start(out[b - 1, 2 * k * P:2 * (k + 1) * P, :].rearrange("(t p) d -> p t d", p=P),
                                     ot[:, k % 2]).then_inc(stored[k % 2], 16)
                if not last:
                    load_x(b + 1, 1 - p)
                for t in range(2, T):
                    load_adj(b, t)
                if not last:
                    load_adj(b + 1, 0)
                    load_adj(b + 1, 1)

            load_x(0, 0)
            load_adj(0, 0)
            load_adj(0, 1)
            batches(sp, body)
            for k in range(4):
                sp.wait_ge(out_done, 4 * (B - 1) + k + 1)
                sp.dma_start(out[B - 1, 2 * k * P:2 * (k + 1) * P, :].rearrange("(t p) d -> p t d", p=P),
                             ot[:, k % 2]).then_inc(stored[k % 2], 16)
            for i in range(2):
                sp.wait_ge(stored[i], 16 * (2 * B + 1))

        @block.gpsimd
        def _(pool):
            for buf in (h1_hi, h1_lo):
                nc.gpsimd.memset(buf[:, :, 0:PAD], 0.0).then_inc(pads, 1)
                nc.gpsimd.memset(buf[:, :, PAD + N:], 0.0).then_inc(pads, 1)
            for i in range(2):
                nc.gpsimd.memset(ot[:, i], 0.0).then_inc(stored[i], 16)
            nc.gpsimd.memset(RS[:], 0.0).then_inc(pads, 1)
            nc.gpsimd.memset(LS[:], 0.0).then_inc(pads, 1)

            def norm(b):
                pool.wait_ge(ln_var, b + 1)
                nc.gpsimd.tensor_tensor(rstd[:], rstd[:], half_neg[:, 0:T], ALU.pow).then_inc(pool_rstd, 1)

            def body(b, p, q, last):
                for t in range(T):
                    pool.wait_ge(act_ahi, T * b + t + 1)
                    nc.gpsimd.tensor_tensor(a_lo[:, t % 4], E[:, t % 2], a_hi[:, t % 4], ALU.subtract).then_inc(pool_alo, 1)
                    if t == 1 and not last:
                        norm(b + 1)
                for i in range(4):
                    m, h = divmod(i, 2)
                    pool.wait_ge(act_cand, 4 * b + i + 1)
                    nc.gpsimd.tensor_tensor(res[:, m, h * HALF:(h + 1) * HALF], h_hi[:, p, m, h * HALF:(h + 1) * HALF],
                                            cand[:, h], ALU.subtract).then_inc(pool_d, 1)

            norm(0)
            batches(pool, body)

        @block.scalar
        def _(act):
            def hidden(b, p):
                for i in range(4):
                    act.wait_ge(pe_h, 4 * b + i + 1)
                    wait(act, h_done, 4 * b + i - 1)
                    nc.scalar.activation(hf[:, i % 2], ps[:, i, :], ACT.Relu).then_inc(act_h, 1)

            def body(b, p, q, last):
                for i in range(4):
                    m = i // 2
                    act.wait_ge(pe_conv1, 4 * b + i + 1)
                    wait(act, h1_done, 4 * b + i - 1)
                    nc.scalar.activation(h1f[:, i % 2], ps[:, 4 + i, :], ACT.Relu, bias=bn_shift[:, m:m + 1],
                                         scale=bn_psum[:, m:m + 1]).then_inc(act_h1, 1)
                wait(act, pe_in, 4 * b)
                for t in range(T):
                    act.wait_ge(msg_f, T * b + t + 1)
                    nc.scalar.activation(m_hi[:, t], mf[:, t % 2], ACT.Relu).then_inc(act_msg, 1)
                wait(act, pe_dist, T * b)
                for i, dst in enumerate((RT, LT)):
                    act.wait_ge(pe_stack, 2 * b + i + 1)
                    nc.scalar.activation(dst[:], ps[:, 4 + i, :].bitcast(BF16), ACT.Copy).then_inc(act_stack, 1)

                def weigh(t):
                    bank = 0 if t >= 4 else (4 if t % 2 else 6)
                    act.wait_ge(pe_dist, T * b + t + 1)
                    wait(act, pool_alo, T * b + t - 1)
                    nc.scalar.activation(E[:, t % 2], ps[:, bank:bank + 2, :].rearrange("p a n -> p (a n)"), ACT.Exp,
                                         bias=nsq[:, t:t + 1]).then_inc(act_exp, 1)
                    act.wait_ge(a_done, T * b + t + 1)
                    wait(act, pe_chunk, T * b + t - 3)
                    nc.scalar.activation(a_hi[:, t % 4], E[:, t % 2], ACT.Copy).then_inc(act_ahi, 1)

                def conv2_relu(m):
                    for h in range(H):
                        act.wait_ge(c2_done, 4 * b + 2 * m + h + 1)
                        nc.scalar.activation(c2f[:, h], c2f[:, h], ACT.Relu, bias=bn_shift[:, 2 + m:3 + m]).then_inc(act_xc, 1)

                for t in range(4):
                    weigh(t)
                conv2_relu(0)
                for t in range(4, T):
                    weigh(t)
                conv2_relu(1)
                for i in range(4):
                    act.wait_ge(pe_chunk, T * (b + 1))
                    wait(act, n_done, 4 * b + i - 1)
                    nc.scalar.activation(nf[:, i % 2], ps[:, 4 + i, :], ACT.Copy, scale=1.0 / ASCALE).then_inc(act_nmp, 1)
                if not last:
                    hidden(b + 1, 1 - p)
                for m in range(C):
                    for h in range(H):
                        i = 4 * b + 2 * m + h
                        act.wait_ge(pe_hn, i + 1)
                        wait(act, g_res, i - 1)
                        nc.scalar.activation(cand[:, h], ps[:, h, :], ACT.Identity, bias=gate_b[:, 4 + m:5 + m],
                                             scale=0.5 / WSCALE).then_inc(act_hn, 1)
                    for h in range(H):
                        act.wait_ge(pe_r, 4 * b + 2 * m + h + 1)
                        nc.scalar.activation(tr[:, h], ps[:, 2 + h, :], ACT.Tanh, bias=gate_b[:, m:m + 1],
                                             scale=0.5 / WSCALE).then_inc(act_r, 1)
                    for h in range(H):
                        act.wait_ge(pe_z, 4 * b + 2 * m + h + 1)
                        nc.scalar.activation(tz[:, h], ps[:, 4 + h, :], ACT.Tanh, bias=gate_b[:, 2 + m:3 + m],
                                             scale=0.5 / WSCALE).then_inc(act_z, 1)
                    for h in range(H):
                        act.wait_ge(g_cand, 4 * b + 2 * m + h + 1)
                        nc.scalar.activation(cand[:, h], cand[:, h], ACT.Tanh, bias=cols[:, 20 + m:21 + m]).then_inc(act_cand, 1)

            hidden(0, 0)
            batches(act, body)

        @block.vector
        def _(dve):
            def norm_stats(b, p, q):
                dve.wait_ge(x_in[p], 48 * (q + 1))
                for t in range(T):
                    last = nc.vector.bn_stats(stats[:, t], xrow[:, p, t])
                last.then_inc(ln_stats, 1)
                dve.wait_ge(ln_stats, b + 1)
                nc.vector.tensor_tensor(mv[:, :, 0], stats[:, :, 1], stats[:, :, 4], ALU.add)
                nc.vector.tensor_tensor(mv[:, :, 1], stats[:, :, 1], stats[:, :, 4], ALU.subtract)
                nc.vector.tensor_tensor(mv[:, :, 2], stats[:, :, 2], stats[:, :, 5], ALU.add).then_inc(ln_sums, 1)
                dve.wait_ge(ln_sums, b + 1)
                nc.vector.tensor_scalar(mv[:, :, 0], mv[:, :, 0], 0.5, None, ALU.mult)
                nc.vector.tensor_tensor(mv[:, :, 1], mv[:, :, 1], mv[:, :, 1], ALU.mult)
                nc.vector.tensor_scalar(mv[:, :, 2], mv[:, :, 2], 1.0 / D, EPS, ALU.mult, ALU.add).then_inc(ln_terms, 1)
                dve.wait_ge(ln_terms, b + 1)
                nc.vector.scalar_tensor_tensor(rstd[:], mv[:, :, 1], 0.25, mv[:, :, 2], ALU.mult, ALU.add).then_inc(ln_var, 1)

            def norm_apply(b, p):
                dve.wait_ge(pool_rstd, b + 1)
                wait(dve, pe_out, 4 * b - 4)
                for t in range(T):
                    nc.vector.tensor_scalar(xn[:, t], xrow[:, p, t], mv[:, t, 0:1], rstd[:, t:t + 1],
                                            ALU.subtract, ALU.mult).then_inc(ln_xn, 1)

            def hidden(b, p):
                for i in range(4):
                    c, h = divmod(i, 2)
                    cut = slice(h * HALF, (h + 1) * HALF)
                    dve.wait_ge(act_h, 4 * b + i + 1)
                    nc.vector.tensor_copy(h_hi[:, p, c, cut], hf[:, i % 2]).then_inc(h_hi_done, 1)
                    dve.wait_ge(h_hi_done, 4 * b + i + 1)
                    nc.vector.tensor_tensor(h_lo[:, p, c, cut], hf[:, i % 2], h_hi[:, p, c, cut], ALU.subtract).then_inc(h_done, 1)

            def body(b, p, q, last):
                wait(dve, pe_conv2, 4 * b)
                if first(b):
                    dve.wait_ge(pads, 6)
                for i in range(4):
                    c, h = divmod(i, 2)
                    cut = slice(PAD + h * HALF, PAD + (h + 1) * HALF)
                    dve.wait_ge(act_h1, 4 * b + i + 1)
                    nc.vector.tensor_copy(h1_hi[:, c, cut], h1f[:, i % 2]).then_inc(h1_hi_done, 1)
                    dve.wait_ge(h1_hi_done, 4 * b + i + 1)
                    nc.vector.tensor_tensor(h1_lo[:, c, cut], h1f[:, i % 2], h1_hi[:, c, cut], ALU.subtract).then_inc(h1_done, 1)

                def low_message(t):
                    dve.wait_ge(act_msg, T * b + t + 1)
                    nc.vector.scalar_tensor_tensor(m_lo[:, t], mf[:, t % 2], 0.0, m_hi[:, t],
                                                   ALU.max, ALU.subtract).then_inc(m_done, 1)

                for t in range(T):
                    dve.wait_ge(pe_msg, T * b + t + 1)
                    wait(dve, m_done, T * b + t - 1)
                    nc.vector.scalar_tensor_tensor(emb[:, t, 0:3], ps[:, t % 4, D:MW], 1.0 / WSCALE, row_b[:, D:MW],
                                                   ALU.mult, ALU.add)
                    nc.vector.scalar_tensor_tensor(mf[:, t % 2], ps[:, t % 4, 0:D], 1.0 / WSCALE, row_b[:, 0:D],
                                                   ALU.mult, ALU.add).then_inc(msg_f, 1)
                    if t >= 1:
                        low_message(t - 1)
                low_message(T - 1)
                if not first(b):
                    add_rows(b - 1, 1 - p)
                CH = 7
                n = 0

                def link(ins):
                    nonlocal n
                    n += 1
                    ins.then_inc(emb_chain, 1)
                    dve.wait_ge(emb_chain, CH * b + n)

                wait(dve, act_exp, T * b)
                dve.wait_ge(msg_f, T * (b + 1))
                link(nc.vector.tensor_tensor(ssq[:], emb[:, :, 0:3], emb[:, :, 0:3], ALU.mult))
                link(nc.vector.tensor_reduce(emb[:, :, 3], ssq[:], AX.X, ALU.add))
                nc.vector.tensor_scalar(nsq[:], emb[:, :, 3], -1.0, None, ALU.mult)
                link(nc.vector.tensor_copy(parts[0][:], emb[:]))
                link(nc.vector.tensor_tensor(emb_r[:], emb[:], parts[0][:], ALU.subtract))
                link(nc.vector.tensor_copy(parts[1][:], emb_r[:]))
                link(nc.vector.tensor_tensor(emb_r[:], emb_r[:], parts[1][:], ALU.subtract))
                link(nc.vector.tensor_copy(parts[2][:], emb_r[:]))
                wait(dve, pe_stack, 2 * b)
                for k, (left, right) in enumerate(PAIRS):
                    if first(b) and left == 0:
                        nc.vector.memset(LS[:, :, 4 * k + 3:4 * k + 4], -1.0)
                    nc.vector.tensor_copy(RS[:, :, 4 * k:4 * k + 4], parts[right][:])
                    ins = nc.vector.tensor_scalar(LS[:, :, 4 * k:4 * k + 3], parts[left][:, :, 0:3], 2.0, None, ALU.mult)
                ins.then_inc(stack_done, 1)

                def weigh(t):
                    dve.wait_ge(adj_in[t % 2], 16 * (4 * b + t // 2 + 1))
                    dve.wait_ge(act_exp, T * b + t + 1)
                    nc.vector.scalar_tensor_tensor(E[:, t % 2], E[:, t % 2], ASCALE, adj[:, t % 2],
                                                   ALU.mult, ALU.mult).then_inc(a_done, 1)

                def conv2_out(m):
                    for h in range(H):
                        i = 4 * b + 2 * m + h
                        cut = slice(h * HALF, (h + 1) * HALF)
                        dve.wait_ge(pe_conv2, i + 1)
                        wait(dve, xc_done, i - 1)
                        nc.vector.scalar_tensor_tensor(c2f[:, h], ps[:, 2 * m + h, :], bn_psum[:, 2 + m:3 + m],
                                                       h_hi[:, p, m, cut], ALU.mult, ALU.add).then_inc(c2_hi, 1)
                        dve.wait_ge(c2_hi, i + 1)
                        nc.vector.tensor_tensor(c2f[:, h], c2f[:, h], h_lo[:, p, m, cut], ALU.add).then_inc(c2_done, 1)
                    if m == 0:
                        wait(dve, pe_in, 4 * b)
                    for h in range(H):
                        i = 4 * b + 2 * m + h
                        cut = slice(h * HALF, (h + 1) * HALF)
                        dve.wait_ge(act_xc, i + 1)
                        nc.vector.tensor_copy(xc_hi[:, m, cut], c2f[:, h]).then_inc(xc_hi_done, 1)
                        dve.wait_ge(xc_hi_done, i + 1)
                        nc.vector.tensor_tensor(xc_lo[:, m, cut], c2f[:, h], xc_hi[:, m, cut], ALU.subtract).then_inc(xc_done, 1)

                weigh(0)
                if not last:
                    norm_stats(b + 1, 1 - p, q + p)
                weigh(1)
                if not last:
                    norm_apply(b + 1, 1 - p)
                weigh(2)
                weigh(3)
                conv2_out(0)
                for t in range(4, T):
                    weigh(t)
                conv2_out(1)
                for i in range(4):
                    c, h = divmod(i, 2)
                    cut = slice(h * HALF, (h + 1) * HALF)
                    dve.wait_ge(act_nmp, 4 * b + i + 1)
                    nc.vector.tensor_copy(n_hi[:, c, cut], nf[:, i % 2]).then_inc(n_hi_done, 1)
                    dve.wait_ge(n_hi_done, 4 * b + i + 1)
                    nc.vector.tensor_tensor(n_lo[:, c, cut], nf[:, i % 2], n_hi[:, c, cut], ALU.subtract).then_inc(n_done, 1)
                if not last:
                    hidden(b + 1, 1 - p)
                for m in range(C):
                    for h in range(H):
                        i = 4 * b + 2 * m + h
                        dve.wait_ge(act_r, i + 1)
                        nc.vector.scalar_tensor_tensor(cand[:, h], tr[:, h], 1.0, cand[:, h], ALU.add, ALU.mult).then_inc(g_rh, 1)
                        dve.wait_ge(pe_in, i + 1)
                        dve.wait_ge(g_rh, i + 1)
                        nc.vector.scalar_tensor_tensor(cand[:, h], ps[:, 6 + h, :], 1.0 / WSCALE, cand[:, h],
                                                       ALU.mult, ALU.add).then_inc(g_cand, 1)
                    for h in range(H):
                        i = 4 * b + 2 * m + h
                        cut = slice(h * HALF, (h + 1) * HALF)
                        dve.wait_ge(pool_d, i + 1)
                        nc.vector.tensor_tensor(res[:, m, cut], res[:, m, cut], h_lo[:, p, m, cut], ALU.add).then_inc(g_dlo, 1)
                        dve.wait_ge(g_dlo, i + 1)
                        dve.wait_ge(act_z, i + 1)
                        nc.vector.scalar_tensor_tensor(res[:, m, cut], tz[:, h], 1.0, res[:, m, cut], ALU.add, ALU.mult).then_inc(g_mix, 1)
                        dve.wait_ge(g_mix, i + 1)
                        nc.vector.scalar_tensor_tensor(res[:, m, cut], res[:, m, cut], 0.5, cand[:, h],
                                                       ALU.mult, ALU.add).then_inc(g_res, 1)

            def add_rows(b, p):
                for k in range(4):
                    dve.wait_ge(pe_out, 4 * b + k + 1)
                    dve.wait_ge(stored[k % 2], 16 * (2 * b + k // 2 + 1))
                    nc.vector.tensor_tensor(ot[:, k % 2], ps[:, 4 + k, :].rearrange("p (t d) -> p t d", t=2),
                                            xrow[:, p, 2 * k:2 * k + 2], ALU.add).then_inc(out_done, 1)

            norm_stats(0, 0, 0)
            norm_apply(0, 0)
            hidden(0, 0)
            batches(dve, body)
            add_rows(B - 1, 1)

        @block.tensor
        def _(pe):
            def weight(off, k, width, lo, n):
                at = off + k * width + lo
                return w_hi[:, at:at + n], w_lo[:, at:at + n]

            def three(banks, w, v_hi, v_lo, start, stop):
                for n, (wt, v) in enumerate(((w[0], v_hi), (w[0], v_lo), (w[1], v_hi))):
                    for h, bank in enumerate(banks):
                        out_ins[h] = nc.tensor.matmul(ps[:, bank, :], wt, v(h), start=(start and n == 0), stop=(stop and n == 2))

            out_ins = [None, None]

            def transposed(b):
                for i in range(4):
                    c, h = divmod(i, 2)
                    pe.wait_ge(ln_xn, T * b + 4 * h + 4)
                    if not first(b):
                        if i == 0:
                            pe.wait_ge(act_exp, T * b)
                        if i == 2:
                            pe.wait_ge(c2_hi, 4 * b)
                    for t in range(4):
                        last = nc.tensor.transpose(ps[:, i, t * P:(t + 1) * P], xn[:, 4 * h + t, c * P:(c + 1) * P], eye[:])
                    last.then_inc(pe_h, 1)

            def to_rows(b):
                pe.wait_ge(g_res, 4 * (b + 1))
                for k in range(4):
                    for t in range(2):
                        for c in range(C):
                            last = nc.tensor.transpose(ps[:, 4 + k, t * D + c * P:t * D + (c + 1) * P],
                                                       res[:, c, (2 * k + t) * P:(2 * k + t + 1) * P], eye[:])
                    last.then_inc(pe_out, 1)

            def body(b, p, q, last):
                pe.wait_ge(h_done, 4 * (b + 1))
                wait(pe, act_z, 4 * b)
                wait(pe, g_cand, 4 * b)
                for m in range(C):
                    for k in range(C):
                        three((4 + 2 * m, 5 + 2 * m), weight(OFF_CONV1, k, D, m * P, P),
                              lambda h: h_hi[:, p, k, h * HALF:(h + 1) * HALF],
                              lambda h: h_lo[:, p, k, h * HALF:(h + 1) * HALF], k == 0, k == C - 1)
                    out_ins[0].then_inc(pe_conv1, 1)
                    out_ins[1].then_inc(pe_conv1, 1)
                wait(pe, act_hn, 4 * b)
                wait(pe, act_r, 4 * b)
                if first(b):
                    pe.wait_ge(act_h, 4)
                for t in range(T):
                    if t >= 4:
                        pe.wait_ge(msg_f, T * b + t - 3)
                    for k in range(C):
                        wh, wl = weight(OFF_MSG, k, MW, 0, MW)
                        cut = slice(t * P, (t + 1) * P)
                        for n, (v, w) in enumerate(((h_hi, wh), (h_hi, wl), (h_lo, wh))):
                            ins = nc.tensor.matmul(ps[:, t % 4, 0:MW], v[:, p, k, cut], w,
                                                   start=(k == 0 and n == 0), stop=(k == C - 1 and n == 2))
                    ins.then_inc(pe_msg, 1)
                if not first(b):
                    pe.wait_ge(act_h1, 4 * (b + 1))
                    to_rows(b - 1)
                pe.wait_ge(h1_done, 4 * (b + 1))

                def stacks():
                    pe.wait_ge(stack_done, b + 1)
                    if first(b):
                        pe.wait_ge(act_h1, 4)
                    wait(pe, out_done, 4 * b)
                    for i, src in enumerate((RS, LS)):
                        for t in range(T):
                            ins = nc.tensor.transpose(ps[:, 4 + i, :].bitcast(BF16)[:, t * P:(t + 1) * P], src[:, t], eye_b[:])
                        ins.then_inc(pe_stack, 1)

                def distances(t):
                    if t >= 4:
                        bank = 0
                        if t == 4:
                            pe.wait_ge(c2_hi, 4 * b + 2)
                        else:
                            pe.wait_ge(act_exp, T * b + t)
                    else:
                        bank = 4 if t % 2 else 6
                        pe.wait_ge(act_stack, 2 * (b + 1))
                        if t >= 2:
                            pe.wait_ge(act_exp, T * b + t - 1)
                    for h in range(H):
                        ins = nc.tensor.matmul(ps[:, bank + h, :], LT[:, t * P:(t + 1) * P], RT[:, h * HALF:(h + 1) * HALF],
                                               start=True, stop=True)
                    ins.then_inc(pe_dist, 1)

                def passing(t):
                    if t == 0:
                        pe.wait_ge(act_exp, T * b + 4)
                    pe.wait_ge(pool_alo, T * b + t + 1)
                    if t == 0:
                        pe.wait_ge(m_done, T * (b + 1))
                    for d in range(C):
                        cut = slice(d * P, (d + 1) * P)
                        three((4 + 2 * d, 5 + 2 * d), (m_hi[:, t, cut], m_lo[:, t, cut]),
                              lambda h: a_hi[:, t % 4, h * HALF:(h + 1) * HALF],
                              lambda h: a_lo[:, t % 4, h * HALF:(h + 1) * HALF], t == 0, t == T - 1)
                    out_ins[1].then_inc(pe_chunk, 1)

                between = {(0, 4): [stacks]}
                for t in range(4):
                    between[0, 8 + 6 * t] = [lambda t=t: distances(t)]
                    between[1, 1 + 6 * t] = [lambda t=t: passing(t)]
                    between[1, 2 + 6 * t] = [lambda t=t: distances(4 + t)]
                    between[1, 24 + 3 * t] = [lambda t=t: passing(4 + t)]
                wait(pe, msg_f, T * (b + 1))
                for m in range(C):
                    for s in range(C * TAPS):
                        k, tap = divmod(s, TAPS)
                        at = OFF_CONV2 + (k * TAPS + tap) * D + m * P
                        three((2 * m, 2 * m + 1), (w_hi[:, at:at + P], w_lo[:, at:at + P]),
                              lambda h: h1_hi[:, k, tap + h * HALF:tap + (h + 1) * HALF],
                              lambda h: h1_lo[:, k, tap + h * HALF:tap + (h + 1) * HALF], s == 0, s == C * TAPS - 1)
                        if s == C * TAPS - 1:
                            out_ins[0].then_inc(pe_conv2, 1)
                            out_ins[1].then_inc(pe_conv2, 1)
                        for f in between.get((m, s), ()):
                            f()
                if not last:
                    transposed(b + 1)

                def gate(banks, col, srcs, done):
                    for n, (off, k, hi, lo) in enumerate(srcs):
                        three(banks, weight(off, k, 3 * D, col, P), hi, lo, n == 0, n == len(srcs) - 1)
                    out_ins[0].then_inc(done, 1)
                    out_ins[1].then_inc(done, 1)

                def operand(off, k, hi, lo):
                    return (off, k, lambda h: hi[:, h * HALF:(h + 1) * HALF], lambda h: lo[:, h * HALF:(h + 1) * HALF])

                from_h = [operand(OFF_HH, k, h_hi[:, p, k], h_lo[:, p, k]) for k in range(C)]
                from_c = [operand(OFF_IH, k, xc_hi[:, k], xc_lo[:, k]) for k in range(C)]
                from_n = [operand(OFF_IH, C + k, n_hi[:, k], n_lo[:, k]) for k in range(C)]
                for m in range(C):
                    if m == 0:
                        if last:
                            pe.wait_ge(act_exp, T * (b + 1))
                            pe.wait_ge(c2_hi, 4 * (b + 1))
                        else:
                            pe.wait_ge(act_h, 4 * (b + 2))
                    else:
                        pe.wait_ge(act_hn, 4 * b + 2)
                        pe.wait_ge(act_r, 4 * b + 2)
                    gate((0, 1), 2 * D + m * P, from_h, pe_hn)
                    if m == 0:
                        pe.wait_ge(xc_done, 4 * (b + 1))
                        pe.wait_ge(n_done, 4 * (b + 1))
                    gate((2, 3), m * P, from_h + from_c + from_n, pe_r)
                    if m == 0:
                        pe.wait_ge(act_nmp, 4 * (b + 1))
                    else:
                        pe.wait_ge(act_z, 4 * b + 2)
                        pe.wait_ge(g_cand, 4 * b + 2)
                    gate((4, 5), D + m * P, from_h + from_c + from_n, pe_z)
                    gate((6, 7), 2 * D + m * P, from_c + from_n, pe_in)

            pe.wait_ge(w_used, NCHUNK)
            transposed(0)
            batches(pe, body)
            pe.wait_ge(g_cand, 4 * B)
            pe.wait_ge(act_z, 4 * B)
            to_rows(B - 1)


def kernel(x, adj, L0_gnn_W1, L0_gnn_b1, L0_gnn_W2, L0_gnn_b2, L0_gnn_fusion_w,
           L1_gnn_w_se, L1_gnn_b_se, L1_gnn_conv1_w, L1_gnn_bn1_g, L1_gnn_bn1_b, L1_gnn_bn1_m, L1_gnn_bn1_v,
           L1_gnn_conv2_w, L1_gnn_bn2_g, L1_gnn_bn2_b, L1_gnn_bn2_m, L1_gnn_bn2_v, L1_gnn_w_msg, L1_gnn_b_msg,
           L1_gnn_w_ih, L1_gnn_b_ih, L1_gnn_w_hh, L1_gnn_b_hh):
    import numpy as np
    import concourse.bacc as bacc
    from concourse.bass_utils import run_bass_kernel_spmd

    def chunks(w):
        w = np.asarray(w)
        return np.moveaxis(w.reshape(w.shape[0] // P, P, -1), 0, 1).reshape(P, -1)

    def columns(v):
        return np.asarray(v).reshape(-1, P).T

    masks = np.zeros((P, NG * P + NG), np.float32)
    for g, nodes in enumerate(GROUPS):
        for j in range(PER):
            masks[:, [g * P + j * SLOT + n for n in nodes]] = 1
            masks[[j * SLOT + n for n in nodes], NG * P + g] = 1
    t = np.transpose
    arrays = {
        "x": x,
        "adj_t": t(adj, (0, 2, 1)),
        "adj_head": adj[:, :NODES, :NODES],
        "l0_w1": L0_gnn_W1,
        "l0_w2": L0_gnn_W2,
        "l0_b1": columns(L0_gnn_b1.reshape(-1)),
        "l0_b2": L0_gnn_b2,
        "fusion_w": L0_gnn_fusion_w,
        "masks": masks,
        "eye": np.eye(P, dtype=np.float32),
        "weights": np.concatenate([
            chunks(t(L1_gnn_conv1_w[:, :, 0])),
            chunks(np.concatenate([t(L1_gnn_w_msg), t(L1_gnn_w_se)], axis=1)),
            chunks(t(L1_gnn_conv2_w, (1, 2, 0))),
            chunks(t(L1_gnn_w_ih)),
            chunks(t(L1_gnn_w_hh))], axis=1),
        "cols": np.concatenate([columns(v) for v in (
            L1_gnn_bn1_g, L1_gnn_bn1_b, L1_gnn_bn1_m, L1_gnn_bn1_v,
            L1_gnn_bn2_g, L1_gnn_bn2_b, L1_gnn_bn2_m, L1_gnn_bn2_v, L1_gnn_b_ih, L1_gnn_b_hh)], axis=1),
        "row": np.concatenate([L1_gnn_b_msg, L1_gnn_b_se]),
    }
    arrays = {f"in_{name}": np.ascontiguousarray(a) for name, a in arrays.items()}
    nc = bacc.Bacc("TRN2", target_bir_lowering=False, num_devices=1)
    args = [nc.dram_tensor(name, a.shape, mybir.dt.from_np(a.dtype), kind="ExternalInput").ap()
            for name, a in arrays.items()]
    out = nc.dram_tensor("out_0", x.shape, F32, kind="ExternalOutput").ap()
    build(nc, *args, out)
    ran = run_bass_kernel_spmd(nc, [arrays], core_ids=[0])
    return ran.results[0]["out_0"]
```

```python
from contextlib import ExitStack

import concourse.bass as bass
from concourse import mybir

F32 = mybir.dt.float32
F16 = mybir.dt.float16
BF16 = mybir.dt.bfloat16
ALU = mybir.AluOpType
ACT = mybir.ActivationFunctionType
AX = mybir.AxisListType

P = 128
HALF = 512
WSCALE = 16.0
ASCALE = 256.0
EPS = 1e-5

NODES = 25
GROUPS = [list(range(25)), list(range(9)), [0, 9, 10, 11, 12, 13, 14],
          [6, 7, 8, 12, 13, 14], [3, 4, 5, 9, 10, 11]]
RUN = [(min(g), max(g) - min(g) + 1) for g in GROUPS]
NG = len(GROUPS)
SLOT = 32
PER = P // SLOT

PAIRS = [(0, 0), (0, 1), (1, 0), (1, 1), (0, 2), (2, 0)]


def wait(engine, sem, value):
    if isinstance(value, int) and value <= 0:
        return
    engine.wait_ge(sem, value)


def build(nc, x, adj_t, adj_head, l0_w1, l0_w2, l0_b1, l0_b2, fusion_w, masks, eye_d, weights, cols_d, row_d, out):
    B, N, D = x.shape
    HID = l0_w1.shape[-1]
    C = D // P
    HC = HID // P
    T = N // P
    H = N // HALF
    Q = B // PER
    TAPS = 17
    PAD = TAPS // 4
    QCUT = HALF // 2 + 1
    ADJ_RING = 4
    ROWS = NODES + 1
    MW = D + 3
    OFF_CONV1 = 0
    OFF_MSG = OFF_CONV1 + C * D
    OFF_CONV2 = OFF_MSG + C * MW
    OFF_IH = OFF_CONV2 + C * TAPS * D
    OFF_HH = OFF_IH + 2 * C * 3 * D
    NW = OFF_HH + C * 3 * D
    OFF_SUM = NW
    WCHUNK = 4 * D
    NCHUNK = -(-NW // WCHUNK)
    NSUM = C * 8 * D // WCHUNK
    WACT = NCHUNK + NSUM - NG
    assert weights.shape[1] == NW and H == 2 and C == 2 and T == 8

    with ExitStack() as ctx:
        def sem(name):
            return ctx.enter_context(nc.semaphore(name))

        def keep(name, shape, dt):
            return ctx.enter_context(nc.sbuf_tensor(name, shape, dt))

        w_hi = keep("w_hi", [P, NW + NSUM * WCHUNK], F16)
        w_lo = keep("w_lo", [P, NW + NSUM * WCHUNK], F16)
        eye = keep("eye", [P, P], F32)
        eye_b = keep("eye_b", [P, P], BF16)
        cols = keep("cols", [P, 28], F32)
        bn_scale = keep("bn_scale", [P, 4], F32)
        bn_psum = keep("bn_psum", [P, 4], F32)
        bn_shift = keep("bn_shift", [P, 4], F32)
        gate_b = keep("gate_b", [P, 6], F32)
        row_b = keep("row_b", [P, MW], F32)
        half_neg = keep("half_neg", [P, 4 * NG], F32)
        ps = ctx.enter_context(nc.psum_tensor("ps", [P, 8, HALF], F32))
        xnew = nc.dram_tensor("xnew", [B, ROWS, D], F32).ap()

        l0_small = sem("l0_small_loaded")
        l0_x = sem("l0_x_loaded")
        l0_w1_in = sem("l0_w1_loaded")
        l0_w2_in = [sem(f"l0_w2_loaded{g}") for g in range(NG)]
        w_in = [sem(f"w_raw_loaded{i}") for i in range(4)]
        w_summed = sem("w_summed")
        zeroed = sem("l0_zeroed")
        chain = sem("dve_chain")
        deg_ready = sem("deg_ready")
        pool_dinv = sem("pool_dinv")
        b_ready = sem("l0_b_ready")
        pe_nt = sem("pe_nt")
        nt_ready = sem("nt_ready")
        var0_ready = sem("var0_ready")
        pool_rstd0 = sem("pool_rstd0")
        h0_ready = sem("h0_ready")
        pe_agg1 = sem("pe_agg1")
        g_ready = sem("g_ready")
        pe_w1 = sem("pe_w1")
        h2_ready = sem("h2_ready")
        pe_w2 = sem("pe_w2")
        s2t_ready = sem("s2t_ready")
        pe_s2 = sem("pe_s2")
        s2_ready = sem("s2_ready")
        pe_agg2 = sem("pe_agg2")
        act_chain = sem("act_chain")
        fus_ready = sem("fus_ready")
        fus_max = sem("fus_max")
        rw_ready = sem("rw_ready")
        relu2 = sem("relu2")
        acc_done = sem("acc_done")
        xnew_ready = sem("xnew_ready")
        xnew_stored = sem("xnew_stored")
        var_bn = sem("var_bn")
        pool_bn = sem("pool_bn")
        w_split = sem("w_split")
        w_used = sem("w_raw_used")
        consts_ready = sem("consts_ready")
        half_set = sem("half_set")
        eyeb_ready = sem("eyeb_ready")

        with ExitStack() as l0:
            def sb(name, shape, dt=F32):
                return l0.enter_context(nc.sbuf_tensor(name, shape, dt))

            x0 = sb("x0", [P, Q, D])
            h0 = sb("h0", [P, Q, D])
            A = sb("A", [P, Q, P])
            AM = sb("AM", [P, NG, Q, P])
            NT = sb("NT", [P, NG, Q, P])
            mask = sb("mask", [P, NG, P])
            rowmask = sb("rowmask", [P, NG])
            W = sb("W", [P, NG, C * HID])
            W1 = W[:].rearrange("p g (c h) -> p g c h", c=C)
            W2 = W[:].rearrange("p g (c d) -> p g c d", c=HC)
            w_raw = sb("w_raw", [P, 4, WCHUNK])
            b1 = sb("b1", [P, NG, HC])
            b2 = sb("b2", [1, NG, D])
            ones = sb("ones", [1, P])
            fus = sb("fus", [P, NG])
            fmx = sb("fmx", [P, 1])
            fex = sb("fex", [P, NG])
            fsum = sb("fsum", [P, 2])
            rw = sb("rw", [P, NG])
            deg = sb("deg", [P, NG, Q])
            nz = sb("nz", [P, NG, Q])
            dinv = sb("dinv", [P, NG, Q])
            dm = sb("dm", [P, NG, Q])
            st0 = sb("st0", [P, Q, 6])
            mv0 = sb("mv0", [P, Q, 2])
            rs0 = sb("rs0", [P, Q])
            nm0 = sb("nm0", [P, Q])
            gT = [sb(f"gT{g}", [P, C, B * RUN[g][1]]) for g in range(NG)]
            h2 = [sb(f"h2{g}", [P, HC, B * RUN[g][1]]) for g in range(NG)]
            s2T = sb("s2T", [P, 2, C, B, SLOT])
            S2 = sb("S2", [P, 2, Q, D])
            r2 = sb("r2", [P, 2, Q, D])
            acc = sb("acc", [P, Q, D])

            with nc.Block() as block:
                @block.sync
                def _(sp):
                    sp.dma_start(mask[:], masks[:, 0:NG * P].rearrange("p (g n) -> p g n", g=NG)).then_inc(l0_small, 16)
                    sp.dma_start(rowmask[:], masks[:, NG * P:]).then_inc(l0_small, 16)
                    sp.dma_start(eye[:], eye_d).then_inc(l0_small, 16)
                    sp.dma_start(cols[:], cols_d).then_inc(l0_small, 16)
                    sp.dma_start(row_b[:], row_d.partition_broadcast(P)).then_inc(l0_small, 16)
                    sp.dma_start(fus[:], fusion_w.partition_broadcast(P)).then_inc(l0_small, 16)
                    sp.dma_start(b1[:], l0_b1.rearrange("p (g h) -> p g h", g=NG)).then_inc(l0_small, 16)
                    sp.dma_start(b2[:], l0_b2.rearrange("(a g) d -> a g d", a=1)).then_inc(l0_small, 16)
                    sp.wait_ge(zeroed, 2)
                    for j in range(PER):
                        lo = SLOT * j
                        sp.dma_start(A[lo:lo + NODES, :, lo:lo + NODES],
                                     adj_head.rearrange("(q j) n m -> j n q m", j=PER)[j]).then_inc(l0_small, 16)
                        sp.dma_start(x0[lo:lo + ROWS, :, :],
                                     x[:, 0:ROWS, :].rearrange("(q j) n d -> j n q d", j=PER)[j]).then_inc(l0_x, 16)
                    for g in range(NG):
                        sp.dma_start(W1[:, g], l0_w1[g].rearrange("(c p) h -> p c h", p=P)).then_inc(l0_w1_in, 16)
                    for i in range(NCHUNK + 2 * NSUM):
                        freed = i - 3 if i - 3 <= NCHUNK else NCHUNK + (i - 3 - NCHUNK + 1) // 2
                        wait(sp, w_used, freed)
                        if i < NCHUNK:
                            lo, n = i * WCHUNK, min(WCHUNK, NW - i * WCHUNK)
                        else:
                            s, addend = divmod(i - NCHUNK, 2)
                            k, half = divmod(s, 2)
                            lo, n = OFF_CONV2 + k * TAPS * D + (1, 9)[addend] * D + half * WCHUNK, WCHUNK
                        sp.dma_start(w_raw[:, i % 4, 0:n], weights[:, lo:lo + n]).then_inc(w_in[i % 4], 16)
                    sp.wait_ge(xnew_ready, 1)
                    for j in range(PER):
                        sp.dma_start(xnew.rearrange("(q j) n d -> j n q d", j=PER)[j],
                                     acc[SLOT * j:SLOT * j + ROWS, :, :]).then_inc(xnew_stored, 16)
                    sp.wait_ge(xnew_stored, 16 * PER)

                @block.gpsimd
                def _(pool):
                    nc.gpsimd.memset(A[:], 0.0).then_inc(zeroed, 1)
                    nc.gpsimd.memset(x0[:], 0.0).then_inc(zeroed, 1)
                    nc.gpsimd.memset(half_neg[:], -0.5).then_inc(half_set, 1)
                    nc.gpsimd.memset(s2T[:], 0.0).then_inc(zeroed, 1)
                    nc.gpsimd.memset(ones[:], 1.0).then_inc(zeroed, 1)
                    pool.wait_ge(half_set, 1)
                    pool.wait_ge(deg_ready, 1)
                    nc.gpsimd.tensor_tensor(dinv[:].rearrange("p g q -> p (g q)"), deg[:].rearrange("p g q -> p (g q)"),
                                            half_neg[:], ALU.pow).then_inc(pool_dinv, 1)
                    pool.wait_ge(var0_ready, 1)
                    nc.gpsimd.tensor_tensor(rs0[:], rs0[:], half_neg[:, 0:Q], ALU.pow).then_inc(pool_rstd0, 1)
                    pool.wait_ge(var_bn, 1)
                    nc.gpsimd.tensor_tensor(bn_scale[:], bn_scale[:], half_neg[:, 0:4], ALU.pow).then_inc(pool_bn, 1)

                @block.vector
                def _(dve):
                    step = [0]

                    def link(ins):
                        step[0] += 1
                        ins.then_inc(chain, 1)
                        dve.wait_ge(chain, step[0])

                    dve.wait_ge(l0_small, 16 * (8 + PER))
                    link(nc.vector.tensor_tensor(A[:], A[:], eye[:].unsqueeze(1).to_broadcast([P, Q, P]), ALU.add))
                    for g in range(NG):
                        last = nc.vector.tensor_tensor(AM[:, g], A[:], mask[:, g].unsqueeze(1).to_broadcast([P, Q, P]), ALU.mult)
                    link(last)
                    link(nc.vector.tensor_reduce(deg[:], AM[:], AX.X, ALU.add))
                    link(nc.vector.tensor_scalar(nz[:], deg[:], 0.0, None, ALU.is_equal))
                    nc.vector.tensor_tensor(deg[:], deg[:], nz[:], ALU.add).then_inc(deg_ready, 1)
                    dve.wait_ge(deg_ready, 1)
                    link(nc.vector.tensor_scalar(nz[:], nz[:], -1.0, 1.0, ALU.mult, ALU.add))
                    dve.wait_ge(l0_x, 16 * PER)
                    for q in range(Q):
                        last = nc.vector.bn_stats(st0[:, q], x0[:, q])
                    link(last)
                    for q in range(Q):
                        last = nc.vector.bn_aggr(mv0[:, q], st0[:, q])
                    link(last)
                    nc.vector.tensor_scalar(rs0[:], mv0[:, :, 1], EPS, None, ALU.add).then_inc(var0_ready, 1)
                    nc.vector.tensor_scalar(bn_scale[:, 0:2], cols[:, 6:8], EPS, None, ALU.add)
                    nc.vector.tensor_scalar(bn_scale[:, 2:4], cols[:, 14:16], EPS, None, ALU.add).then_inc(var_bn, 1)
                    dve.wait_ge(pool_dinv, 1)
                    link(nc.vector.tensor_tensor(dinv[:], dinv[:], nz[:], ALU.mult))
                    nc.vector.tensor_tensor(dm[:], dinv[:], rowmask[:].unsqueeze(2).to_broadcast([P, NG, Q]), ALU.mult)
                    link(nc.vector.tensor_tensor(AM[:].rearrange("p g q n -> p (g q) n"), AM[:].rearrange("p g q n -> p (g q) n"),
                                                 dinv[:].rearrange("p g q -> p (g q)").unsqueeze(2).to_broadcast([P, NG * Q, P]), ALU.mult))
                    nc.vector.tensor_copy(eye_b[:], eye[:]).then_inc(b_ready, 1)
                    dve.wait_ge(pool_rstd0, 1)
                    for q in range(Q):
                        last = nc.vector.tensor_scalar(h0[:, q], x0[:, q], mv0[:, q, 0:1], rs0[:, q:q + 1], ALU.subtract, ALU.mult)
                    link(last)
                    nc.vector.tensor_scalar(h0[:], h0[:], 0.0, None, ALU.max).then_inc(h0_ready, 1)
                    for g in range(NG):
                        dve.wait_ge(pe_nt, g + 1)
                        nc.vector.tensor_tensor(NT[:, g], ps[:, g, :].rearrange("p (q n) -> p q n", q=Q),
                                                dm[:, g].unsqueeze(2).to_broadcast([P, Q, P]), ALU.mult).then_inc(nt_ready, 1)
                    link(nc.vector.tensor_reduce(fmx[:], fus[:], AX.X, ALU.max))
                    nc.vector.tensor_scalar(fus[:], fus[:], fmx[:], None, ALU.subtract).then_inc(fus_max, 1)
                    dve.wait_ge(fus_ready, 1)
                    link(nc.vector.tensor_reduce(fsum[:, 0:1], fex[:], AX.X, ALU.add))
                    link(nc.vector.reciprocal(fsum[:, 1:2], fsum[:, 0:1]))
                    nc.vector.scalar_tensor_tensor(rw[:], fex[:], fsum[:, 1:2], rowmask[:], ALU.mult, ALU.mult).then_inc(rw_ready, 1)
                    dve.wait_ge(pool_bn, 1)
                    link(nc.vector.tensor_tensor(bn_scale[:, 0:2], bn_scale[:, 0:2], cols[:, 0:2], ALU.mult))
                    link(nc.vector.tensor_tensor(bn_scale[:, 2:4], bn_scale[:, 2:4], cols[:, 8:10], ALU.mult))
                    nc.vector.tensor_scalar(bn_psum[:], bn_scale[:], 1.0 / WSCALE, None, ALU.mult)
                    nc.vector.tensor_tensor(bn_shift[:, 0:2], bn_scale[:, 0:2], cols[:, 4:6], ALU.mult)
                    link(nc.vector.tensor_tensor(bn_shift[:, 2:4], bn_scale[:, 2:4], cols[:, 12:14], ALU.mult))
                    nc.vector.tensor_tensor(bn_shift[:, 0:2], cols[:, 2:4], bn_shift[:, 0:2], ALU.subtract)
                    nc.vector.tensor_tensor(bn_shift[:, 2:4], cols[:, 10:12], bn_shift[:, 2:4], ALU.subtract)
                    nc.vector.tensor_scalar(gate_b[:, 4:6], cols[:, 26:28], 0.5, None, ALU.mult)
                    link(nc.vector.tensor_tensor(gate_b[:, 0:4], cols[:, 16:20], cols[:, 22:26], ALU.add))
                    nc.vector.tensor_scalar(gate_b[:, 0:4], gate_b[:, 0:4], 0.5, None, ALU.mult).then_inc(consts_ready, 1)
                    def split(i):
                        at = i * WCHUNK
                        if i < NCHUNK:
                            n = min(WCHUNK, NW - at)
                            slot = i % 4
                            dve.wait_ge(w_in[slot], 16 * (i // 4 + 1))
                        else:
                            item = NCHUNK + 2 * (i - NCHUNK)
                            n = WCHUNK
                            at = OFF_SUM + (i - NCHUNK) * WCHUNK
                            slot = item % 4
                            dve.wait_ge(w_in[(item + 1) % 4], 16 * ((item + 1) // 4 + 1))
                            dve.wait_ge(w_in[slot], 16 * (item // 4 + 1))
                            nc.vector.tensor_tensor(w_raw[:, slot], w_raw[:, slot], w_raw[:, (item + 1) % 4], ALU.add).then_inc(w_summed, 1)
                            dve.wait_ge(w_summed, i - NCHUNK + 1)
                        if i >= WACT:
                            nc.vector.tensor_scalar(w_hi[:, at:at + n], w_raw[:, slot, 0:n], WSCALE, None, ALU.mult).then_inc(w_split, 1)
                        dve.wait_ge(w_split, i + 1)
                        nc.vector.scalar_tensor_tensor(w_lo[:, at:at + n], w_raw[:, slot, 0:n], WSCALE, w_hi[:, at:at + n],
                                                       ALU.mult, ALU.subtract).then_inc(w_used, 1)

                    for i in range(WACT):
                        split(i)
                    dve.wait_ge(zeroed, 4)

                    def slots(g):
                        lo, n = RUN[g]
                        for d in range(C):
                            i = g * C + d
                            dve.wait_ge(pe_w2, i + 1)
                            if g >= 2:
                                dve.wait_ge(pe_s2, 2 * (g - 1))
                            nc.vector.tensor_copy(s2T[:, g % 2, d, :, lo:lo + n],
                                                  ps[:, 5 + i % 3, 0:B * n].rearrange("p (b n) -> p b n", n=n)).then_inc(s2t_ready, 1)

                    def rows(g):
                        for k in range(2):
                            i = 2 * g + k
                            dve.wait_ge(pe_s2, i + 1)
                            if g >= 2:
                                dve.wait_ge(pe_agg2, 2 * (g - 1))
                            nc.vector.tensor_copy(S2[:, g % 2, 2 * k:2 * k + 2, :],
                                                  ps[:, i % 2, :].rearrange("p (q d) -> p q d", q=2)).then_inc(s2_ready, 1)

                    def fuse(g):
                        dve.wait_ge(relu2, 2 * g + 2)
                        if g == 0:
                            dve.wait_ge(h0_ready, 1)
                            nc.vector.tensor_tensor(acc[:], x0[:], r2[:, 0], ALU.add).then_inc(acc_done, 1)
                        else:
                            dve.wait_ge(acc_done, g)
                            ins = nc.vector.tensor_tensor(acc[:], acc[:], r2[:, g % 2], ALU.add)
                            ins.then_inc(xnew_ready if g == NG - 1 else acc_done, 1)

                    for g in range(NG + 2):
                        if g < NG:
                            slots(g)
                        if 1 <= g <= NG:
                            rows(g - 1)
                        if g >= 2:
                            fuse(g - 2)
                        if g < NG:
                            split(WACT + g)

                @block.scalar
                def _(act):
                    act.wait_ge(fus_max, 1)
                    nc.scalar.activation(fex[:], fus[:], ACT.Exp).then_inc(fus_ready, 1)
                    for i in range(NG * C):
                        g, c = divmod(i, C)
                        act.wait_ge(pe_agg1, i + 1)
                        nc.scalar.activation(gT[g][:, c, :], ps[:, 5 + i % 3, 0:B * RUN[g][1]], ACT.Copy).then_inc(g_ready, 1)
                    for i in range(NG * HC):
                        g, hc = divmod(i, HC)
                        if i < WACT:
                            n = min(WCHUNK, NW - i * WCHUNK)
                            act.wait_ge(w_in[i % 4], 16 * (i // 4 + 1))
                            nc.scalar.activation(w_hi[:, i * WCHUNK:i * WCHUNK + n], w_raw[:, i % 4, 0:n], ACT.Copy,
                                                 scale=WSCALE).then_inc(w_split, 1)
                        act.wait_ge(pe_w1, i + 1)
                        nc.scalar.activation(h2[g][:, hc, :], ps[:, i % 5, 0:B * RUN[g][1]], ACT.Relu,
                                             bias=b1[:, g, hc:hc + 1]).then_inc(h2_ready, 1)
                        if hc == HC - 1:
                            act.dma_start(W2[:, g], l0_w2[g].rearrange("(c p) d -> p c d", p=P)).then_inc(l0_w2_in[g], 16)
                    act.wait_ge(rw_ready, 1)
                    for i in range(NG * 2):
                        g, k = divmod(i, 2)
                        act.wait_ge(pe_agg2, i + 1)
                        if g >= 2:
                            act.wait_ge(acc_done, g - 1)
                        nc.scalar.activation(r2[:, g % 2, 2 * k:2 * k + 2, :],
                                             ps[:, 2 + i % 3, :].rearrange("p (q d) -> p q d", q=2),
                                             ACT.Relu, scale=rw[:, g:g + 1]).then_inc(relu2, 1)

                @block.tensor
                def _(pe):
                    pe.wait_ge(b_ready, 1)
                    pe.wait_ge(chain, 9)
                    for g in range(NG):
                        for q in range(Q):
                            last = nc.tensor.transpose(ps[:, g, q * P:(q + 1) * P], AM[:, g, q], eye[:])
                        last.then_inc(pe_nt, 1)
                    pe.wait_ge(h0_ready, 1)
                    for i in range(NG * C):
                        g, c = divmod(i, C)
                        lo, n = RUN[g]
                        pe.wait_ge(nt_ready, g + 1)
                        wait(pe, g_ready, i - 2)
                        for q in range(Q):
                            last = nc.tensor.matmul(ps[:, 5 + i % 3, q * PER * n:(q + 1) * PER * n].rearrange("p (j n) -> p j n", n=n),
                                                    h0[:, q, c * P:(c + 1) * P],
                                                    NT[:, g, q].rearrange("p (j n) -> p j n", n=SLOT)[:, :, lo:lo + n],
                                                    start=True, stop=True)
                        last.then_inc(pe_agg1, 1)
                    pe.wait_ge(l0_w1_in, 16 * NG)
                    for i in range(NG * HC):
                        g, hc = divmod(i, HC)
                        n = B * RUN[g][1]
                        pe.wait_ge(g_ready, C * (g + 1))
                        pe.wait_ge(nt_ready, NG)
                        wait(pe, h2_ready, i - 4)
                        for c in range(C):
                            last = nc.tensor.matmul(ps[:, i % 5, 0:n], W1[:, g, c, hc * P:(hc + 1) * P], gT[g][:, c, :],
                                                    start=(c == 0), stop=(c == C - 1))
                        last.then_inc(pe_w1, 1)
                    def second(g):
                        n = B * RUN[g][1]
                        pe.wait_ge(l0_w2_in[g], 16)
                        for d in range(C):
                            i = g * C + d
                            wait(pe, s2t_ready, i - 2)
                            for hc in range(HC):
                                last = nc.tensor.matmul(ps[:, 5 + i % 3, 0:n], W2[:, g, hc, d * P:(d + 1) * P], h2[g][:, hc, :],
                                                        start=(hc == 0), stop=(hc == HC - 1))
                            last.then_inc(pe_w2, 1)

                    def to_rows(g):
                        pe.wait_ge(s2t_ready, C * (g + 1))
                        for k in range(2):
                            i = 2 * g + k
                            wait(pe, s2_ready, i - 1)
                            for q in range(2):
                                for d in range(C):
                                    src = s2T[:, g % 2, d, (2 * k + q) * PER:(2 * k + q + 1) * PER, :].rearrange("p b n -> p (b n)")
                                    last = nc.tensor.transpose(ps[:, i % 2, q * D + d * P:q * D + (d + 1) * P], src, eye[:])
                            last.then_inc(pe_s2, 1)

                    def aggregate(g):
                        for k in range(2):
                            i = 2 * g + k
                            pe.wait_ge(s2_ready, i + 1)
                            wait(pe, relu2, i - 2)
                            for q in range(2):
                                dst = ps[:, 2 + i % 3, q * D:(q + 1) * D]
                                nc.tensor.matmul(dst, NT[:, g, 2 * k + q], S2[:, g % 2, 2 * k + q], start=True, stop=False)
                                last = nc.tensor.matmul(dst, ones[0:1, :], b2[0:1, g, :], start=False, stop=True)
                            last.then_inc(pe_agg2, 1)

                    pe.wait_ge(g_ready, NG * C)
                    pe.wait_ge(h2_ready, NG * HC)
                    pe.wait_ge(zeroed, 4)
                    for g in range(NG + 2):
                        if g < NG:
                            second(g)
                        if 1 <= g <= NG:
                            to_rows(g - 1)
                        if g >= 2:
                            aggregate(g - 2)

        def sb(name, shape, dt=F32):
            return ctx.enter_context(nc.sbuf_tensor(name, shape, dt))

        xrow = sb("xrow", [P, 2, T, D])
        xn = sb("xn", [P, T, D])
        res = xn[:].rearrange("p t d -> p (t d)").rearrange("p (c n) -> p c n", c=C)
        evac = sb("evac", [P, 4, HALF])
        mix = sb("mix", [P, HALF])
        odd = sb("odd", [P, HALF + 1])
        h_hi = sb("h_hi", [P, 2, C, N], F16)
        h_lo = sb("h_lo", [P, 2, C, N], F16)
        seq_hi = sb("seq_hi", [P, C, 3, HALF + 2 * PAD], F16)
        seq_lo = sb("seq_lo", [P, C, 3, HALF + 2 * PAD], F16)
        mf = sb("mf", [P, 4, D])
        m_hi = sb("m_hi", [P, T, D], F16)
        m_lo = sb("m_lo", [P, T, D], F16)
        emb = sb("emb", [P, T, 4])
        emb_r = sb("emb_r", [P, T, 4])
        parts = [sb(f"part{i}", [P, T, 4], BF16) for i in range(3)]
        ssq = sb("ssq", [P, T, 3])
        nsq = sb("nsq", [P, T])
        RS = sb("RS", [P, T, P], BF16)
        LS = sb("LS", [P, T, P], BF16)
        RT = sb("RT", [P, N], BF16)
        LT = sb("LT", [P, N], BF16)
        E = sb("E", [P, 2, HALF])
        a_hi = sb("a_hi", [P, T, HALF], F16)
        a_lo = sb("a_lo", [P, T, HALF], F16)
        adj = sb("adj", [P, ADJ_RING, HALF])
        c2f = sb("c2f", [P, 2, HALF])
        xc_hi = sb("xc_hi", [P, C, N], F16)
        xc_lo = sb("xc_lo", [P, C, N], F16)
        cand = sb("cand", [P, 2, HALF])
        tr = sb("tr", [P, 2, HALF])
        tz = sb("tz", [P, 2, HALF])

        def out_rows(k):
            return (c2f, tr)[k // 2][:, k % 2].rearrange("p (t d) -> p t d", t=2)

        stats = sb("stats", [P, T, 6])
        mv = sb("mv", [P, T, 3])
        rstd = sb("rstd", [P, T])

        def in_seq(buf, c, s):
            return buf[:, c, s, PAD:PAD + HALF]

        x_in = [sem(f"x_loaded{i}") for i in range(2)]
        adj_in = [sem(f"adj_loaded{i}") for i in range(ADJ_RING)]
        pads = sem("pads_zeroed")
        pe_h = sem("pe_h")
        pe_conv1 = sem("pe_conv1")
        pe_msg = sem("pe_msg")
        pe_out = sem("pe_out")
        pe_even = sem("pe_conv2_even_taps")
        pe_odd = sem("pe_conv2_odd_taps")
        pe_both = sem("pe_conv2_summed_taps")
        pe_stack = sem("pe_stack")
        pe_dist = sem("pe_dist")
        pe_piece = sem("pe_piece")
        pe_hn = sem("pe_hn")
        pe_r = sem("pe_r")
        pe_z = sem("pe_z")
        pe_in = sem("pe_in")
        seq_hi_done = sem("seq_hi_done")
        act_h = sem("act_h")
        act_h1 = sem("act_h1")
        act_relu_m = sem("act_relu_m")
        act_msg = sem("act_msg")
        act_stack = sem("act_stack")
        act_exp = sem("act_exp")
        act_ahi = sem("act_ahi")
        act_odd = sem("act_odd")
        act_xc = sem("act_xc")
        act_nmp = sem("act_nmp")
        act_hn = sem("act_hn")
        act_r = sem("act_r")
        act_z = sem("act_z")
        act_cand = sem("act_cand")
        ln_stats = sem("ln_stats")
        ln_sums = sem("ln_sums")
        ln_terms = sem("ln_terms")
        ln_var = sem("ln_var")
        ln_xn = sem("ln_xn")
        h_hi_done = sem("h_hi_done")
        h_done = sem("h_done")
        seq_sum = sem("seq_sum")
        sum_hi_done = sem("sum_hi_done")
        sum_done = sem("sum_done")
        seq_done = sem("seq_done")
        msg_f = sem("msg_f")
        emb_chain = sem("emb_chain")
        stack_done = sem("stack_done")
        out_done = sem("out_done")
        a_done = sem("a_done")
        c2_raw = sem("c2_raw")
        c2_hi = sem("c2_plus_hi")
        c2_done = sem("c2_done")
        xc_hi_done = sem("xc_hi_done")
        xc_done = sem("xc_done")
        n_hi_done = sem("n_hi_done")
        n_done = sem("n_done")
        g_rh = sem("g_rh")
        g_cand = sem("g_cand")
        g_dlo = sem("g_dlo")
        g_mix = sem("g_mix")
        g_res = sem("g_res")
        pool_rstd = sem("pool_rstd")
        pool_mlo = sem("pool_mlo")
        pool_alo = sem("pool_alo")
        pool_d = sem("pool_d")
        stored = [sem(f"out_stored{i}") for i in range(4)]

        BANK_CONV1 = (4, 5, 0, 1)
        BANK_MSG = (6, 7, 2, 3)
        BANK_OUT = (0, 1, 4, 5)
        BANK_STACK = (6, 7)
        BANK_DIST = (6, 7)
        BANK_EVEN, BANK_ODD, BANK_BOTH = 0, (1, 2), 3
        BANK_NMP = ((4, 5), (0, 1))
        BANK_H = (6, 7, 2, 3)
        BANK_HN, BANK_R, BANK_Z, BANK_IN = (6, 7), (2, 3), (4, 5), (0, 1)
        PIECES = H * T

        block = ctx.enter_context(nc.Block())

        def batches(engine, body):
            body(0, 0, 0, False)
            with engine.Fori(0, B // 2 - 1) as j:
                body(2 * j + 1, 1, j, False)
                body(2 * j + 2, 0, j + 1, False)
            body(B - 1, 1, B // 2 - 1, True)

        def first(b):
            return isinstance(b, int) and b == 0

        @block.sync
        def _(sp):
            def load_x(b, p):
                k = ROWS // 2
                sp.dma_start(xrow[k:P, p, 0:2, :], x[b, ROWS:2 * P, :].rearrange("(p r) d -> p r d", r=2)).then_inc(x_in[p], 16)
                for u in range(1, T // 2):
                    sp.dma_start(xrow[:, p, 2 * u:2 * u + 2, :],
                                 x[b, 2 * u * P:2 * (u + 1) * P, :].rearrange("(p r) d -> p r d", r=2)).then_inc(x_in[p], 16)
                sp.dma_start(xrow[0:k, p, 0:2, :], xnew[b].rearrange("(p r) d -> p r d", r=2)).then_inc(x_in[p], 16)

            def load_adj(b, j):
                h, t = divmod(j, T)
                wait(sp, a_done, PIECES * b + j + 1 - ADJ_RING)
                sp.dma_start(adj[:, j % ADJ_RING, :], adj_t[b, t * P:(t + 1) * P, h * HALF:(h + 1) * HALF])\
                    .then_inc(adj_in[j % ADJ_RING], 16)

            def store(b):
                for k in range(4):
                    sp.wait_ge(out_done, 4 * b + k + 1)
                    sp.dma_start(out[b, 2 * k * P:2 * (k + 1) * P, :].rearrange("(p r) d -> p r d", r=2),
                                 out_rows(k)).then_inc(stored[k], 16)

            def body(b, p, q, last):
                if not first(b):
                    store(b - 1)
                if not last:
                    load_x(b + 1, 1 - p)
                for j in range(ADJ_RING, PIECES):
                    load_adj(b, j)
                if not last:
                    for j in range(ADJ_RING):
                        load_adj(b + 1, j)

            load_x(0, 0)
            for j in range(ADJ_RING):
                load_adj(0, j)
            batches(sp, body)
            store(B - 1)
            for k in range(4):
                sp.wait_ge(stored[k], 16 * (B + 1))

        @block.gpsimd
        def _(pool):
            for buf in (seq_hi, seq_lo):
                nc.gpsimd.memset(buf[:], 0.0).then_inc(pads, 1)
            for k in range(4):
                nc.gpsimd.memset(out_rows(k), 0.0).then_inc(stored[k], 16)
            nc.gpsimd.memset(RS[:], 0.0).then_inc(pads, 1)
            nc.gpsimd.memset(LS[:], 0.0).then_inc(pads, 1)

            def norm(b):
                pool.wait_ge(ln_var, b + 1)
                nc.gpsimd.tensor_tensor(rstd[:], rstd[:], half_neg[:, 0:T], ALU.pow).then_inc(pool_rstd, 1)

            def body(b, p, q, last):
                for t in range(T):
                    pool.wait_ge(act_msg, T * b + t + 1)
                    nc.gpsimd.tensor_tensor(m_lo[:, t], mf[:, t % 4], m_hi[:, t], ALU.subtract).then_inc(pool_mlo, 1)
                for j in range(PIECES):
                    pool.wait_ge(act_ahi, PIECES * b + j + 1)
                    nc.gpsimd.tensor_tensor(a_lo[:, j % T], E[:, j % 2], a_hi[:, j % T], ALU.subtract).then_inc(pool_alo, 1)
                    if j == 2 and not last:
                        norm(b + 1)
                for i in range(4):
                    m, h = divmod(i, 2)
                    pool.wait_ge(act_cand, 4 * b + i + 1)
                    nc.gpsimd.tensor_tensor(res[:, m, h * HALF:(h + 1) * HALF], h_hi[:, p, m, h * HALF:(h + 1) * HALF],
                                            cand[:, h], ALU.subtract).then_inc(pool_d, 1)

            norm(0)
            batches(pool, body)

        @block.scalar
        def _(act):
            def hidden(b, p):
                for i in range(4):
                    act.wait_ge(pe_h, 4 * b + i + 1)
                    wait(act, n_done, 4 * (b - 1) + i + 1)
                    nc.scalar.activation(evac[:, i], ps[:, BANK_H[i], :], ACT.Relu).then_inc(act_h, 1)

            def body(b, p, q, last):
                if first(b):
                    act.wait_ge(pads, 4)
                for i in range(4):
                    m = i // 2
                    act.wait_ge(pe_conv1, 4 * b + i + 1)
                    act.wait_ge(h_done, 4 * b + i + 1)
                    nc.scalar.activation(evac[:, i], ps[:, BANK_CONV1[i], :], ACT.Relu, bias=bn_shift[:, m:m + 1],
                                         scale=bn_psum[:, m:m + 1]).then_inc(act_h1, 1)
                    act.wait_ge(act_h1, 4 * b + i + 1)
                    wait(act, pe_in, 4 * b)
                    nc.scalar.activation(in_seq(seq_hi, m, i % 2), evac[:, i], ACT.Copy).then_inc(seq_hi_done, 1)
                for t in range(T):
                    act.wait_ge(msg_f, T * b + t + 1)
                    nc.scalar.activation(mf[:, t % 4], mf[:, t % 4], ACT.Relu).then_inc(act_relu_m, 1)
                    act.wait_ge(act_relu_m, T * b + t + 1)
                    wait(act, pe_piece, PIECES * b)
                    nc.scalar.activation(m_hi[:, t], mf[:, t % 4], ACT.Copy).then_inc(act_msg, 1)
                wait(act, pe_dist, PIECES * b)
                for i, dst in enumerate((RT, LT)):
                    act.wait_ge(pe_stack, 2 * b + i + 1)
                    nc.scalar.activation(dst[:], ps[:, BANK_STACK[i], :].bitcast(BF16), ACT.Copy).then_inc(act_stack, 1)

                def weigh(j):
                    t = j % T
                    act.wait_ge(pe_dist, PIECES * b + j + 1)
                    wait(act, pool_alo, PIECES * b + j - 1)
                    nc.scalar.activation(E[:, j % 2], ps[:, BANK_DIST[j % 2], :], ACT.Exp, bias=nsq[:, t:t + 1]).then_inc(act_exp, 1)
                    act.wait_ge(a_done, PIECES * b + j + 1)
                    wait(act, pe_piece, PIECES * b + j - T + 1)
                    nc.scalar.activation(a_hi[:, t], E[:, j % 2], ACT.Copy).then_inc(act_ahi, 1)

                def odd_copy(m):
                    act.wait_ge(pe_odd, 2 * b + m + 1)
                    wait(act, c2_raw, 6 * b + 3 * m)
                    nc.scalar.activation(odd[:, 0:QCUT], ps[:, BANK_ODD[0], 0:QCUT], ACT.Copy).then_inc(act_odd, 1)
                    nc.scalar.activation(odd[:, QCUT:HALF + 1], ps[:, BANK_ODD[1], 0:HALF + 1 - QCUT], ACT.Copy).then_inc(act_odd, 1)

                def conv2_relu(m):
                    for r in range(H):
                        act.wait_ge(c2_done, 4 * b + 2 * m + r + 1)
                        nc.scalar.activation(c2f[:, r], c2f[:, r], ACT.Relu, bias=bn_shift[:, 2 + m:3 + m]).then_inc(act_xc, 1)

                for j in range(PIECES):
                    weigh(j)
                    if j % T == 5:
                        odd_copy(j // T)
                    if j == T:
                        conv2_relu(0)
                for i in range(4):
                    h, d = divmod(i, 2)
                    act.wait_ge(pe_piece, PIECES * b + (h + 1) * T)
                    act.wait_ge(sum_done, 2 * (b + 1))
                    nc.scalar.activation(evac[:, i], ps[:, BANK_NMP[h][d], :], ACT.Copy, scale=1.0 / ASCALE).then_inc(act_nmp, 1)
                    if i == 1:
                        conv2_relu(1)
                if not last:
                    hidden(b + 1, 1 - p)
                for m in range(C):
                    for h in range(H):
                        i = 4 * b + 2 * m + h
                        act.wait_ge(pe_hn, i + 1)
                        wait(act, g_res, i - 1)
                        nc.scalar.activation(cand[:, h], ps[:, BANK_HN[h], :], ACT.Identity, bias=gate_b[:, 4 + m:5 + m],
                                             scale=0.5 / WSCALE).then_inc(act_hn, 1)
                    for h in range(H):
                        act.wait_ge(pe_r, 4 * b + 2 * m + h + 1)
                        if m == 0:
                            act.wait_ge(stored[2 + h], 16 * (b + 1))
                        nc.scalar.activation(tr[:, h], ps[:, BANK_R[h], :], ACT.Tanh, bias=gate_b[:, m:m + 1],
                                             scale=0.5 / WSCALE).then_inc(act_r, 1)
                    for h in range(H):
                        act.wait_ge(pe_z, 4 * b + 2 * m + h + 1)
                        nc.scalar.activation(tz[:, h], ps[:, BANK_Z[h], :], ACT.Tanh, bias=gate_b[:, 2 + m:3 + m],
                                             scale=0.5 / WSCALE).then_inc(act_z, 1)
                    for h in range(H):
                        act.wait_ge(g_cand, 4 * b + 2 * m + h + 1)
                        nc.scalar.activation(cand[:, h], cand[:, h], ACT.Tanh, bias=cols[:, 20 + m:21 + m]).then_inc(act_cand, 1)

            hidden(0, 0)
            batches(act, body)

        @block.vector
        def _(dve):
            def norm_stats(b, p, q):
                dve.wait_ge(x_in[p], 16 * (T // 2 + 1) * (q + 1))
                for t in range(T):
                    last = nc.vector.bn_stats(stats[:, t], xrow[:, p, t])
                last.then_inc(ln_stats, 1)
                dve.wait_ge(ln_stats, b + 1)
                nc.vector.tensor_tensor(mv[:, :, 0], stats[:, :, 1], stats[:, :, 4], ALU.add)
                nc.vector.tensor_tensor(mv[:, :, 1], stats[:, :, 1], stats[:, :, 4], ALU.subtract)
                nc.vector.tensor_tensor(mv[:, :, 2], stats[:, :, 2], stats[:, :, 5], ALU.add).then_inc(ln_sums, 1)
                dve.wait_ge(ln_sums, b + 1)
                nc.vector.tensor_scalar(mv[:, :, 0], mv[:, :, 0], 0.5, None, ALU.mult)
                nc.vector.tensor_tensor(mv[:, :, 1], mv[:, :, 1], mv[:, :, 1], ALU.mult)
                nc.vector.tensor_scalar(mv[:, :, 2], mv[:, :, 2], 1.0 / D, EPS, ALU.mult, ALU.add).then_inc(ln_terms, 1)
                dve.wait_ge(ln_terms, b + 1)
                nc.vector.scalar_tensor_tensor(rstd[:], mv[:, :, 1], 0.25, mv[:, :, 2], ALU.mult, ALU.add).then_inc(ln_var, 1)

            def norm_apply(b, p):
                dve.wait_ge(pool_rstd, b + 1)
                wait(dve, pe_out, 4 * b - 4)
                for t in range(T):
                    ins = nc.vector.tensor_scalar(xn[:, t], xrow[:, p, t], mv[:, t, 0:1], rstd[:, t:t + 1],
                                                  ALU.subtract, ALU.mult)
                ins.then_inc(ln_xn, 1)

            def hidden(b, p):
                for i in range(4):
                    c, h = divmod(i, 2)
                    cut = slice(h * HALF, (h + 1) * HALF)
                    dve.wait_ge(act_h, 4 * b + i + 1)
                    nc.vector.tensor_copy(h_hi[:, p, c, cut], evac[:, i]).then_inc(h_hi_done, 1)
                    dve.wait_ge(h_hi_done, 4 * b + i + 1)
                    nc.vector.tensor_tensor(h_lo[:, p, c, cut], evac[:, i], h_hi[:, p, c, cut], ALU.subtract).then_inc(h_done, 1)

            def add_rows(b, p, ks):
                for k in ks:
                    dve.wait_ge(pe_out, 4 * b + k + 1)
                    dve.wait_ge(stored[k], 16 * (b + 1))
                    nc.vector.tensor_tensor(out_rows(k), ps[:, BANK_OUT[k], :].rearrange("p (t d) -> p t d", t=2),
                                            xrow[:, p, 2 * k:2 * k + 2], ALU.add).then_inc(out_done, 1)

            def body(b, p, q, last):
                def split_conv1(c, s):
                    i = 4 * b + 2 * c + s + 1
                    dve.wait_ge(seq_hi_done, i)
                    nc.vector.tensor_tensor(in_seq(seq_lo, c, s), evac[:, 2 * c + s], in_seq(seq_hi, c, s),
                                            ALU.subtract).then_inc(seq_done, 1)

                def split_sum(c):
                    i = 2 * b + c + 1
                    wait(dve, sum_done, i - 1)
                    nc.vector.tensor_tensor(mix[:], evac[:, 2 * c], evac[:, 2 * c + 1], ALU.add).then_inc(seq_sum, 1)
                    dve.wait_ge(seq_sum, i)
                    nc.vector.tensor_copy(in_seq(seq_hi, c, 2), mix[:]).then_inc(sum_hi_done, 1)
                    dve.wait_ge(sum_hi_done, i)
                    nc.vector.tensor_tensor(in_seq(seq_lo, c, 2), mix[:], in_seq(seq_hi, c, 2), ALU.subtract).then_inc(sum_done, 1)

                def message(t):
                    bank = BANK_MSG[t % 4]
                    dve.wait_ge(pe_msg, T * b + t + 1)
                    nc.vector.scalar_tensor_tensor(emb[:, t, 0:3], ps[:, bank, D:MW], 1.0 / WSCALE, row_b[:, D:MW],
                                                   ALU.mult, ALU.add)
                    wait(dve, pool_mlo, T * b + t - 3)
                    nc.vector.scalar_tensor_tensor(mf[:, t % 4], ps[:, bank, 0:D], 1.0 / WSCALE, row_b[:, 0:D],
                                                   ALU.mult, ALU.add).then_inc(msg_f, 1)

                wait(dve, pe_in, 4 * b)
                if first(b):
                    dve.wait_ge(pads, 4)
                for i in range(3):
                    split_conv1(i // 2, i % 2)
                    message(2 * i)
                    message(2 * i + 1)
                message(T - 2)
                message(T - 1)
                if not first(b):
                    add_rows(b - 1, 1 - p, (0, 1))
                split_conv1(1, 1)
                if not first(b):
                    add_rows(b - 1, 1 - p, (2, 3))
                LINKS = 7
                n = 0

                def link(ins):
                    nonlocal n
                    n += 1
                    ins.then_inc(emb_chain, 1)
                    dve.wait_ge(emb_chain, LINKS * b + n)

                wait(dve, act_exp, PIECES * b)
                dve.wait_ge(msg_f, T * (b + 1))
                link(nc.vector.tensor_tensor(ssq[:], emb[:, :, 0:3], emb[:, :, 0:3], ALU.mult))
                link(nc.vector.tensor_reduce(emb[:, :, 3], ssq[:], AX.X, ALU.add))
                nc.vector.tensor_scalar(nsq[:], emb[:, :, 3], -1.0, None, ALU.mult)
                link(nc.vector.tensor_copy(parts[0][:], emb[:]))
                link(nc.vector.tensor_tensor(emb_r[:], emb[:], parts[0][:], ALU.subtract))
                link(nc.vector.tensor_copy(parts[1][:], emb_r[:]))
                link(nc.vector.tensor_tensor(emb_r[:], emb_r[:], parts[1][:], ALU.subtract))
                link(nc.vector.tensor_copy(parts[2][:], emb_r[:]))
                wait(dve, pe_stack, 2 * b)
                for k, (left, right) in enumerate(PAIRS):
                    if first(b) and left == 0:
                        nc.vector.memset(LS[:, :, 4 * k + 3:4 * k + 4], -1.0)
                    nc.vector.tensor_copy(RS[:, :, 4 * k:4 * k + 4], parts[right][:])
                    ins = nc.vector.tensor_scalar(LS[:, :, 4 * k:4 * k + 3], parts[left][:, :, 0:3], 2.0, None, ALU.mult)
                ins.then_inc(stack_done, 1)

                def weigh(j):
                    per = PIECES // ADJ_RING
                    dve.wait_ge(adj_in[j % ADJ_RING], 16 * (per * b + j // ADJ_RING + 1))
                    dve.wait_ge(act_exp, PIECES * b + j + 1)
                    nc.vector.scalar_tensor_tensor(E[:, j % 2], E[:, j % 2], ASCALE, adj[:, j % ADJ_RING],
                                                   ALU.mult, ALU.mult).then_inc(a_done, 1)

                def even_rows(m):
                    dve.wait_ge(pe_even, 2 * b + m + 1)
                    dve.wait_ge(act_odd, 4 * b + 2 * m + 2)
                    wait(dve, xc_done, 4 * b + 2 * m - 1)
                    if m == 0:
                        for k in range(2):
                            dve.wait_ge(stored[k], 16 * (b + 1))
                    nc.vector.tensor_tensor(c2f[:, 0], ps[:, BANK_EVEN, :], odd[:, 0:HALF], ALU.add).then_inc(c2_raw, 1)
                    nc.vector.tensor_tensor(mix[:], ps[:, BANK_EVEN, :], odd[:, 1:HALF + 1], ALU.add).then_inc(c2_raw, 1)

                def odd_rows(m):
                    dve.wait_ge(pe_both, 2 * b + m + 1)
                    dve.wait_ge(c2_raw, 6 * b + 3 * m + 2)
                    wait(dve, xc_done, 4 * b + 2 * m)
                    nc.vector.tensor_tensor(c2f[:, 1], ps[:, BANK_BOTH, :], mix[:], ALU.subtract).then_inc(c2_raw, 1)
                    for r in range(H):
                        i = 4 * b + 2 * m + r
                        cut = slice(r * HALF, (r + 1) * HALF)
                        if r == 1:
                            dve.wait_ge(c2_raw, 6 * b + 3 * m + 3)
                        nc.vector.scalar_tensor_tensor(c2f[:, r], c2f[:, r], bn_psum[:, 2 + m:3 + m],
                                                       h_hi[:, p, m, cut], ALU.mult, ALU.add).then_inc(c2_hi, 1)
                        dve.wait_ge(c2_hi, i + 1)
                        nc.vector.tensor_tensor(c2f[:, r], c2f[:, r], h_lo[:, p, m, cut], ALU.add).then_inc(c2_done, 1)

                def split_conv2(m):
                    if m == 0:
                        wait(dve, pe_in, 4 * b)
                    for r in range(H):
                        i = 4 * b + 2 * m + r
                        cut = slice(r * HALF, (r + 1) * HALF)
                        dve.wait_ge(act_xc, i + 1)
                        nc.vector.tensor_copy(xc_hi[:, m, cut], c2f[:, r]).then_inc(xc_hi_done, 1)
                        dve.wait_ge(xc_hi_done, i + 1)
                        nc.vector.tensor_tensor(xc_lo[:, m, cut], c2f[:, r], xc_hi[:, m, cut], ALU.subtract).then_inc(xc_done, 1)

                def split_nmp(i):
                    h, d = divmod(i, 2)
                    dve.wait_ge(act_nmp, 4 * b + i + 1)
                    nc.vector.tensor_copy(in_seq(seq_hi, d, h), evac[:, i]).then_inc(n_hi_done, 1)
                    dve.wait_ge(n_hi_done, 4 * b + i + 1)
                    nc.vector.tensor_tensor(in_seq(seq_lo, d, h), evac[:, i], in_seq(seq_hi, d, h),
                                            ALU.subtract).then_inc(n_done, 1)

                for j in range(PIECES):
                    weigh(j)
                    if j == 0:
                        split_sum(0)
                        split_sum(1)
                    if j == 1 and not last:
                        norm_stats(b + 1, 1 - p, q + p)
                    if j == 4 and not last:
                        norm_apply(b + 1, 1 - p)
                    if j == 6:
                        even_rows(0)
                    if j == 7:
                        odd_rows(0)
                    if j == 8:
                        split_conv2(0)
                    if j == 14:
                        even_rows(1)
                odd_rows(1)
                split_nmp(0)
                split_nmp(1)
                split_conv2(1)
                split_nmp(2)
                split_nmp(3)
                if not last:
                    hidden(b + 1, 1 - p)
                for m in range(C):
                    for h in range(H):
                        i = 4 * b + 2 * m + h
                        dve.wait_ge(act_r, i + 1)
                        nc.vector.scalar_tensor_tensor(cand[:, h], tr[:, h], 1.0, cand[:, h], ALU.add, ALU.mult).then_inc(g_rh, 1)
                        dve.wait_ge(pe_in, i + 1)
                        dve.wait_ge(g_rh, i + 1)
                        nc.vector.scalar_tensor_tensor(cand[:, h], ps[:, BANK_IN[h], :], 1.0 / WSCALE, cand[:, h],
                                                       ALU.mult, ALU.add).then_inc(g_cand, 1)
                    for h in range(H):
                        i = 4 * b + 2 * m + h
                        cut = slice(h * HALF, (h + 1) * HALF)
                        dve.wait_ge(pool_d, i + 1)
                        nc.vector.tensor_tensor(res[:, m, cut], res[:, m, cut], h_lo[:, p, m, cut], ALU.add).then_inc(g_dlo, 1)
                        dve.wait_ge(g_dlo, i + 1)
                        dve.wait_ge(act_z, i + 1)
                        nc.vector.scalar_tensor_tensor(res[:, m, cut], tz[:, h], 1.0, res[:, m, cut], ALU.add, ALU.mult).then_inc(g_mix, 1)
                        dve.wait_ge(g_mix, i + 1)
                        nc.vector.scalar_tensor_tensor(res[:, m, cut], res[:, m, cut], 0.5, cand[:, h],
                                                       ALU.mult, ALU.add).then_inc(g_res, 1)

            norm_stats(0, 0, 0)
            norm_apply(0, 0)
            hidden(0, 0)
            batches(dve, body)
            add_rows(B - 1, 1, range(4))

        @block.tensor
        def _(pe):
            out_ins = [None, None]

            def weight(off, k, width, lo, n):
                at = off + k * width + lo
                return w_hi[:, at:at + n], w_lo[:, at:at + n]

            def three(banks, w, v_hi, v_lo, start, stop):
                for n, (wt, v) in enumerate(((w[0], v_hi), (w[0], v_lo), (w[1], v_hi))):
                    for h, bank in enumerate(banks):
                        out_ins[h] = nc.tensor.matmul(ps[:, bank, :], wt, v(h), start=(start and n == 0), stop=(stop and n == 2))

            def transposed(b):
                pe.wait_ge(ln_xn, b + 1)
                wait(pe, act_exp, PIECES * b)
                wait(pe, c2_raw, 6 * b)
                for i in range(4):
                    c, h = divmod(i, 2)
                    for u in range(T // 2):
                        last = nc.tensor.transpose(ps[:, BANK_H[i], u * P:(u + 1) * P], xn[:, 2 * u + h, c * P:(c + 1) * P], eye[:])
                    last.then_inc(pe_h, 1)

            def to_rows(b):
                pe.wait_ge(g_res, 4 * (b + 1))
                for k in range(4):
                    for r in range(2):
                        for c in range(C):
                            last = nc.tensor.transpose(ps[:, BANK_OUT[k], r * D + c * P:r * D + (c + 1) * P],
                                                       res[:, c, r * HALF + k * P:r * HALF + (k + 1) * P], eye[:])
                    last.then_inc(pe_out, 1)

            def body(b, p, q, last):
                pe.wait_ge(h_done, 4 * (b + 1))
                for m in range(C):
                    if m == 0:
                        wait(pe, act_z, 4 * b)
                    else:
                        wait(pe, g_cand, 4 * b)
                    for k in range(C):
                        three(BANK_CONV1[2 * m:2 * m + 2], weight(OFF_CONV1, k, D, m * P, P),
                              lambda h: h_hi[:, p, k, h * HALF:(h + 1) * HALF],
                              lambda h: h_lo[:, p, k, h * HALF:(h + 1) * HALF], k == 0, k == C - 1)
                    out_ins[0].then_inc(pe_conv1, 1)
                    out_ins[1].then_inc(pe_conv1, 1)
                if first(b):
                    pe.wait_ge(act_h, 4)
                else:
                    pe.wait_ge(act_hn, 4 * b)
                    pe.wait_ge(act_r, 4 * b)
                for t in range(T):
                    if t >= 4:
                        pe.wait_ge(msg_f, T * b + t - 3)
                    for k in range(C):
                        wh, wl = weight(OFF_MSG, k, MW, 0, MW)
                        cut = slice(t * P, (t + 1) * P)
                        for n, (v, w) in enumerate(((h_hi, wh), (h_hi, wl), (h_lo, wh))):
                            ins = nc.tensor.matmul(ps[:, BANK_MSG[t % 4], 0:MW], v[:, p, k, cut], w,
                                                   start=(k == 0 and n == 0), stop=(k == C - 1 and n == 2))
                    ins.then_inc(pe_msg, 1)
                pe.wait_ge(act_h1, 4 * (b + 1))
                if not first(b):
                    to_rows(b - 1)

                def stacks():
                    pe.wait_ge(stack_done, b + 1)
                    for i, src in enumerate((RS, LS)):
                        for t in range(T):
                            ins = nc.tensor.transpose(ps[:, BANK_STACK[i], :].bitcast(BF16)[:, t * P:(t + 1) * P], src[:, t], eye_b[:])
                        ins.then_inc(pe_stack, 1)

                def distances(j):
                    h, t = divmod(j, T)
                    if j == 0:
                        pe.wait_ge(act_stack, 2 * (b + 1))
                    if j >= 2:
                        pe.wait_ge(act_exp, PIECES * b + j - 1)
                    nc.tensor.matmul(ps[:, BANK_DIST[j % 2], :], LT[:, t * P:(t + 1) * P], RT[:, h * HALF:(h + 1) * HALF],
                                     start=True, stop=True).then_inc(pe_dist, 1)

                def passing(j):
                    h, t = divmod(j, T)
                    if j == 0:
                        pe.wait_ge(pool_mlo, T * (b + 1))
                        wait(pe, out_done, 4 * b)
                    if j == T:
                        pe.wait_ge(act_odd, 4 * (b + 1))
                        pe.wait_ge(c2_raw, 6 * b + 5)
                    pe.wait_ge(pool_alo, PIECES * b + j + 1)
                    for d in range(C):
                        cut = slice(d * P, (d + 1) * P)
                        for n, (w, v) in enumerate(((m_hi, a_hi), (m_hi, a_lo), (m_lo, a_hi))):
                            ins = nc.tensor.matmul(ps[:, BANK_NMP[h][d], :], w[:, t, cut], v[:, t],
                                                   start=(t == 0 and n == 0), stop=(t == T - 1 and n == 2))
                    ins.then_inc(pe_piece, 1)

                between = {(0, 7): [stacks]}
                for t in range(T):
                    between.setdefault((0, 10 + 5 * t), []).append(lambda t=t: distances(t))
                    between.setdefault((1, 2 + 6 * t), []).append(lambda t=t: passing(t))
                    between.setdefault((1, 3 + 6 * t), []).append(lambda t=t: distances(T + t))

                def taps(m, kind):
                    for k in range(C):
                        raw = OFF_CONV2 + k * TAPS * D + m * P
                        for i in range(8 if kind == 1 else 9):
                            if kind == 0:
                                yield k, raw + i * D, 0, i
                            elif kind == 1:
                                yield k, raw + (9 + i) * D, 1, i
                            else:
                                yield k, (raw if i == 0 else OFF_SUM + (k * 8 + i - 1) * D + m * P), 2, i

                for m in range(C):
                    step = 0
                    for kind, done in enumerate((pe_even, pe_odd, pe_both)):
                        if kind == 0:
                            if m == 0:
                                wait(pe, out_done, 4 * b - 3)
                            else:
                                pe.wait_ge(c2_raw, 6 * b + 2)
                            spans = [(BANK_EVEN, 0, HALF)]
                        elif kind == 1:
                            if m == 0:
                                wait(pe, out_done, 4 * b - 2)
                                pe.wait_ge(msg_f, T * (b + 1))
                            else:
                                pe.wait_ge(act_odd, 4 * b + 2)
                            spans = [(BANK_ODD[0], 0, QCUT), (BANK_ODD[1], QCUT, HALF + 1 - QCUT)]
                        else:
                            if m == 1:
                                pe.wait_ge(c2_raw, 6 * b + 3)
                            spans = [(BANK_BOTH, 0, HALF)]
                        every = list(taps(m, kind))
                        for n, (k, at, s, col) in enumerate(every):
                            if m == 0 and col == 0 and kind < 2:
                                pe.wait_ge(seq_done, 4 * b + 2 * k + s + 1)
                            if m == 0 and col == 0 and kind == 2:
                                pe.wait_ge(sum_done, 2 * b + k + 1)
                            for i, (w, v) in enumerate(((w_hi, seq_hi), (w_hi, seq_lo), (w_lo, seq_hi))):
                                for bank, lo, width in spans:
                                    ins = nc.tensor.matmul(ps[:, bank, 0:width], w[:, at:at + P], v[:, k, s, col + lo:col + lo + width],
                                                           start=(n == 0 and i == 0), stop=(n == len(every) - 1 and i == 2))
                            if n == len(every) - 1:
                                ins.then_inc(done, 1)
                            for f in between.pop((m, step), ()):
                                f()
                            step += 1
                assert not between
                for t in range(T):
                    passing(T + t)
                if not last:
                    transposed(b + 1)

                def gate(banks, col, srcs, done, ready=None):
                    for n, (off, k, hi, lo) in enumerate(srcs):
                        if ready and n == len(srcs) - C:
                            pe.wait_ge(*ready)
                        three(banks, weight(off, k, 3 * D, col, P), hi, lo, n == 0, n == len(srcs) - 1)
                    out_ins[0].then_inc(done, 1)
                    out_ins[1].then_inc(done, 1)

                def operand(off, k, hi, lo):
                    return (off, k, lambda h: hi[:, h * HALF:(h + 1) * HALF], lambda h: lo[:, h * HALF:(h + 1) * HALF])

                from_h = [operand(OFF_HH, k, h_hi[:, p, k], h_lo[:, p, k]) for k in range(C)]
                from_c = [operand(OFF_IH, k, xc_hi[:, k], xc_lo[:, k]) for k in range(C)]
                from_n = [(OFF_IH, C + k, lambda h, k=k: in_seq(seq_hi, k, h), lambda h, k=k: in_seq(seq_lo, k, h)) for k in range(C)]
                for m in range(C):
                    if m == 0:
                        if last:
                            pe.wait_ge(act_exp, PIECES * (b + 1))
                            pe.wait_ge(c2_raw, 6 * (b + 1))
                        else:
                            pe.wait_ge(act_h, 4 * b + 6)
                    else:
                        pe.wait_ge(act_hn, 4 * b + 2)
                    gate(BANK_HN, 2 * D + m * P, from_h, pe_hn)
                    if m == 0:
                        if not last:
                            pe.wait_ge(act_h, 4 * (b + 2))
                        pe.wait_ge(xc_done, 4 * (b + 1))
                    else:
                        pe.wait_ge(act_r, 4 * b + 2)
                    gate(BANK_R, m * P, from_h + from_c + from_n, pe_r, (n_done, 4 * (b + 1)))
                    if m == 0:
                        pe.wait_ge(act_nmp, 4 * (b + 1))
                    else:
                        pe.wait_ge(act_z, 4 * b + 2)
                    gate(BANK_Z, D + m * P, from_h + from_c + from_n, pe_z)
                    if m == 1:
                        pe.wait_ge(g_cand, 4 * b + 2)
                    gate(BANK_IN, 2 * D + m * P, from_c + from_n, pe_in)

            pe.wait_ge(w_used, NCHUNK + NSUM)
            transposed(0)
            batches(pe, body)
            pe.wait_ge(g_cand, 4 * B)
            pe.wait_ge(act_z, 4 * B)
            to_rows(B - 1)


def kernel(x, adj, L0_gnn_W1, L0_gnn_b1, L0_gnn_W2, L0_gnn_b2, L0_gnn_fusion_w,
           L1_gnn_w_se, L1_gnn_b_se, L1_gnn_conv1_w, L1_gnn_bn1_g, L1_gnn_bn1_b, L1_gnn_bn1_m, L1_gnn_bn1_v,
           L1_gnn_conv2_w, L1_gnn_bn2_g, L1_gnn_bn2_b, L1_gnn_bn2_m, L1_gnn_bn2_v, L1_gnn_w_msg, L1_gnn_b_msg,
           L1_gnn_w_ih, L1_gnn_b_ih, L1_gnn_w_hh, L1_gnn_b_hh):
    import numpy as np
    import concourse.bacc as bacc
    from concourse.bass_utils import run_bass_kernel_spmd

    def chunks(w):
        w = np.asarray(w)
        return np.moveaxis(w.reshape(w.shape[0] // P, P, -1), 0, 1).reshape(P, -1)

    def columns(v):
        return np.asarray(v).reshape(-1, P).T

    masks = np.zeros((P, NG * P + NG), np.float32)
    for g, nodes in enumerate(GROUPS):
        for j in range(PER):
            masks[:, [g * P + j * SLOT + n for n in nodes]] = 1
            masks[[j * SLOT + n for n in nodes], NG * P + g] = 1
    t = np.transpose
    B, N, _ = x.shape
    arrays = {
        "x": x,
        "adj_t": t(adj.reshape(B, N // (2 * P), P, 2, N // (2 * P), P, 2), (0, 6, 4, 5, 3, 1, 2)).reshape(B, N, N),
        "adj_head": adj[:, :NODES, :NODES],
        "l0_w1": L0_gnn_W1,
        "l0_w2": L0_gnn_W2,
        "l0_b1": columns(L0_gnn_b1.reshape(-1)),
        "l0_b2": L0_gnn_b2,
        "fusion_w": L0_gnn_fusion_w,
        "masks": masks,
        "eye": np.eye(P, dtype=np.float32),
        "weights": np.concatenate([
            chunks(t(L1_gnn_conv1_w[:, :, 0])),
            chunks(np.concatenate([t(L1_gnn_w_msg), t(L1_gnn_w_se)], axis=1)),
            chunks(t(np.concatenate([L1_gnn_conv2_w[:, :, 0::2], L1_gnn_conv2_w[:, :, 1::2]], axis=2), (1, 2, 0))),
            chunks(t(L1_gnn_w_ih)),
            chunks(t(L1_gnn_w_hh))], axis=1),
        "cols": np.concatenate([columns(v) for v in (
            L1_gnn_bn1_g, L1_gnn_bn1_b, L1_gnn_bn1_m, L1_gnn_bn1_v,
            L1_gnn_bn2_g, L1_gnn_bn2_b, L1_gnn_bn2_m, L1_gnn_bn2_v, L1_gnn_b_ih, L1_gnn_b_hh)], axis=1),
        "row": np.concatenate([L1_gnn_b_msg, L1_gnn_b_se]),
    }
    arrays = {f"in_{name}": np.ascontiguousarray(a) for name, a in arrays.items()}
    nc = bacc.Bacc("TRN2", target_bir_lowering=False, num_devices=1, dynamic_dma_scratch_size=1024)
    args = [nc.dram_tensor(name, a.shape, mybir.dt.from_np(a.dtype), kind="ExternalInput").ap()
            for name, a in arrays.items()]
    out = nc.dram_tensor("out_0", x.shape, F32, kind="ExternalOutput").ap()
    build(nc, *args, out)
    ran = run_bass_kernel_spmd(nc, [arrays], core_ids=[0])
    return ran.results[0]["out_0"]
```

```python
from contextlib import ExitStack

import concourse.bass as bass
from concourse import mybir

F32 = mybir.dt.float32
F16 = mybir.dt.float16
BF16 = mybir.dt.bfloat16
ALU = mybir.AluOpType
ACT = mybir.ActivationFunctionType
AX = mybir.AxisListType

P = 128
HALF = 512
WSCALE = 16.0
ASCALE = 256.0
EPS = 1e-5

NODES = 25
GROUPS = [list(range(25)), list(range(9)), [0, 9, 10, 11, 12, 13, 14],
          [6, 7, 8, 12, 13, 14], [3, 4, 5, 9, 10, 11]]
RUN = [(min(g), max(g) - min(g) + 1) for g in GROUPS]
NG = len(GROUPS)
SLOT = 32
PER = P // SLOT

PAIRS = [(0, 0), (0, 1), (1, 0), (1, 1), (0, 2), (2, 0)]


def wait(engine, sem, value):
    if isinstance(value, int) and value <= 0:
        return
    engine.wait_ge(sem, value)


def build(nc, x, adj_t, adj_head, l0_w1, l0_w2, l0_b1, l0_b2, fusion_w, masks, ones_row, eye_d, weights, cols_d, row_d, out):
    B, N, D = x.shape
    HID = l0_w1.shape[-1]
    C = D // P
    HC = HID // P
    T = N // P
    H = N // HALF
    Q = B // PER
    TAPS = 17
    FOUR = 4
    V = N // FOUR
    PAD = 2
    ADJ_RING = 4
    ROWS = NODES + 3
    MW = D + 3
    OFF_CONV1 = 0
    OFF_MSG = OFF_CONV1 + C * D
    OFF_IH = OFF_MSG + C * MW
    OFF_HH = OFF_IH + 2 * C * 3 * D
    OFF_E0 = OFF_HH + C * 3 * D
    OFF_TAPS = OFF_E0 + C * D
    BLOCK = 4 * D
    EE, EO, OE, OO, SE, GE, SO, GO, GT = range(9)
    PLAIN = 6
    WCHUNK = 2 * -(-OFF_TAPS // (2 * PLAIN))
    SPLITS = PLAIN + 9 * C
    EARLY = PLAIN + 4
    assert weights.shape[1] == OFF_TAPS + 4 * C * BLOCK and H == 2 and C == 2 and T == 8 and TAPS == 17

    with ExitStack() as ctx:
        def sem(name):
            return ctx.enter_context(nc.semaphore(name))

        def keep(name, shape, dt):
            return ctx.enter_context(nc.sbuf_tensor(name, shape, dt))

        w_hi = keep("w_hi", [P, OFF_TAPS + 9 * C * BLOCK], F16)
        w_lo = keep("w_lo", [P, OFF_TAPS + 9 * C * BLOCK], F16)
        eye = keep("eye", [P, P], F32)
        eye_b = keep("eye_b", [P, P], BF16)
        cols = keep("cols", [P, 28], F32)
        bn_scale = keep("bn_scale", [P, 4], F32)
        bn_psum = keep("bn_psum", [P, 4], F32)
        bn_shift = keep("bn_shift", [P, 4], F32)
        gate_b = keep("gate_b", [P, 6], F32)
        row_b = keep("row_b", [P, MW], F32)
        half_neg = keep("half_neg", [P, 4 * NG], F32)
        ps = ctx.enter_context(nc.psum_tensor("ps", [P, 8, HALF], F32))
        xrow = keep("xrow", [P, T, D], F32)
        x_in = sem("x_loaded")
        xnew = nc.dram_tensor("xnew", [B, ROWS, D], F32).ap()

        l0_first = sem("l0_adj_mask_eye_loaded")
        l0_small = sem("l0_small_loaded")
        bias_row_in = sem("l0_bias_row_loaded")
        l0_x = sem("l0_x_loaded")
        l0_w1_in = sem("l0_w1_loaded")
        l0_w2_in = [sem(f"l0_w2_loaded{g}") for g in range(NG)]
        w_in = [sem(f"w_raw_loaded{i}") for i in range(4)]
        w_summed = sem("w_summed")
        zeroed = sem("l0_zeroed")
        chain = sem("dve_chain")
        deg_ready = sem("deg_ready")
        pool_dinv = sem("pool_dinv")
        b_ready = sem("l0_b_ready")
        pe_nt = sem("pe_nt")
        nt_ready = sem("nt_ready")
        var0_ready = sem("var0_ready")
        pool_rstd0 = sem("pool_rstd0")
        h0_ready = sem("h0_ready")
        pe_agg1 = sem("pe_agg1")
        g_ready = sem("g_ready")
        pe_w1 = sem("pe_w1")
        h2_ready = sem("h2_ready")
        pe_w2 = sem("pe_w2")
        s2t_ready = sem("s2t_ready")
        pe_s2 = sem("pe_s2")
        s2_ready = sem("s2_ready")
        pe_agg2 = sem("pe_agg2")
        fus_ready = sem("fus_ready")
        fus_max = sem("fus_max")
        rw_ready = sem("rw_ready")
        relu2 = sem("relu2")
        acc_done = sem("acc_done")
        xnew_ready = sem("xnew_ready")
        xnew_stored = sem("xnew_stored")
        var_bn = sem("var_bn")
        pool_bn = sem("pool_bn")
        w_split = sem("w_split")
        w_used = sem("w_raw_used")
        consts_ready = sem("consts_ready")
        half_set = sem("half_set")

        def load_new(sp, b):
            sp.dma_start(xrow[0:ROWS // FOUR, 0:FOUR, :], xnew[b].rearrange("(p r) d -> p r d", r=FOUR)).then_inc(x_in, 16)

        def load_rest(sp, b):
            sp.dma_start(xrow[ROWS // FOUR:P, 0:FOUR, :], x[b, ROWS:HALF, :].rearrange("(p r) d -> p r d", r=FOUR)).then_inc(x_in, 16)
            sp.dma_start(xrow[:, FOUR:2 * FOUR, :], x[b, HALF:N, :].rearrange("(p r) d -> p r d", r=FOUR)).then_inc(x_in, 16)

        with ExitStack() as l0:
            def sb(name, shape, dt=F32):
                return l0.enter_context(nc.sbuf_tensor(name, shape, dt))

            x0 = sb("x0", [P, Q, D])
            h0 = sb("h0", [P, Q, D])
            A = sb("A", [P, Q, P])
            AM = sb("AM", [P, NG, Q, P])
            NT = sb("NT", [P, NG, Q, P])
            mask = sb("mask", [P, NG, P])
            rowmask = sb("rowmask", [P, NG])
            W = sb("W", [P, NG, C * HID])
            W1 = W[:].rearrange("p g (c h) -> p g c h", c=C)
            W2 = W[:].rearrange("p g (c d) -> p g c d", c=HC)
            w_raw = sb("w_raw", [P, 4, WCHUNK])
            w_sum = h0[:].rearrange("p q d -> p (q d)")
            b1 = sb("b1", [P, NG, HC])
            b2 = sb("b2", [P, NG, C])
            fus = sb("fus", [P, NG])
            fmx = sb("fmx", [P, 1])
            fex = sb("fex", [P, NG])
            fsum = sb("fsum", [P, 2])
            rw = sb("rw", [P, NG])
            deg = sb("deg", [P, NG, Q])
            nz = sb("nz", [P, NG, Q])
            dinv = sb("dinv", [P, NG, Q])
            dm = sb("dm", [P, NG, Q])
            st0 = sb("st0", [P, Q, 6])
            mv0 = sb("mv0", [P, Q, 2])
            rs0 = sb("rs0", [P, Q])
            at = [C * B * sum(n for _, n in RUN[:g]) for g in range(NG + 1)]
            aggregated = sb("aggregated", [P, max(at[NG], 2 * Q * D)])
            gT = [aggregated[:, at[g]:at[g + 1]].rearrange("p (c n) -> p c n", c=C) for g in range(NG)]
            h2 = [sb(f"h2{g}", [P, HC, B * RUN[g][1]]) for g in range(NG)]
            s2T = sb("s2T", [P, 2, C, B, SLOT])
            S2 = AM[:].rearrange("p g q n -> p (g q n)")[:, 0:2 * Q * D].rearrange("p (s q d) -> p s q d", s=2, q=Q)
            r2 = aggregated[:, 0:2 * Q * D].rearrange("p (s q d) -> p s q d", s=2, q=Q)
            acc = sb("acc", [P, Q, D])

            def piece(i):
                if i < PLAIN:
                    lo, n = i * WCHUNK, min(WCHUNK, OFF_TAPS - i * WCHUNK)
                    return w_raw[:, i % 4, 0:n], slice(lo, lo + n)
                block = (i - PLAIN) % 9
                lo = OFF_TAPS + (i - PLAIN) * BLOCK
                held = {GE: EE, SO: OO, GO: OE}.get(block, block)
                src = w_sum if block in (SE, GT) else w_raw[:, (PLAIN + held) % 4, 0:BLOCK]
                return src, slice(lo, lo + BLOCK)

            def turn(k):
                return [("split", k, SE), ("add", k, GT), ("split", k, GE), ("split", k, SO), ("split", k, GO), ("split", k, GT)]

            LATE = {0: turn(0)[:5], 1: turn(0)[5:], 2: [("split", 1, block) for block in (EE, EO)],
                    3: [("split", 1, block) for block in (OE, OO)] + [("add", 1, block) for block in (SE, GE)],
                    4: [("add", 1, block) for block in (SO, GO)] + turn(1)[:2], NG + 1: turn(1)[2:]}
            first_late = PLAIN + 9
            LATE_HIGH = [range(EARLY, first_late), range(first_late, first_late + 2),
                         range(first_late + 2, first_late + 4), range(first_late + 4, first_late + 8), range(first_late + 8, SPLITS)]

            with nc.Block() as block:
                @block.sync
                def _(sp):
                    sp.dma_start(mask[:], masks[:, 0:NG * P].rearrange("p (g n) -> p g n", g=NG)).then_inc(l0_first, 16)
                    sp.dma_start(eye[:], eye_d).then_inc(l0_first, 16)
                    sp.wait_ge(zeroed, 1)
                    for j in range(PER):
                        lo = SLOT * j
                        sp.dma_start(A[lo:lo + NODES, :, lo:lo + NODES],
                                     adj_head.rearrange("(q j) n m -> j n q m", j=PER)[j]).then_inc(l0_first, 16)
                    sp.wait_ge(zeroed, 2)
                    for j in range(PER):
                        lo = SLOT * j
                        sp.dma_start(x0[lo:lo + ROWS, :, :],
                                     x[:, 0:ROWS, :].rearrange("(q j) n d -> j n q d", j=PER)[j]).then_inc(l0_x, 16)
                    sp.dma_start(rowmask[:], masks[:, NG * P:]).then_inc(l0_small, 16)
                    sp.dma_start(cols[:], cols_d).then_inc(l0_small, 16)
                    sp.dma_start(row_b[:], row_d.partition_broadcast(P)).then_inc(l0_small, 16)
                    sp.dma_start(fus[:], fusion_w.partition_broadcast(P)).then_inc(l0_small, 16)
                    sp.dma_start(b1[:], l0_b1.rearrange("p (g h) -> p g h", g=NG)).then_inc(l0_small, 16)
                    sp.dma_start(b2[:], l0_b2.rearrange("p (g c) -> p g c", g=NG)).then_inc(l0_small, 16)
                    for g in range(NG):
                        sp.dma_start(W1[:, g], l0_w1[g].rearrange("(c p) h -> p c h", p=P)).then_inc(l0_w1_in, 16)
                    for i in range(PLAIN + 4 * C):
                        if i == PLAIN + 2:
                            sp.wait_ge(pe_agg1, NG * C)
                            sp.dma_start(NT[SLOT - 1:SLOT].rearrange("p g q n -> p (g q n)"), ones_row).then_inc(bias_row_in, 16)
                        if i < PLAIN + 4:
                            wait(sp, w_used, i - 3)
                            lo = i * WCHUNK if i < PLAIN else OFF_TAPS + (i - PLAIN) * BLOCK
                            n = min(WCHUNK, OFF_TAPS - lo) if i < PLAIN else BLOCK
                        else:
                            block = i - PLAIN - 4
                            if block == EE:
                                sp.wait_ge(w_used, PLAIN + GE + 1)
                            elif block == OE:
                                sp.wait_ge(w_used, PLAIN + GO + 1)
                            else:
                                sp.wait_ge(w_summed, 5)
                            lo, n = OFF_TAPS + (i - PLAIN) * BLOCK, BLOCK
                        sp.dma_start(w_raw[:, i % 4, 0:n], weights[:, lo:lo + n]).then_inc(w_in[i % 4], 16)
                    load_rest(sp, 0)
                    sp.wait_ge(xnew_ready, 1)
                    for j in range(PER):
                        sp.dma_start(xnew.rearrange("(q j) n d -> j n q d", j=PER)[j],
                                     acc[SLOT * j:SLOT * j + ROWS, :, :]).then_inc(xnew_stored, 16)
                    sp.wait_ge(xnew_stored, 16 * PER)
                    load_new(sp, 0)

                @block.gpsimd
                def _(pool):
                    nc.gpsimd.memset(A[:], 0.0).then_inc(zeroed, 1)
                    nc.gpsimd.memset(x0[:], 0.0).then_inc(zeroed, 1)
                    nc.gpsimd.memset(half_neg[:], -0.5).then_inc(half_set, 1)
                    nc.gpsimd.memset(s2T[:], 0.0).then_inc(zeroed, 1)
                    pool.wait_ge(half_set, 1)
                    pool.wait_ge(deg_ready, 1)
                    nc.gpsimd.tensor_tensor(dinv[:].rearrange("p g q -> p (g q)"), deg[:].rearrange("p g q -> p (g q)"),
                                            half_neg[:], ALU.pow).then_inc(pool_dinv, 1)
                    pool.wait_ge(var0_ready, 1)
                    nc.gpsimd.tensor_tensor(rs0[:], rs0[:], half_neg[:, 0:Q], ALU.pow).then_inc(pool_rstd0, 1)
                    pool.wait_ge(var_bn, 1)
                    nc.gpsimd.tensor_tensor(bn_scale[:], bn_scale[:], half_neg[:, 0:4], ALU.pow).then_inc(pool_bn, 1)

                @block.vector
                def _(dve):
                    step = [0]

                    def link(ins):
                        step[0] += 1
                        ins.then_inc(chain, 1)
                        dve.wait_ge(chain, step[0])

                    dve.wait_ge(l0_first, 16 * (2 + PER))
                    link(nc.vector.tensor_tensor(A[:], A[:], eye[:].unsqueeze(1).to_broadcast([P, Q, P]), ALU.add))
                    for g in range(NG):
                        last = nc.vector.tensor_tensor(AM[:, g], A[:], mask[:, g].unsqueeze(1).to_broadcast([P, Q, P]), ALU.mult)
                    link(last)
                    link(nc.vector.tensor_reduce(deg[:], AM[:], AX.X, ALU.add))
                    link(nc.vector.tensor_scalar(nz[:], deg[:], 0.0, None, ALU.is_equal))
                    nc.vector.tensor_tensor(deg[:], deg[:], nz[:], ALU.add).then_inc(deg_ready, 1)
                    dve.wait_ge(deg_ready, 1)
                    link(nc.vector.tensor_scalar(nz[:], nz[:], -1.0, 1.0, ALU.mult, ALU.add))
                    dve.wait_ge(l0_x, 16 * PER)
                    for q in range(Q):
                        last = nc.vector.bn_stats(st0[:, q], x0[:, q])
                    link(last)
                    for q in range(Q):
                        last = nc.vector.bn_aggr(mv0[:, q], st0[:, q])
                    link(last)
                    nc.vector.tensor_scalar(rs0[:], mv0[:, :, 1], EPS, None, ALU.add).then_inc(var0_ready, 1)
                    dve.wait_ge(l0_small, 16 * 6)
                    nc.vector.tensor_scalar(bn_scale[:, 0:2], cols[:, 6:8], EPS, None, ALU.add)
                    nc.vector.tensor_scalar(bn_scale[:, 2:4], cols[:, 14:16], EPS, None, ALU.add).then_inc(var_bn, 1)
                    dve.wait_ge(pool_dinv, 1)
                    link(nc.vector.tensor_tensor(dinv[:], dinv[:], nz[:], ALU.mult))
                    nc.vector.tensor_tensor(dm[:], dinv[:], rowmask[:].unsqueeze(2).to_broadcast([P, NG, Q]), ALU.mult)
                    link(nc.vector.tensor_tensor(AM[:].rearrange("p g q n -> p (g q) n"), AM[:].rearrange("p g q n -> p (g q) n"),
                                                 dinv[:].rearrange("p g q -> p (g q)").unsqueeze(2).to_broadcast([P, NG * Q, P]), ALU.mult))
                    nc.vector.tensor_copy(eye_b[:], eye[:]).then_inc(b_ready, 1)
                    dve.wait_ge(pool_rstd0, 1)
                    for q in range(Q):
                        last = nc.vector.tensor_scalar(h0[:, q], x0[:, q], mv0[:, q, 0:1], rs0[:, q:q + 1], ALU.subtract, ALU.mult)
                    link(last)
                    nc.vector.tensor_scalar(h0[:], h0[:], 0.0, None, ALU.max).then_inc(h0_ready, 1)
                    for g in range(NG):
                        dve.wait_ge(pe_nt, g + 1)
                        nc.vector.tensor_tensor(NT[:, g], ps[:, g, :].rearrange("p (q n) -> p q n", q=Q),
                                                dm[:, g].unsqueeze(2).to_broadcast([P, Q, P]), ALU.mult).then_inc(nt_ready, 1)
                    link(nc.vector.tensor_reduce(fmx[:], fus[:], AX.X, ALU.max))
                    nc.vector.tensor_scalar(fus[:], fus[:], fmx[:], None, ALU.subtract).then_inc(fus_max, 1)
                    dve.wait_ge(fus_ready, 1)
                    link(nc.vector.tensor_reduce(fsum[:, 0:1], fex[:], AX.X, ALU.add))
                    link(nc.vector.reciprocal(fsum[:, 1:2], fsum[:, 0:1]))
                    nc.vector.scalar_tensor_tensor(rw[:], fex[:], fsum[:, 1:2], rowmask[:], ALU.mult, ALU.mult).then_inc(rw_ready, 1)
                    dve.wait_ge(pool_bn, 1)
                    link(nc.vector.tensor_tensor(bn_scale[:, 0:2], bn_scale[:, 0:2], cols[:, 0:2], ALU.mult))
                    link(nc.vector.tensor_tensor(bn_scale[:, 2:4], bn_scale[:, 2:4], cols[:, 8:10], ALU.mult))
                    nc.vector.tensor_scalar(bn_psum[:], bn_scale[:], 1.0 / WSCALE, None, ALU.mult)
                    nc.vector.tensor_tensor(bn_shift[:, 0:2], bn_scale[:, 0:2], cols[:, 4:6], ALU.mult)
                    link(nc.vector.tensor_tensor(bn_shift[:, 2:4], bn_scale[:, 2:4], cols[:, 12:14], ALU.mult))
                    nc.vector.tensor_tensor(bn_shift[:, 0:2], cols[:, 2:4], bn_shift[:, 0:2], ALU.subtract)
                    nc.vector.tensor_tensor(bn_shift[:, 2:4], cols[:, 10:12], bn_shift[:, 2:4], ALU.subtract)
                    nc.vector.tensor_scalar(gate_b[:, 4:6], cols[:, 26:28], 0.5, None, ALU.mult)
                    link(nc.vector.tensor_tensor(gate_b[:, 0:4], cols[:, 16:20], cols[:, 22:26], ALU.add))
                    nc.vector.tensor_scalar(gate_b[:, 0:4], gate_b[:, 0:4], 0.5, None, ALU.mult).then_inc(consts_ready, 1)
                    def split(i):
                        src, dst = piece(i)
                        dve.wait_ge(w_split, i + 1)
                        nc.vector.scalar_tensor_tensor(w_lo[:, dst], src, WSCALE, w_hi[:, dst],
                                                       ALU.mult, ALU.subtract).then_inc(w_used, 1)

                    def slot(block):
                        return w_raw[:, (PLAIN + block) % 4, 0:BLOCK]

                    def add(k, block):
                        n = (SE, GE, SO, GO, GT).index(block)
                        dst, one, two, used = ((w_sum, slot(EE), slot(EO), OO + 1), (slot(EE), slot(EE), slot(OO), OO + 1),
                                               (slot(OO), slot(OO), slot(OE), OO + 1), (slot(OE), slot(OE), slot(EO), OO + 1),
                                               (w_sum, w_sum, slot(OO), SE + 1))[n]
                        dve.wait_ge(w_used, PLAIN + 9 * k + used)
                        wait(dve, w_summed, 5 * k + n if block != GT else 5 * k + 4)
                        nc.vector.tensor_tensor(dst, one, two, ALU.add).then_inc(w_summed, 1)

                    for i in range(EARLY):
                        split(i)
                    dve.wait_ge(g_ready, NG * C)
                    for block in (SE, GE, SO, GO):
                        add(0, block)

                    def weights_beside(g):
                        for kind, k, block in LATE.get(g, ()):
                            if kind == "add":
                                add(k, block)
                            else:
                                split(PLAIN + 9 * k + block)
                    dve.wait_ge(zeroed, 3)

                    def slots(g):
                        lo, n = RUN[g]
                        for d in range(C):
                            i = g * C + d
                            dve.wait_ge(pe_w2, i + 1)
                            if g >= 2:
                                dve.wait_ge(pe_s2, 2 * (g - 1))
                            if d == 0:
                                nc.vector.tensor_copy(s2T[:, g % 2, :, 0:B:PER, SLOT - 1], b2[:, g].unsqueeze(2).to_broadcast([P, C, Q]))
                            nc.vector.tensor_copy(s2T[:, g % 2, d, :, lo:lo + n],
                                                  ps[:, 5 + i % 3, 0:B * n].rearrange("p (b n) -> p b n", n=n)).then_inc(s2t_ready, 1)

                    def rows(g):
                        for k in range(2):
                            i = 2 * g + k
                            dve.wait_ge(pe_s2, i + 1)
                            if g >= 2:
                                dve.wait_ge(pe_agg2, 2 * (g - 1))
                            nc.vector.tensor_copy(S2[:, g % 2, 2 * k:2 * k + 2, :],
                                                  ps[:, i % 2, :].rearrange("p (q d) -> p q d", q=2)).then_inc(s2_ready, 1)

                    def fuse(g):
                        dve.wait_ge(relu2, 2 * g + 2)
                        if g == 0:
                            dve.wait_ge(h0_ready, 1)
                            nc.vector.tensor_tensor(acc[:], x0[:], r2[:, 0], ALU.add).then_inc(acc_done, 1)
                        else:
                            dve.wait_ge(acc_done, g)
                            ins = nc.vector.tensor_tensor(acc[:], acc[:], r2[:, g % 2], ALU.add)
                            ins.then_inc(xnew_ready if g == NG - 1 else acc_done, 1)

                    for g in range(NG + 2):
                        if g < NG:
                            slots(g)
                        if 1 <= g <= NG:
                            rows(g - 1)
                        if g >= 2:
                            fuse(g - 2)
                        weights_beside(g)

                @block.scalar
                def _(act):
                    def high(i):
                        src, dst = piece(i)
                        block = (i - PLAIN) % 9
                        if i < PLAIN or block < 4:
                            item = i if i < PLAIN else PLAIN + (i - PLAIN) // 9 * 4 + block
                            act.wait_ge(w_in[item % 4], 16 * (item // 4 + 1))
                        else:
                            act.wait_ge(w_summed, (i - PLAIN) // 9 * 5 + block - 3)
                        nc.scalar.activation(w_hi[:, dst], src, ACT.Copy, scale=WSCALE).then_inc(w_split, 1)

                    act.wait_ge(fus_max, 1)
                    nc.scalar.activation(fex[:], fus[:], ACT.Exp).then_inc(fus_ready, 1)
                    for i in range(NG * C):
                        g, c = divmod(i, C)
                        act.wait_ge(pe_agg1, i + 1)
                        nc.scalar.activation(gT[g][:, c, :], ps[:, 5 + i % 3, 0:B * RUN[g][1]], ACT.Copy).then_inc(g_ready, 1)
                        if i >= NG * C - 4:
                            high(i - (NG * C - 4))
                    for i in range(NG * HC):
                        g, hc = divmod(i, HC)
                        if i % 3 == 2:
                            high(4 + i // 3)
                        act.wait_ge(pe_w1, i + 1)
                        nc.scalar.activation(h2[g][:, hc, :], ps[:, i % 5, 0:B * RUN[g][1]], ACT.Relu,
                                             bias=b1[:, g, hc:hc + 1]).then_inc(h2_ready, 1)
                        if hc == HC - 1:
                            act.dma_start(W2[:, g], l0_w2[g].rearrange("(c p) d -> p c d", p=P)).then_inc(l0_w2_in[g], 16)
                    act.wait_ge(rw_ready, 1)
                    for i in range(NG * 2):
                        g, k = divmod(i, 2)
                        if k == 0:
                            for n in LATE_HIGH[g]:
                                high(n)
                        act.wait_ge(pe_agg2, i + 1)
                        if g >= 2:
                            act.wait_ge(acc_done, g - 1)
                        nc.scalar.activation(r2[:, g % 2, 2 * k:2 * k + 2, :],
                                             ps[:, 2 + i % 3, :].rearrange("p (q d) -> p q d", q=2),
                                             ACT.Relu, scale=rw[:, g:g + 1]).then_inc(relu2, 1)

                @block.tensor
                def _(pe):
                    pe.wait_ge(b_ready, 1)
                    pe.wait_ge(chain, 9)
                    for g in range(NG):
                        for q in range(Q):
                            last = nc.tensor.transpose(ps[:, g, q * P:(q + 1) * P], AM[:, g, q], eye[:])
                        last.then_inc(pe_nt, 1)
                    pe.wait_ge(h0_ready, 1)
                    for i in range(NG * C):
                        g, c = divmod(i, C)
                        lo, n = RUN[g]
                        pe.wait_ge(nt_ready, g + 1)
                        wait(pe, g_ready, i - 2)
                        for q in range(Q):
                            last = nc.tensor.matmul(ps[:, 5 + i % 3, q * PER * n:(q + 1) * PER * n].rearrange("p (j n) -> p j n", n=n),
                                                    h0[:, q, c * P:(c + 1) * P],
                                                    NT[:, g, q].rearrange("p (j n) -> p j n", n=SLOT)[:, :, lo:lo + n],
                                                    start=True, stop=True)
                        last.then_inc(pe_agg1, 1)
                    pe.wait_ge(l0_w1_in, 16 * NG)
                    for i in range(NG * HC):
                        g, hc = divmod(i, HC)
                        n = B * RUN[g][1]
                        pe.wait_ge(g_ready, C * (g + 1))
                        pe.wait_ge(nt_ready, NG)
                        wait(pe, h2_ready, i - 4)
                        for c in range(C):
                            last = nc.tensor.matmul(ps[:, i % 5, 0:n], W1[:, g, c, hc * P:(hc + 1) * P], gT[g][:, c, :],
                                                    start=(c == 0), stop=(c == C - 1))
                        last.then_inc(pe_w1, 1)
                    def second(g):
                        n = B * RUN[g][1]
                        pe.wait_ge(l0_w2_in[g], 16)
                        for d in range(C):
                            i = g * C + d
                            wait(pe, s2t_ready, i - 2)
                            for hc in range(HC):
                                last = nc.tensor.matmul(ps[:, 5 + i % 3, 0:n], W2[:, g, hc, d * P:(d + 1) * P], h2[g][:, hc, :],
                                                        start=(hc == 0), stop=(hc == HC - 1))
                            last.then_inc(pe_w2, 1)

                    def to_rows(g):
                        pe.wait_ge(s2t_ready, C * (g + 1))
                        for k in range(2):
                            i = 2 * g + k
                            wait(pe, s2_ready, i - 1)
                            for q in range(2):
                                for d in range(C):
                                    src = s2T[:, g % 2, d, (2 * k + q) * PER:(2 * k + q + 1) * PER, :].rearrange("p b n -> p (b n)")
                                    last = nc.tensor.transpose(ps[:, i % 2, q * D + d * P:q * D + (d + 1) * P], src, eye[:])
                            last.then_inc(pe_s2, 1)

                    def aggregate(g):
                        for k in range(2):
                            i = 2 * g + k
                            pe.wait_ge(s2_ready, i + 1)
                            wait(pe, relu2, i - 2)
                            for q in range(2):
                                dst = ps[:, 2 + i % 3, q * D:(q + 1) * D]
                                last = nc.tensor.matmul(dst, NT[:, g, 2 * k + q], S2[:, g % 2, 2 * k + q], start=True, stop=True)
                            last.then_inc(pe_agg2, 1)

                    pe.wait_ge(g_ready, NG * C)
                    pe.wait_ge(h2_ready, NG * HC)
                    pe.wait_ge(zeroed, 3)
                    pe.wait_ge(bias_row_in, 16)
                    for g in range(NG + 2):
                        if g < NG:
                            second(g)
                        if 1 <= g <= NG:
                            to_rows(g - 1)
                        if g >= 2:
                            aggregate(g - 2)

        def sb(name, shape, dt=F32):
            return ctx.enter_context(nc.sbuf_tensor(name, shape, dt))

        evac = sb("evac", [P, 4, HALF])
        mix = sb("mix", [P, 5, V + 1])
        shifted = sb("shifted", [P, 2, V + 1])
        h_hi = sb("h_hi", [P, 2, C, N], F16)
        h_lo = sb("h_lo", [P, 2, C, N], F16)
        X01, X23, X02, XALL, X31 = range(4, 9)
        seq_hi = sb("seq_hi", [P, C, 9, V + 2 * PAD], F16)
        seq_lo = sb("seq_lo", [P, C, 9, V + 2 * PAD], F16)
        mf = sb("mf", [P, 4, D])
        m_hi = sb("m_hi", [P, T, D], F16)
        m_lo = sb("m_lo", [P, T, D], F16)
        emb = sb("emb", [P, T, 4])
        emb_r = sb("emb_r", [P, T, 4])
        parts = [sb(f"part{i}", [P, T, 4], BF16) for i in range(3)]
        ssq = sb("ssq", [P, T, 3])
        nsq = sb("nsq", [P, T])
        RS = sb("RS", [P, T, P], BF16)
        LS = sb("LS", [P, T, P], BF16)
        RT = sb("RT", [P, N], BF16)
        LT = sb("LT", [P, N], BF16)
        E = sb("E", [P, 2, HALF])
        a_hi = sb("a_hi", [P, T, HALF], F16)
        a_lo = sb("a_lo", [P, T, HALF], F16)
        adj = sb("adj", [P, ADJ_RING, HALF])
        c2f = sb("c2f", [P, 2, HALF])
        xc_hi = sb("xc_hi", [P, C, N], F16)
        xc_lo = sb("xc_lo", [P, C, N], F16)
        tr = sb("tr", [P, 2, HALF])
        stats = sb("stats", [P, T, 6])
        mv = sb("mv", [P, T, 3])
        rstd = sb("rstd", [P, T])

        res = a_hi[:].rearrange("p t n -> p (t n)").bitcast(F32).rearrange("p (c n) -> p c n", c=C)
        gates = a_lo[:].rearrange("p t n -> p (t n)").bitcast(F32).rearrange("p (s h n) -> p s h n", s=2, h=H)
        cand, tz = gates[:, 0], gates[:, 1]
        rest = E[:].rearrange("p s n -> p (s n)").bitcast(F16)
        n_hi = (RT[:].bitcast(F16), rest[:, 0:C * HALF])
        n_lo = (LT[:].bitcast(F16), rest[:, C * HALF:])

        def out_rows(k):
            return (c2f, tr)[k // 2][:, k % 2].rearrange("p (t d) -> p t d", t=2)

        def phases(buf, c, h):
            return buf[:, c, 2 * h:2 * h + 2, PAD:PAD + V]

        residual_in = [sem(f"residual_loaded{i}") for i in range(4)]
        adj_in = [sem(f"adj_loaded{i}") for i in range(ADJ_RING)]
        pads = sem("pads_zeroed")
        pe_h = sem("pe_h")
        pe_conv1 = sem("pe_conv1")
        pe_msg = sem("pe_msg")
        pe_out = sem("pe_out")
        pe_c2 = sem("pe_conv2_products")
        pe_stack = sem("pe_stack")
        pe_dist = sem("pe_dist")
        pe_piece = sem("pe_piece")
        pe_hn = sem("pe_hn")
        pe_r = sem("pe_r")
        pe_z = sem("pe_z")
        pe_in = sem("pe_in")
        seq_hi_done = sem("seq_hi_done")
        act_h = sem("act_h")
        act_h1 = sem("act_h1")
        act_relu_m = sem("act_relu_m")
        act_msg = sem("act_msg")
        act_stack = sem("act_stack")
        act_exp = sem("act_exp")
        act_ahi = sem("act_ahi")
        act_shifted = sem("act_shifted")
        act_xc = sem("act_xc")
        act_nmp = sem("act_nmp")
        act_hn = sem("act_hn")
        act_r = sem("act_r")
        act_z = sem("act_z")
        act_cand = sem("act_cand")
        ln_stats = sem("ln_stats")
        ln_sums = sem("ln_sums")
        ln_terms = sem("ln_terms")
        ln_var = sem("ln_var")
        ln_xn = sem("ln_xn")
        h_hi_done = sem("h_hi_done")
        h_done = sem("h_done")
        seq_sum = sem("seq_sum")
        sum_hi_done = sem("sum_hi_done")
        sum_done = sem("sum_done")
        seq_done = sem("seq_done")
        msg_f = sem("msg_f")
        emb_chain = sem("emb_chain")
        stack_done = sem("stack_done")
        out_done = sem("out_done")
        a_done = sem("a_done")
        c2_step = sem("c2_step")
        c2_hi = sem("c2_plus_hi")
        c2_done = sem("c2_done")
        xc_hi_done = sem("xc_hi_done")
        xc_done = sem("xc_done")
        n_hi_done = sem("n_hi_done")
        n_done = sem("n_done")
        g_rh = sem("g_rh")
        g_cand = sem("g_cand")
        g_dlo = sem("g_dlo")
        g_mix = sem("g_mix")
        g_res = sem("g_res")
        pool_rstd = sem("pool_rstd")
        pool_mlo = sem("pool_mlo")
        pool_alo = sem("pool_alo")
        pool_d = sem("pool_d")
        stored = [sem(f"out_stored{i}") for i in range(4)]

        BANK_CONV1 = (4, 5, 0, 1)
        BANK_MSG = (6, 7, 2, 3)
        BANK_OUT = (1, 0, 4, 5)
        BANK_STACK = (6, 7)
        BANK_DIST = (6, 7)
        BANK_NMP = ((4, 5), (0, 1))
        BANK_H = (6, 7, 2, 3)
        BANK_HN, BANK_R, BANK_Z, BANK_IN = (6, 7), (2, 3), (4, 5), (0, 1)
        PIECES = H * T

        PRODUCTS = {"Pe": (EE, True, 0, V), "Re": (EO, False, 2, V + 1), "Te": (SE, True, X02, V),
                    "Po": (OE, False, 1, V + 1), "Ro": (OO, False, 3, V + 1), "To": (SO, False, X31, V),
                    "Pg": (GE, True, X01, V), "Rg": (GO, False, X23, V + 1), "Tg": (GT, True, XALL, V)}
        ORDER = [(name, k) for k in range(C) for name in ("Pe", "Re", "Ro", "Po")] + \
                [(name, k) for name in ("Te", "To", "Rg", "Pg", "Tg") for k in range(C)]
        FINISH = [name for name, k in ORDER if k == C - 1]
        PLACE = [{"Pe": (p, 0), "Te": (p, V), "Re": (0, 0), "Ro": (2, 0), "Po": (4 - p, 0), "To": (0, 0),
                  "Rg": (2, 0), "Pg": (p, 0), "Tg": (p, V)} for p in (1, 3)]
        STEPS = 15

        def finished(b, m, name):
            return 9 * (C * b + m) + FINISH.index(name) + 1

        def summed(b, m, n):
            return STEPS * (C * b + m) + n

        block = ctx.enter_context(nc.Block())

        def batches(engine, body):
            body(0, 0, 0, False)
            with engine.Fori(0, B // 2 - 1) as j:
                body(2 * j + 1, 1, j, False)
                body(2 * j + 2, 0, j + 1, False)
            body(B - 1, 1, B // 2 - 1, True)

        def first(b):
            return isinstance(b, int) and b == 0

        @block.sync
        def _(sp):
            def load_x(b):
                sp.wait_ge(pe_h, 4 * b)
                load_rest(sp, b)
                load_new(sp, b)

            def load_residual(b):
                for k in range(4):
                    w, f = divmod(k, 2)
                    if k == 0:
                        sp.wait_ge(xc_done, 4 * (b + 1))
                    if k == 2:
                        sp.wait_ge(g_rh, 4 * (b + 1))
                    if w == 0:
                        n = ROWS // FOUR
                        sp.dma_start(out_rows(k)[n:P], x[b, ROWS:HALF, :].rearrange("(p r) d -> p r d", r=FOUR)[:, 2 * f:2 * f + 2])\
                            .then_inc(residual_in[k], 16)
                        sp.dma_start(out_rows(k)[0:n], xnew[b].rearrange("(p r) d -> p r d", r=FOUR)[:, 2 * f:2 * f + 2])\
                            .then_inc(residual_in[k], 16)
                    else:
                        sp.dma_start(out_rows(k), x[b, HALF:N, :].rearrange("(p r) d -> p r d", r=FOUR)[:, 2 * f:2 * f + 2])\
                            .then_inc(residual_in[k], 16)

            def load_adj(b, j):
                h, t = divmod(j, T)
                wait(sp, a_done, PIECES * b + j + 1 - ADJ_RING)
                sp.dma_start(adj[:, j % ADJ_RING, :], adj_t[b, t * P:(t + 1) * P, h * HALF:(h + 1) * HALF])\
                    .then_inc(adj_in[j % ADJ_RING], 16)

            def store(b):
                for k in (1, 0, 2, 3):
                    w, f = divmod(k, 2)
                    if k > 0:
                        sp.wait_ge(out_done, 4 * b + k + 1)
                    sp.dma_start(out[b, w * HALF:(w + 1) * HALF, :].rearrange("(p r) d -> p r d", r=FOUR)[:, 2 * f:2 * f + 2],
                                 out_rows(k)).then_inc(stored[k], 16)

            def body(b, p, q, last):
                if not first(b):
                    store(b - 1)
                if not last:
                    load_x(b + 1)
                for j in range(ADJ_RING, PIECES):
                    load_adj(b, j)
                if not last:
                    for j in range(ADJ_RING):
                        load_adj(b + 1, j)
                load_residual(b)

            for j in range(ADJ_RING):
                load_adj(0, j)
            batches(sp, body)
            store(B - 1)
            for k in range(4):
                sp.wait_ge(stored[k], 16 * B)

        @block.gpsimd
        def _(pool):

            def norm(b):
                pool.wait_ge(ln_var, b + 1)
                nc.gpsimd.tensor_tensor(rstd[:], rstd[:], half_neg[:, 0:T], ALU.pow).then_inc(pool_rstd, 1)

            def body(b, p, q, last):
                for t in range(T):
                    pool.wait_ge(act_msg, T * b + t + 1)
                    nc.gpsimd.tensor_tensor(m_lo[:, t], mf[:, t % 4], m_hi[:, t], ALU.subtract).then_inc(pool_mlo, 1)
                for j in range(PIECES):
                    pool.wait_ge(act_ahi, PIECES * b + j + 1)
                    nc.gpsimd.tensor_tensor(a_lo[:, j % T], E[:, j % 2], a_hi[:, j % T], ALU.subtract).then_inc(pool_alo, 1)
                    if j == 7 and not last:
                        norm(b + 1)
                for i in range(4):
                    m, h = divmod(i, 2)
                    pool.wait_ge(act_cand, 4 * b + i + 1)
                    nc.gpsimd.tensor_tensor(res[:, m, h * HALF:(h + 1) * HALF], h_hi[:, p, m, h * HALF:(h + 1) * HALF],
                                            cand[:, h], ALU.subtract).then_inc(pool_d, 1)

            for buf in (seq_hi, seq_lo):
                for lo in (0, PAD + V):
                    nc.gpsimd.memset(buf[:, :, :, lo:lo + PAD], 0.0).then_inc(pads, 1)
            norm(0)
            for buf in (RS, LS):
                nc.gpsimd.memset(buf[:], 0.0).then_inc(pads, 1)
            batches(pool, body)

        @block.scalar
        def _(act):
            def hidden(b, c):
                for i in (2 * c, 2 * c + 1):
                    act.wait_ge(pe_h, 4 * b + i + 1)
                    wait(act, n_done, 4 * (b - 1) + i + 1)
                    nc.scalar.activation(evac[:, i], ps[:, BANK_H[i], :], ACT.Relu).then_inc(act_h, 1)

            def body(b, p, q, last):
                if first(b):
                    act.wait_ge(pads, 4)
                for i in range(4):
                    m = i // 2
                    act.wait_ge(pe_conv1, 4 * b + i + 1)
                    act.wait_ge(h_done, 4 * b + i + 1)
                    nc.scalar.activation(evac[:, i], ps[:, BANK_CONV1[i], :], ACT.Relu, bias=bn_shift[:, m:m + 1],
                                         scale=bn_psum[:, m:m + 1]).then_inc(act_h1, 1)
                    act.wait_ge(act_h1, 4 * b + i + 1)
                    wait(act, pe_c2, 2 * 9 * b)
                    nc.scalar.activation(phases(seq_hi, m, i % 2), evac[:, i].rearrange("p (f v) -> p f v", f=2),
                                         ACT.Copy).then_inc(seq_hi_done, 1)
                for t in range(T):
                    act.wait_ge(msg_f, T * b + t + 1)
                    nc.scalar.activation(mf[:, t % 4], mf[:, t % 4], ACT.Relu).then_inc(act_relu_m, 1)
                    act.wait_ge(act_relu_m, T * b + t + 1)
                    wait(act, pe_piece, PIECES * b)
                    nc.scalar.activation(m_hi[:, t], mf[:, t % 4], ACT.Copy).then_inc(act_msg, 1)
                wait(act, pe_dist, PIECES * b)
                for i, dst in enumerate((RT, LT)):
                    act.wait_ge(pe_stack, 2 * b + i + 1)
                    nc.scalar.activation(dst[:], ps[:, BANK_STACK[i], :].bitcast(BF16), ACT.Copy).then_inc(act_stack, 1)

                def exponential(j):
                    act.wait_ge(pe_dist, PIECES * b + j + 1)
                    wait(act, pool_alo, PIECES * b + j - 1)
                    nc.scalar.activation(E[:, j % 2], ps[:, BANK_DIST[j % 2], :], ACT.Exp,
                                         bias=nsq[:, j % T:j % T + 1]).then_inc(act_exp, 1)

                def high(j):
                    act.wait_ge(a_done, PIECES * b + j + 1)
                    wait(act, pe_piece, PIECES * b + j - T + 1)
                    nc.scalar.activation(a_hi[:, j % T], E[:, j % 2], ACT.Copy).then_inc(act_ahi, 1)

                def shifted_copy(m, name):
                    act.wait_ge(pe_c2, finished(b, m, name))
                    if name == "Rg":
                        act.wait_ge(c2_step, summed(b, m, 2))
                    else:
                        wait(act, c2_step, summed(b, m, STEPS) - STEPS)
                    nc.scalar.activation(shifted[:, 1 if name == "Ro" else 0], ps[:, PLACE[m][name][0], 0:V + 1],
                                         ACT.Copy).then_inc(act_shifted, 1)

                def conv2_relu(m):
                    for r in range(H):
                        act.wait_ge(c2_done, 4 * b + 2 * m + r + 1)
                        nc.scalar.activation(c2f[:, r], c2f[:, r], ACT.Relu, bias=bn_shift[:, 2 + m:3 + m]).then_inc(act_xc, 1)

                exponential(0)
                for j in range(PIECES):
                    if j + 1 < PIECES:
                        exponential(j + 1)
                    high(j)
                    if j in (0, T + 1):
                        shifted_copy(j // T, "Re")
                        shifted_copy(j // T, "Ro")
                    if j in (4, T + 5):
                        shifted_copy(j // T, "Rg")
                    if j == T + 1:
                        conv2_relu(0)
                for i in range(4):
                    h, d = divmod(i, 2)
                    act.wait_ge(pe_piece, PIECES * b + (h + 1) * T)
                    act.wait_ge(sum_done, 2 * (b + 1))
                    nc.scalar.activation(evac[:, i], ps[:, BANK_NMP[h][d], :], ACT.Copy, scale=1.0 / ASCALE).then_inc(act_nmp, 1)
                    if i == 1:
                        conv2_relu(1)
                        if not last:
                            hidden(b + 1, 0)
                if not last:
                    hidden(b + 1, 1)
                for m in range(C):
                    for h in range(H):
                        i = 4 * b + 2 * m + h
                        act.wait_ge(pe_hn, i + 1)
                        wait(act, g_res, i - 1)
                        nc.scalar.activation(cand[:, h], ps[:, BANK_HN[h], :], ACT.Identity, bias=gate_b[:, 4 + m:5 + m],
                                             scale=0.5 / WSCALE).then_inc(act_hn, 1)
                    for h in range(H):
                        act.wait_ge(pe_r, 4 * b + 2 * m + h + 1)
                        if m == 0:
                            wait(act, stored[2 + h], 16 * b)
                        nc.scalar.activation(tr[:, h], ps[:, BANK_R[h], :], ACT.Tanh, bias=gate_b[:, m:m + 1],
                                             scale=0.5 / WSCALE).then_inc(act_r, 1)
                    for h in range(H):
                        act.wait_ge(pe_z, 4 * b + 2 * m + h + 1)
                        nc.scalar.activation(tz[:, h], ps[:, BANK_Z[h], :], ACT.Tanh, bias=gate_b[:, 2 + m:3 + m],
                                             scale=0.5 / WSCALE).then_inc(act_z, 1)
                    for h in range(H):
                        act.wait_ge(g_cand, 4 * b + 2 * m + h + 1)
                        nc.scalar.activation(cand[:, h], cand[:, h], ACT.Tanh, bias=cols[:, 20 + m:21 + m]).then_inc(act_cand, 1)

            hidden(0, 0)
            hidden(0, 1)
            batches(act, body)

        @block.vector
        def _(dve):
            def norm_stats(b):
                dve.wait_ge(x_in, 16 * 3 * (b + 1))
                for t in range(T):
                    last = nc.vector.bn_stats(stats[:, t], xrow[:, t])
                last.then_inc(ln_stats, 1)
                dve.wait_ge(ln_stats, b + 1)
                nc.vector.tensor_tensor(mv[:, :, 0], stats[:, :, 1], stats[:, :, 4], ALU.add)
                nc.vector.tensor_tensor(mv[:, :, 1], stats[:, :, 1], stats[:, :, 4], ALU.subtract)
                nc.vector.tensor_tensor(mv[:, :, 2], stats[:, :, 2], stats[:, :, 5], ALU.add).then_inc(ln_sums, 1)
                dve.wait_ge(ln_sums, b + 1)
                nc.vector.tensor_scalar(mv[:, :, 0], mv[:, :, 0], 0.5, None, ALU.mult)
                nc.vector.tensor_tensor(mv[:, :, 1], mv[:, :, 1], mv[:, :, 1], ALU.mult)
                nc.vector.tensor_scalar(mv[:, :, 2], mv[:, :, 2], 1.0 / D, EPS, ALU.mult, ALU.add).then_inc(ln_terms, 1)
                dve.wait_ge(ln_terms, b + 1)
                nc.vector.scalar_tensor_tensor(rstd[:], mv[:, :, 1], 0.25, mv[:, :, 2], ALU.mult, ALU.add).then_inc(ln_var, 1)

            def norm_apply(b):
                dve.wait_ge(pool_rstd, b + 1)
                for t in range(T):
                    ins = nc.vector.tensor_scalar(xrow[:, t], xrow[:, t], mv[:, t, 0:1], rstd[:, t:t + 1],
                                                  ALU.subtract, ALU.mult)
                ins.then_inc(ln_xn, 1)

            def hidden(b, p, chunk):
                for i in (2 * chunk, 2 * chunk + 1):
                    c, h = divmod(i, 2)
                    cut = slice(h * HALF, (h + 1) * HALF)
                    dve.wait_ge(act_h, 4 * b + i + 1)
                    nc.vector.tensor_copy(h_hi[:, p, c, cut], evac[:, i]).then_inc(h_hi_done, 1)
                    dve.wait_ge(h_hi_done, 4 * b + i + 1)
                    nc.vector.tensor_tensor(h_lo[:, p, c, cut], evac[:, i], h_hi[:, p, c, cut], ALU.subtract).then_inc(h_done, 1)

            def add_rows(b, ks):
                for k in ks:
                    dve.wait_ge(pe_out, 4 * b + k + 1)
                    dve.wait_ge(residual_in[k], 16 * (1 if k // 2 else 2) * (b + 1))
                    nc.vector.tensor_tensor(out_rows(k), ps[:, BANK_OUT[k], :].rearrange("p (t d) -> p t d", t=2),
                                            out_rows(k), ALU.add).then_inc(out_done, 1)

            def body(b, p, q, last):
                def split_conv1(c, s):
                    i = 4 * b + 2 * c + s + 1
                    dve.wait_ge(seq_hi_done, i)
                    nc.vector.tensor_tensor(phases(seq_lo, c, s), evac[:, 2 * c + s].rearrange("p (f v) -> p f v", f=2),
                                            phases(seq_hi, c, s), ALU.subtract).then_inc(seq_done, 1)

                def split_sum(c):
                    i = 2 * b + c
                    x01, x23 = (evac[:, 2 * c + h].rearrange("p (f v) -> p f v", f=2) for h in range(2))
                    both = evac[:, 2 * c:2 * c + 2].rearrange("p h (f v) -> p h f v", f=2)
                    if c == 0:
                        wait(dve, c2_step, summed(b, 0, 0))
                    else:
                        dve.wait_ge(sum_done, 2 * i)
                    nc.vector.tensor_tensor(mix[:, 0:2, 0:V], both[:, :, 0], both[:, :, 1], ALU.add).then_inc(seq_sum, 1)
                    nc.vector.tensor_tensor(mix[:, 2, 0:V], x01[:, 0], x23[:, 0], ALU.add)
                    nc.vector.tensor_copy(mix[:, 4, 0:1], x01[:, 1, 0:1])
                    nc.vector.tensor_tensor(mix[:, 4, 1:V], x23[:, 1, 0:V - 1], x01[:, 1, 1:V], ALU.add)
                    nc.vector.tensor_copy(mix[:, 4, V:V + 1], x23[:, 1, V - 1:V]).then_inc(seq_sum, 1)
                    dve.wait_ge(seq_sum, 3 * i + 1)
                    nc.vector.tensor_tensor(mix[:, 3, 0:V], mix[:, 0, 0:V], mix[:, 1, 0:V], ALU.add).then_inc(seq_sum, 1)
                    dve.wait_ge(seq_sum, 3 * i + 3)
                    for n, (dst, src) in enumerate(((slice(X01, X31), slice(0, 4)), (X31, 4))):
                        lo, width = (PAD, V) if n == 0 else (PAD - 1, V + 1)
                        nc.vector.tensor_copy(seq_hi[:, c, dst, lo:lo + width], mix[:, src, 0:width]).then_inc(sum_hi_done, 1)
                    for n, (dst, src) in enumerate(((slice(X01, X31), slice(0, 4)), (X31, 4))):
                        lo, width = (PAD, V) if n == 0 else (PAD - 1, V + 1)
                        dve.wait_ge(sum_hi_done, 2 * i + n + 1)
                        nc.vector.tensor_tensor(seq_lo[:, c, dst, lo:lo + width], mix[:, src, 0:width],
                                                seq_hi[:, c, dst, lo:lo + width], ALU.subtract).then_inc(sum_done, 1)

                def message(t):
                    bank = BANK_MSG[t % 4]
                    dve.wait_ge(pe_msg, T * b + t + 1)
                    nc.vector.scalar_tensor_tensor(emb[:, t, 0:3], ps[:, bank, D:MW], 1.0 / WSCALE, row_b[:, D:MW],
                                                   ALU.mult, ALU.add)
                    wait(dve, pool_mlo, T * b + t - 3)
                    nc.vector.scalar_tensor_tensor(mf[:, t % 4], ps[:, bank, 0:D], 1.0 / WSCALE, row_b[:, 0:D],
                                                   ALU.mult, ALU.add).then_inc(msg_f, 1)

                wait(dve, pe_c2, 2 * 9 * b)
                if first(b):
                    dve.wait_ge(pads, 6)
                for i in range(3):
                    split_conv1(i // 2, i % 2)
                    message(2 * i)
                    message(2 * i + 1)
                message(T - 2)
                if not first(b):
                    add_rows(b - 1, (0,))
                message(T - 1)
                if not first(b):
                    add_rows(b - 1, (1,))
                split_conv1(1, 1)
                if not first(b):
                    add_rows(b - 1, (2, 3))
                LINKS = 7
                n = 0

                def link(ins):
                    nonlocal n
                    n += 1
                    ins.then_inc(emb_chain, 1)
                    dve.wait_ge(emb_chain, LINKS * b + n)

                wait(dve, act_exp, PIECES * b)
                dve.wait_ge(msg_f, T * (b + 1))
                link(nc.vector.tensor_tensor(ssq[:], emb[:, :, 0:3], emb[:, :, 0:3], ALU.mult))
                link(nc.vector.tensor_reduce(emb[:, :, 3], ssq[:], AX.X, ALU.add))
                nc.vector.tensor_scalar(nsq[:], emb[:, :, 3], -1.0, None, ALU.mult)
                link(nc.vector.tensor_copy(parts[0][:], emb[:]))
                link(nc.vector.tensor_tensor(emb_r[:], emb[:], parts[0][:], ALU.subtract))
                link(nc.vector.tensor_copy(parts[1][:], emb_r[:]))
                link(nc.vector.tensor_tensor(emb_r[:], emb_r[:], parts[1][:], ALU.subtract))
                link(nc.vector.tensor_copy(parts[2][:], emb_r[:]))
                wait(dve, pe_stack, 2 * b)
                for k, (left, right) in enumerate(PAIRS):
                    if first(b) and left == 0:
                        nc.vector.memset(LS[:, :, 4 * k + 3:4 * k + 4], -1.0)
                    nc.vector.tensor_copy(RS[:, :, 4 * k:4 * k + 4], parts[right][:])
                    ins = nc.vector.tensor_scalar(LS[:, :, 4 * k:4 * k + 3], parts[left][:, :, 0:3], 2.0, None, ALU.mult)
                ins.then_inc(stack_done, 1)

                def weigh(j):
                    per = PIECES // ADJ_RING
                    dve.wait_ge(adj_in[j % ADJ_RING], 16 * (per * b + j // ADJ_RING + 1))
                    dve.wait_ge(act_exp, PIECES * b + j + 1)
                    nc.vector.scalar_tensor_tensor(E[:, j % 2], E[:, j % 2], ASCALE, adj[:, j % ADJ_RING],
                                                   ALU.mult, ALU.mult).then_inc(a_done, 1)

                y = c2f[:].rearrange("p h (f v) -> p (h f) v", f=2)
                e0, e1, o1, w1, w3 = (mix[:, n, 0:V] for n in range(5))
                now, later = slice(0, V), slice(1, V + 1)

                def product(m, name, cols=now):
                    bank, at = PLACE[m][name]
                    return ps[:, bank, at + cols.start:at + cols.stop]

                def even_part(m):
                    dve.wait_ge(pe_c2, finished(b, m, "Te"))
                    dve.wait_ge(act_shifted, 6 * b + 3 * m + 1)
                    if m == 0:
                        dve.wait_ge(sum_done, 4 * (b + 1))
                    else:
                        dve.wait_ge(c2_step, summed(b, m, 0))
                    re = shifted[:, 0]
                    nc.vector.tensor_tensor(e0, product(m, "Pe"), re[:, now], ALU.add).then_inc(c2_step, 1)
                    nc.vector.tensor_tensor(w1, product(m, "Pe"), re[:, later], ALU.add).then_inc(c2_step, 1)
                    dve.wait_ge(c2_step, summed(b, m, 2))
                    nc.vector.tensor_tensor(e1, product(m, "Te"), w1, ALU.subtract).then_inc(c2_step, 1)

                def odd_part(m):
                    dve.wait_ge(pe_c2, finished(b, m, "To"))
                    dve.wait_ge(act_shifted, 6 * b + 3 * m + 2)
                    ro = shifted[:, 1]
                    nc.vector.tensor_tensor(w3, product(m, "Po", later), ro[:, now], ALU.add).then_inc(c2_step, 1)
                    dve.wait_ge(c2_step, summed(b, m, 4))
                    nc.vector.tensor_tensor(ro[:], product(m, "Po", slice(0, V + 1)), ro[:], ALU.add).then_inc(c2_step, 1)
                    nc.vector.tensor_tensor(o1, product(m, "To"), w3, ALU.subtract).then_inc(c2_step, 1)
                    dve.wait_ge(c2_step, summed(b, m, 6))
                    if m == 0:
                        for k in range(2):
                            wait(dve, stored[k], 16 * b)
                    else:
                        dve.wait_ge(xc_done, 4 * b + 2)
                    nc.vector.tensor_tensor(y[:, 0], e0, ro[:, now], ALU.add).then_inc(c2_step, 1)
                    nc.vector.tensor_tensor(y[:, 2], e1, o1, ALU.add).then_inc(c2_step, 1)
                    nc.vector.tensor_tensor(w1, e0, o1, ALU.add).then_inc(c2_step, 1)
                    nc.vector.tensor_tensor(w3, e1, ro[:, later], ALU.add).then_inc(c2_step, 1)

                def sum_part(m):
                    dve.wait_ge(act_shifted, 6 * b + 3 * m + 3)
                    dve.wait_ge(c2_step, summed(b, m, 10))
                    rg = shifted[:, 0]
                    nc.vector.tensor_tensor(w1, rg[:, now], w1, ALU.subtract).then_inc(c2_step, 1)
                    nc.vector.tensor_tensor(w3, rg[:, later], w3, ALU.add).then_inc(c2_step, 1)

                def last_part(m):
                    dve.wait_ge(pe_c2, finished(b, m, "Tg"))
                    dve.wait_ge(c2_step, summed(b, m, 12))
                    nc.vector.tensor_tensor(y[:, 1], product(m, "Pg"), w1, ALU.add).then_inc(c2_step, 1)
                    nc.vector.tensor_tensor(w3, product(m, "Pg"), w3, ALU.add).then_inc(c2_step, 1)
                    dve.wait_ge(c2_step, summed(b, m, 14))
                    nc.vector.tensor_tensor(y[:, 3], product(m, "Tg"), w3, ALU.subtract).then_inc(c2_step, 1)

                def scaled(m):
                    for r in range(H):
                        i = 4 * b + 2 * m + r
                        cut = slice(r * HALF, (r + 1) * HALF)
                        if r == 0:
                            dve.wait_ge(c2_step, summed(b, m, 15))
                        nc.vector.scalar_tensor_tensor(c2f[:, r], c2f[:, r], bn_psum[:, 2 + m:3 + m],
                                                       h_hi[:, p, m, cut], ALU.mult, ALU.add).then_inc(c2_hi, 1)
                        dve.wait_ge(c2_hi, i + 1)
                        nc.vector.tensor_tensor(c2f[:, r], c2f[:, r], h_lo[:, p, m, cut], ALU.add).then_inc(c2_done, 1)

                def split_conv2(m):
                    if m == 0:
                        wait(dve, pe_in, 4 * b)
                    for r in range(H):
                        i = 4 * b + 2 * m + r
                        cut = slice(r * HALF, (r + 1) * HALF)
                        dve.wait_ge(act_xc, i + 1)
                        nc.vector.tensor_copy(xc_hi[:, m, cut], c2f[:, r]).then_inc(xc_hi_done, 1)
                        dve.wait_ge(xc_hi_done, i + 1)
                        nc.vector.tensor_tensor(xc_lo[:, m, cut], c2f[:, r], xc_hi[:, m, cut], ALU.subtract).then_inc(xc_done, 1)

                def split_nmp(i):
                    h, d = divmod(i, 2)
                    cols = slice(d * HALF, (d + 1) * HALF)
                    if i == 0:
                        dve.wait_ge(pe_dist, PIECES * (b + 1))
                    dve.wait_ge(act_nmp, 4 * b + i + 1)
                    nc.vector.tensor_copy(n_hi[h][:, cols], evac[:, i]).then_inc(n_hi_done, 1)
                    dve.wait_ge(n_hi_done, 4 * b + i + 1)
                    nc.vector.tensor_tensor(n_lo[h][:, cols], evac[:, i], n_hi[h][:, cols], ALU.subtract).then_inc(n_done, 1)

                split_sum(0)
                split_sum(1)
                for j in range(PIECES):
                    weigh(j)
                    if j == 9 and not last:
                        norm_apply(b + 1)
                    if j == 2:
                        even_part(0)
                    if j == 3:
                        odd_part(0)
                    if j == 4 and not last:
                        norm_stats(b + 1)
                    if j == 6:
                        sum_part(0)
                    if j == 7:
                        last_part(0)
                    if j == 8:
                        scaled(0)
                    if j == 10:
                        split_conv2(0)
                    if j == 12:
                        even_part(1)
                    if j == 13:
                        odd_part(1)
                    if j == 14:
                        sum_part(1)
                last_part(1)
                scaled(1)
                split_nmp(0)
                split_nmp(1)
                split_conv2(1)
                if not last:
                    hidden(b + 1, 1 - p, 0)
                split_nmp(2)
                split_nmp(3)
                if not last:
                    hidden(b + 1, 1 - p, 1)
                for m in range(C):
                    for h in range(H):
                        i = 4 * b + 2 * m + h
                        dve.wait_ge(act_r, i + 1)
                        nc.vector.scalar_tensor_tensor(cand[:, h], tr[:, h], 1.0, cand[:, h], ALU.add, ALU.mult).then_inc(g_rh, 1)
                        dve.wait_ge(pe_in, i + 1)
                        dve.wait_ge(g_rh, i + 1)
                        nc.vector.scalar_tensor_tensor(cand[:, h], ps[:, BANK_IN[h], :], 1.0 / WSCALE, cand[:, h],
                                                       ALU.mult, ALU.add).then_inc(g_cand, 1)
                    for h in range(H):
                        i = 4 * b + 2 * m + h
                        cut = slice(h * HALF, (h + 1) * HALF)
                        dve.wait_ge(pool_d, i + 1)
                        nc.vector.tensor_tensor(res[:, m, cut], res[:, m, cut], h_lo[:, p, m, cut], ALU.add).then_inc(g_dlo, 1)
                        dve.wait_ge(g_dlo, i + 1)
                        dve.wait_ge(act_z, i + 1)
                        nc.vector.scalar_tensor_tensor(res[:, m, cut], tz[:, h], 1.0, res[:, m, cut], ALU.add, ALU.mult).then_inc(g_mix, 1)
                        dve.wait_ge(g_mix, i + 1)
                        nc.vector.scalar_tensor_tensor(res[:, m, cut], res[:, m, cut], 0.5, cand[:, h],
                                                       ALU.mult, ALU.add).then_inc(g_res, 1)

            norm_stats(0)
            norm_apply(0)
            hidden(0, 0, 0)
            hidden(0, 0, 1)
            batches(dve, body)
            add_rows(B - 1, range(4))

        @block.tensor
        def _(pe):
            out_ins = [None, None]

            def weight(off, k, width, lo, n):
                at = off + k * width + lo
                return w_hi[:, at:at + n], w_lo[:, at:at + n]

            def three(banks, w, v_hi, v_lo, start, stop):
                for n, (wt, v) in enumerate(((w[0], v_hi), (w[0], v_lo), (w[1], v_hi))):
                    for h, bank in enumerate(banks):
                        out_ins[h] = nc.tensor.matmul(ps[:, bank, :], wt, v(h), start=(start and n == 0), stop=(stop and n == 2))

            def transposed(b, c):
                pe.wait_ge(ln_xn, b + 1)
                if c == 0:
                    wait(pe, act_exp, PIECES * b)
                else:
                    wait(pe, c2_step, summed(b, 0, 0))
                for h in range(H):
                    i = 2 * c + h
                    for u in range(T // 2):
                        f, w = divmod(u, 2)
                        last = nc.tensor.transpose(ps[:, BANK_H[i], u * P:(u + 1) * P],
                                                   xrow[:, FOUR * w + 2 * h + f, c * P:(c + 1) * P], eye[:])
                    last.then_inc(pe_h, 1)

            def to_rows(b):
                pe.wait_ge(g_res, 4 * (b + 1))
                for k in range(4):
                    w = k // 2
                    for r in range(2):
                        at = (2 * (k % 2) + r) * V + w * P
                        for c in range(C):
                            last = nc.tensor.transpose(ps[:, BANK_OUT[k], r * D + c * P:r * D + (c + 1) * P],
                                                       res[:, c, at:at + P], eye[:])
                    last.then_inc(pe_out, 1)

            def body(b, p, q, last):
                pe.wait_ge(h_done, 4 * (b + 1))
                for m in range(C):
                    if m == 0:
                        wait(pe, act_z, 4 * b)
                    else:
                        wait(pe, g_cand, 4 * b)
                    for k in range(C):
                        three(BANK_CONV1[2 * m:2 * m + 2], weight(OFF_CONV1, k, D, m * P, P),
                              lambda h: h_hi[:, p, k, h * HALF:(h + 1) * HALF],
                              lambda h: h_lo[:, p, k, h * HALF:(h + 1) * HALF], k == 0, k == C - 1)
                    out_ins[0].then_inc(pe_conv1, 1)
                    out_ins[1].then_inc(pe_conv1, 1)
                if first(b):
                    pe.wait_ge(act_h, 4)
                else:
                    pe.wait_ge(act_hn, 4 * b)
                    pe.wait_ge(act_r, 4 * b)
                for t in range(T):
                    if t >= 4:
                        pe.wait_ge(msg_f, T * b + t - 3)
                    for k in range(C):
                        wh, wl = weight(OFF_MSG, k, MW, 0, MW)
                        cut = slice(t * P, (t + 1) * P)
                        for n, (v, w) in enumerate(((h_hi, wh), (h_hi, wl), (h_lo, wh))):
                            ins = nc.tensor.matmul(ps[:, BANK_MSG[t % 4], 0:MW], v[:, p, k, cut], w,
                                                   start=(k == 0 and n == 0), stop=(k == C - 1 and n == 2))
                    ins.then_inc(pe_msg, 1)
                pe.wait_ge(act_h1, 4 * (b + 1))
                if not first(b):
                    to_rows(b - 1)

                def stacks():
                    pe.wait_ge(stack_done, b + 1)
                    for i, src in enumerate((RS, LS)):
                        for t in range(T):
                            ins = nc.tensor.transpose(ps[:, BANK_STACK[i], :].bitcast(BF16)[:, t * P:(t + 1) * P], src[:, t], eye_b[:])
                        ins.then_inc(pe_stack, 1)

                def distances(j):
                    h, t = divmod(j, T)
                    if j == 0:
                        pe.wait_ge(act_stack, 2 * (b + 1))
                    if j >= 2:
                        pe.wait_ge(act_exp, PIECES * b + j - 1)
                    nc.tensor.matmul(ps[:, BANK_DIST[j % 2], :], LT[:, t * P:(t + 1) * P], RT[:, h * HALF:(h + 1) * HALF],
                                     start=True, stop=True).then_inc(pe_dist, 1)

                def passing(j):
                    h, t = divmod(j, T)
                    if j == 0:
                        pe.wait_ge(pool_mlo, T * (b + 1))
                        wait(pe, out_done, 4 * b)
                    if j == T:
                        pe.wait_ge(c2_step, summed(b, 1, 6))
                    pe.wait_ge(pool_alo, PIECES * b + j + 1)
                    for d in range(C):
                        cut = slice(d * P, (d + 1) * P)
                        for n, (w, v) in enumerate(((m_hi, a_hi), (m_hi, a_lo), (m_lo, a_hi))):
                            ins = nc.tensor.matmul(ps[:, BANK_NMP[h][d], :], w[:, t, cut], v[:, t],
                                                   start=(t == 0 and n == 0), stop=(t == T - 1 and n == 2))
                    ins.then_inc(pe_piece, 1)

                between = {(0, 16): [stacks]}
                for t in range(T):
                    between.setdefault((0, 22 + 7 * t), []).append(lambda t=t: distances(t))
                    between.setdefault((1, 3 + 9 * t), []).append(lambda t=t: passing(t))
                    between.setdefault((1, 4 + 9 * t), []).append(lambda t=t: distances(T + t))

                def place_free(m, name):
                    if m == 0:
                        if name == "Pe":
                            wait(pe, out_done, 4 * b - 3)
                        elif name == "Re":
                            wait(pe, out_done, 4 * b - 2)
                        elif name == "Ro":
                            pe.wait_ge(msg_f, T * (b + 1))
                    elif name == "Pe":
                        pe.wait_ge(c2_step, summed(b, 0, 6))
                    elif name == "Re":
                        pe.wait_ge(c2_step, summed(b, 0, 6))
                    elif name == "Ro":
                        pe.wait_ge(act_shifted, 6 * b + 3)
                    elif name == "Po":
                        pe.wait_ge(c2_step, summed(b, 0, 15))
                    if name == "To":
                        pe.wait_ge(act_shifted, 6 * b + 3 * m + 1)
                    elif name == "Rg":
                        pe.wait_ge(act_shifted, 6 * b + 3 * m + 2)
                    elif name == "Pg":
                        pe.wait_ge(c2_step, summed(b, m, 3))

                for m in range(C):
                    step = 0
                    for name, k in ORDER:
                        block, tap0, s, width = PRODUCTS[name]
                        bank, at = PLACE[m][name]
                        if k == 0:
                            place_free(m, name)
                        if m == 0:
                            if s < FOUR:
                                pe.wait_ge(seq_done, 4 * b + 2 * k + s // 2 + 1)
                            else:
                                pe.wait_ge(sum_done, 4 * b + 2 * k + 2)
                        taps = [OFF_TAPS + (9 * k + block) * BLOCK + i * D + m * P for i in range(4)]
                        if tap0:
                            taps = [OFF_E0 + k * D + m * P] + taps
                        for a, col in enumerate(taps):
                            for i, (w, v) in enumerate(((w_hi, seq_hi), (w_hi, seq_lo), (w_lo, seq_hi))):
                                ins = nc.tensor.matmul(ps[:, bank, at:at + width], w[:, col:col + P], v[:, k, s, a:a + width],
                                                       start=(k == 0 and a == 0 and i == 0),
                                                       stop=(k == C - 1 and a == len(taps) - 1 and i == 2))
                            if k == C - 1 and a == len(taps) - 1:
                                ins.then_inc(pe_c2, 1)
                            for f in between.pop((m, step), ()):
                                f()
                            step += 1
                assert not between
                for t in range(T):
                    passing(T + t)
                    if t == T - 3 and not last:
                        transposed(b + 1, 0)
                if not last:
                    transposed(b + 1, 1)

                def gate(banks, col, srcs, done, ready=None):
                    for n, (off, k, hi, lo) in enumerate(srcs):
                        if ready and n == len(srcs) - C:
                            pe.wait_ge(*ready)
                        three(banks, weight(off, k, 3 * D, col, P), hi, lo, n == 0, n == len(srcs) - 1)
                    out_ins[0].then_inc(done, 1)
                    out_ins[1].then_inc(done, 1)

                def operand(off, k, hi, lo):
                    return (off, k, lambda h: hi[:, h * HALF:(h + 1) * HALF], lambda h: lo[:, h * HALF:(h + 1) * HALF])

                from_h = [operand(OFF_HH, k, h_hi[:, p, k], h_lo[:, p, k]) for k in range(C)]
                from_c = [operand(OFF_IH, k, xc_hi[:, k], xc_lo[:, k]) for k in range(C)]
                from_n = [(OFF_IH, C + k, lambda h, k=k: n_hi[h][:, k * HALF:(k + 1) * HALF],
                           lambda h, k=k: n_lo[h][:, k * HALF:(k + 1) * HALF]) for k in range(C)]
                for m in range(C):
                    if m == 0:
                        if last:
                            pe.wait_ge(act_exp, PIECES * (b + 1))
                            pe.wait_ge(c2_step, summed(b + 1, 0, 0))
                        else:
                            pe.wait_ge(act_h, 4 * b + 6)
                    else:
                        pe.wait_ge(act_hn, 4 * b + 2)
                    gate(BANK_HN, 2 * D + m * P, from_h, pe_hn)
                    if m == 0:
                        if not last:
                            pe.wait_ge(act_h, 4 * (b + 2))
                        pe.wait_ge(xc_done, 4 * (b + 1))
                    else:
                        pe.wait_ge(act_r, 4 * b + 2)
                    gate(BANK_R, m * P, from_h + from_c + from_n, pe_r, (n_done, 4 * (b + 1)))
                    if m == 0:
                        pe.wait_ge(act_nmp, 4 * (b + 1))
                    else:
                        pe.wait_ge(act_z, 4 * b + 2)
                    gate(BANK_Z, D + m * P, from_h + from_c + from_n, pe_z)
                    if m == 1:
                        pe.wait_ge(g_cand, 4 * b + 2)
                    gate(BANK_IN, 2 * D + m * P, from_c + from_n, pe_in)

            pe.wait_ge(w_used, SPLITS)
            transposed(0, 0)
            transposed(0, 1)
            batches(pe, body)
            pe.wait_ge(g_cand, 4 * B)
            pe.wait_ge(act_z, 4 * B)
            to_rows(B - 1)


def kernel(x, adj, L0_gnn_W1, L0_gnn_b1, L0_gnn_W2, L0_gnn_b2, L0_gnn_fusion_w,
           L1_gnn_w_se, L1_gnn_b_se, L1_gnn_conv1_w, L1_gnn_bn1_g, L1_gnn_bn1_b, L1_gnn_bn1_m, L1_gnn_bn1_v,
           L1_gnn_conv2_w, L1_gnn_bn2_g, L1_gnn_bn2_b, L1_gnn_bn2_m, L1_gnn_bn2_v, L1_gnn_w_msg, L1_gnn_b_msg,
           L1_gnn_w_ih, L1_gnn_b_ih, L1_gnn_w_hh, L1_gnn_b_hh):
    import numpy as np
    import concourse.bacc as bacc
    from concourse.bass_utils import run_bass_kernel_spmd

    def chunks(w):
        w = np.asarray(w)
        return np.moveaxis(w.reshape(w.shape[0] // P, P, -1), 0, 1).reshape(P, -1)

    def columns(v):
        return np.asarray(v).reshape(-1, P).T

    masks = np.zeros((P, NG * P + NG), np.float32)
    for g, nodes in enumerate(GROUPS):
        for j in range(PER):
            masks[:, [g * P + j * SLOT + n for n in nodes]] = 1
            masks[[j * SLOT + n for n in nodes], NG * P + g] = 1
    t = np.transpose
    B, N, _ = x.shape
    arrays = {
        "x": x,
        "adj_t": t(adj.reshape(B, N // (4 * P), P, 4, N // (4 * P), P, 4), (0, 6, 4, 5, 3, 1, 2)).reshape(B, N, N),
        "adj_head": adj[:, :NODES, :NODES],
        "l0_w1": L0_gnn_W1,
        "l0_w2": L0_gnn_W2,
        "l0_b1": columns(L0_gnn_b1.reshape(-1)),
        "l0_b2": columns(L0_gnn_b2.reshape(-1)),
        "fusion_w": L0_gnn_fusion_w,
        "masks": masks,
        "ones_row": np.ones((1, NG * (B // PER) * P), np.float32),
        "eye": np.eye(P, dtype=np.float32),
        "weights": np.concatenate([
            chunks(t(L1_gnn_conv1_w[:, :, 0])),
            chunks(np.concatenate([t(L1_gnn_w_msg), t(L1_gnn_w_se)], axis=1)),
            chunks(t(L1_gnn_w_ih)),
            chunks(t(L1_gnn_w_hh)),
            chunks(t(L1_gnn_conv2_w[:, :, 0])),
            chunks(t(L1_gnn_conv2_w[:, :, [i for lo in (4, 2, 1, 3) for i in range(lo, 17, 4)]], (1, 2, 0)))], axis=1),
        "cols": np.concatenate([columns(v) for v in (
            L1_gnn_bn1_g, L1_gnn_bn1_b, L1_gnn_bn1_m, L1_gnn_bn1_v,
            L1_gnn_bn2_g, L1_gnn_bn2_b, L1_gnn_bn2_m, L1_gnn_bn2_v, L1_gnn_b_ih, L1_gnn_b_hh)], axis=1),
        "row": np.concatenate([L1_gnn_b_msg, L1_gnn_b_se]),
    }
    arrays = {f"in_{name}": np.ascontiguousarray(a) for name, a in arrays.items()}
    nc = bacc.Bacc("TRN2", target_bir_lowering=False, num_devices=1, dynamic_dma_scratch_size=1024)
    args = [nc.dram_tensor(name, a.shape, mybir.dt.from_np(a.dtype), kind="ExternalInput").ap()
            for name, a in arrays.items()]
    out = nc.dram_tensor("out_0", x.shape, F32, kind="ExternalOutput").ap()
    build(nc, *args, out)
    ran = run_bass_kernel_spmd(nc, [arrays], core_ids=[0])
    return ran.results[0]["out_0"]
```
